# Optimizing a Trainium2 kernel written in Bass

```python
import numpy as np
import jax
import jax.numpy as jnp

def _softmax(x, axis=-1):
    return jax.nn.softmax(x, axis=axis)

def _gelu(x):
    return jax.nn.gelu(x, approximate=True)

def _silu(x):
    return jax.nn.silu(x)

def _sigmoid(x):
    return jax.nn.sigmoid(x)

def _layernorm(x, axis=-1, eps=1e-05):
    m = jnp.mean(x, axis=axis, keepdims=True)
    v = jnp.var(x, axis=axis, keepdims=True)
    return (x - m) / jnp.sqrt(v + eps)

def _scatter_add(tgt, idx, src, axis=0):
    return tgt.at[idx].add(src)

def _segment_sum(src, seg, n):
    return jax.ops.segment_sum(src, seg, n)
kernel_name = 'mk_flamingo_gated_d2_seqx_r8_6d8ba3'

def setup_inputs(seed: int=0):
    np.random.seed(seed)
    _w = jnp.asarray

    def _rec_inputs():
        import jax
        import jax.numpy as jnp
        _rk = jax.random.key(seed)
        x = 7.22e-05 + 1 * jax.random.normal(jax.random.fold_in(_rk, 1), (16, 128, 128), jnp.float32)
        _lenS = 128 - jax.random.randint(jax.random.fold_in(_rk, 7), (16,), 0, max(1, 128 // 4) + 1, jnp.int32)
        _lenS2 = 77 - jax.random.randint(jax.random.fold_in(_rk, 8), (16,), 0, max(1, 77 // 4) + 1, jnp.int32)
        _ctx_1024P = jax.random.normal(jax.random.fold_in(_rk, 11), (16, 16, 128), jnp.float32)
        _ctx_1024c = jax.random.dirichlet(jax.random.fold_in(_rk, 511), 0.3 * jnp.ones((16,), jnp.float32), (16, 77))
        _ctx_1024t = jnp.einsum('bsk,bkd->bsd', _ctx_1024c, _ctx_1024P)
        _ctx_1024t = _ctx_1024t * jax.lax.rsqrt(jnp.mean(jnp.square(_ctx_1024t)) + 1e-12) * 0.953939
        ctx_1024 = -1.52775e-05 + 0.999936 * (_ctx_1024t + 0.3 * jax.random.normal(jax.random.fold_in(_rk, 611), (16, 77, 128), jnp.float32))
        _g = jax.random.normal(jax.random.fold_in(_rk, 9001), (2, 2), jnp.float32)
        _g = jnp.sign(_g) * jnp.maximum(jnp.abs(_g), 1.0) + (_g == 0) * 1.0
        g_xattn = _g[0]
        g_ffn = _g[1]
        return (x, ctx_1024, g_xattn, g_ffn)
    x, ctx_1024, g_xattn, g_ffn = _rec_inputs()

    def _L0_xattn_setup():
        import math
        import jax, jax.numpy as jnp
        import numpy as np
        B, TQ, TK, D = (4, 256, 1024, 128)
        N_HEAD = 16
        STRIDE = 16
        key = jax.random.key(seed)
        ks = jax.random.split(key, 7)
        w_scale = 0.02
        return {'q': jax.random.normal(ks[0], (B, TQ, D), jnp.float32), 'k': jax.random.normal(ks[1], (B, TK, D), jnp.float32), 'v': jax.random.normal(ks[2], (B, TK, D), jnp.float32), 'Wq': jax.random.normal(ks[3], (D, D), jnp.float32) * w_scale, 'bq': jnp.zeros((D,), jnp.float32), 'Wk': jax.random.normal(ks[4], (D, D), jnp.float32) * w_scale, 'bk': jnp.zeros((D,), jnp.float32), 'Wv': jax.random.normal(ks[5], (D, D), jnp.float32) * w_scale, 'bv': jnp.zeros((D,), jnp.float32), 'Wo': jax.random.normal(ks[6], (D, D), jnp.float32) * w_scale, 'bo': jnp.zeros((D,), jnp.float32)}
    _L0_xattn_all = _L0_xattn_setup()
    _L0_xattn_in = {k: v for k, v in _L0_xattn_all.items() if k in ('Wq', 'bq', 'Wk', 'bk', 'Wv', 'bv', 'Wo', 'bo')}
    del _L0_xattn_all

    def _L0_ffn_setup():
        import jax, jax.numpy as jnp
        import numpy as np
        D_MODEL = 128
        N_HEADS = 16
        D_HEAD = D_MODEL // N_HEADS
        N_EXPERTS = 8
        TOP_K = 2
        D_FF = 256
        EPS = 1e-06

        def rmsnorm(x, w):
            return x * jax.lax.rsqrt(jnp.mean(x * x, axis=-1, keepdims=True) + EPS) * w

        def swiglu(x, w_gate, w_up, w_down):
            return jax.nn.silu(x @ w_gate) * (x @ w_up) @ w_down
        key = jax.random.key(seed)
        ks = jax.random.split(key, 16)
        s = 0.02
        B, S = (2, 256)
        return {'X': jax.random.normal(ks[0], (B, S, D_MODEL), dtype=jnp.float32), 'norm1_w': jnp.ones((D_MODEL,), jnp.float32), 'norm2_w': jnp.ones((D_MODEL,), jnp.float32), 'wq': jax.random.normal(ks[1], (D_MODEL, D_MODEL), jnp.float32) * s, 'wk': jax.random.normal(ks[2], (D_MODEL, D_MODEL), jnp.float32) * s, 'wv': jax.random.normal(ks[3], (D_MODEL, D_MODEL), jnp.float32) * s, 'wo': jax.random.normal(ks[4], (D_MODEL, D_MODEL), jnp.float32) * s, 'router_w': jax.random.normal(ks[5], (D_MODEL, N_EXPERTS), jnp.float32) * s, 'sh_gate': jax.random.normal(ks[6], (D_MODEL, D_FF), jnp.float32) * s, 'sh_up': jax.random.normal(ks[7], (D_MODEL, D_FF), jnp.float32) * s, 'sh_down': jax.random.normal(ks[8], (D_FF, D_MODEL), jnp.float32) * s, 'e_gate': jax.random.normal(ks[9], (N_EXPERTS, D_MODEL, D_FF), jnp.float32) * s, 'e_up': jax.random.normal(ks[10], (N_EXPERTS, D_MODEL, D_FF), jnp.float32) * s, 'e_down': jax.random.normal(ks[11], (N_EXPERTS, D_FF, D_MODEL), jnp.float32) * s}
    _L0_ffn_all = _L0_ffn_setup()
    _L0_ffn_in = {k: v for k, v in _L0_ffn_all.items() if k in ('norm1_w', 'norm2_w', 'wq', 'wk', 'wv', 'wo', 'router_w', 'sh_gate', 'sh_up', 'sh_down', 'e_gate', 'e_up', 'e_down')}
    del _L0_ffn_all

    def _L1_xattn_setup():
        import jax, jax.numpy as jnp
        import numpy as np
        B, L_ENC, L_DEC, D = (16, 64, 128, 128)
        key = jax.random.key(seed)
        k1, k2, k3, k4, k5, k6 = jax.random.split(key, 6)
        encoder_hc = jax.random.normal(k1, (B, L_ENC, D), dtype=jnp.float32)
        decoder_hq = jax.random.normal(k2, (B, L_DEC, D), dtype=jnp.float32)
        w_sim = jax.random.normal(k3, (3 * D,), dtype=jnp.float32) * 0.02
        b_sim = jax.random.normal(k4, (1,), dtype=jnp.float32) * 0.02
        W_qv = jax.random.normal(k5, (4 * D, D), dtype=jnp.float32) * 0.02
        b_qv = jax.random.normal(k6, (D,), dtype=jnp.float32) * 0.02
        return {'encoder_hc': encoder_hc, 'decoder_hq': decoder_hq, 'w_sim': w_sim, 'b_sim': b_sim, 'W_qv': W_qv, 'b_qv': b_qv}
    _L1_xattn_all = _L1_xattn_setup()
    _L1_xattn_in = {k: v for k, v in _L1_xattn_all.items() if k in ('w_sim', 'b_sim', 'W_qv', 'b_qv')}
    del _L1_xattn_all

    def _L1_ffn_setup():
        import jax, jax.numpy as jnp
        import numpy as np
        DIM = 128
        MOE_HID = 64
        SHARED_HID = 256
        N_EXPERTS = 16
        TOP_K = 2
        NORM_TOPK_PROB = True
        key = jax.random.key(seed)
        ks = jax.random.split(key, 9)
        s = 0.02
        x = jax.random.normal(ks[0], (2, 128, DIM), dtype=jnp.float32)
        Wg = jax.random.normal(ks[1], (N_EXPERTS, DIM), dtype=jnp.float32) * s
        We_gate = jax.random.normal(ks[2], (N_EXPERTS, MOE_HID, DIM), dtype=jnp.float32) * s
        We_up = jax.random.normal(ks[3], (N_EXPERTS, MOE_HID, DIM), dtype=jnp.float32) * s
        We_down = jax.random.normal(ks[4], (N_EXPERTS, DIM, MOE_HID), dtype=jnp.float32) * s
        Ws_gate = jax.random.normal(ks[5], (SHARED_HID, DIM), dtype=jnp.float32) * s
        Ws_up = jax.random.normal(ks[6], (SHARED_HID, DIM), dtype=jnp.float32) * s
        Ws_down = jax.random.normal(ks[7], (DIM, SHARED_HID), dtype=jnp.float32) * s
        Wsg = jax.random.normal(ks[8], (1, DIM), dtype=jnp.float32) * s
        return {'x': x, 'Wg': Wg, 'We_gate': We_gate, 'We_up': We_up, 'We_down': We_down, 'Ws_gate': Ws_gate, 'Ws_up': Ws_up, 'Ws_down': Ws_down, 'Wsg': Wsg}
    _L1_ffn_all = _L1_ffn_setup()
    _L1_ffn_in = {k: v for k, v in _L1_ffn_all.items() if k in ('Wg', 'We_gate', 'We_up', 'We_down', 'Ws_gate', 'Ws_up', 'Ws_down', 'Wsg')}
    del _L1_ffn_all
    return {'x': x, 'ctx_1024': ctx_1024, 'g_xattn': g_xattn, 'g_ffn': g_ffn, 'L0_xattn_Wq': _L0_xattn_in['Wq'], 'L0_xattn_bq': _L0_xattn_in['bq'], 'L0_xattn_Wk': _L0_xattn_in['Wk'], 'L0_xattn_bk': _L0_xattn_in['bk'], 'L0_xattn_Wv': _L0_xattn_in['Wv'], 'L0_xattn_bv': _L0_xattn_in['bv'], 'L0_xattn_Wo': _L0_xattn_in['Wo'], 'L0_xattn_bo': _L0_xattn_in['bo'], 'L0_ffn_norm1_w': _L0_ffn_in['norm1_w'], 'L0_ffn_norm2_w': _L0_ffn_in['norm2_w'], 'L0_ffn_wq': _L0_ffn_in['wq'], 'L0_ffn_wk': _L0_ffn_in['wk'], 'L0_ffn_wv': _L0_ffn_in['wv'], 'L0_ffn_wo': _L0_ffn_in['wo'], 'L0_ffn_router_w': _L0_ffn_in['router_w'], 'L0_ffn_sh_gate': _L0_ffn_in['sh_gate'], 'L0_ffn_sh_up': _L0_ffn_in['sh_up'], 'L0_ffn_sh_down': _L0_ffn_in['sh_down'], 'L0_ffn_e_gate': _L0_ffn_in['e_gate'], 'L0_ffn_e_up': _L0_ffn_in['e_up'], 'L0_ffn_e_down': _L0_ffn_in['e_down'], 'L1_xattn_w_sim': _L1_xattn_in['w_sim'], 'L1_xattn_b_sim': _L1_xattn_in['b_sim'], 'L1_xattn_W_qv': _L1_xattn_in['W_qv'], 'L1_xattn_b_qv': _L1_xattn_in['b_qv'], 'L1_ffn_Wg': _L1_ffn_in['Wg'], 'L1_ffn_We_gate': _L1_ffn_in['We_gate'], 'L1_ffn_We_up': _L1_ffn_in['We_up'], 'L1_ffn_We_down': _L1_ffn_in['We_down'], 'L1_ffn_Ws_gate': _L1_ffn_in['Ws_gate'], 'L1_ffn_Ws_up': _L1_ffn_in['Ws_up'], 'L1_ffn_Ws_down': _L1_ffn_in['Ws_down'], 'L1_ffn_Wsg': _L1_ffn_in['Wsg']}

def reference(x, ctx_1024, g_xattn, g_ffn, L0_xattn_Wq, L0_xattn_bq, L0_xattn_Wk, L0_xattn_bk, L0_xattn_Wv, L0_xattn_bv, L0_xattn_Wo, L0_xattn_bo, L0_ffn_norm1_w, L0_ffn_norm2_w, L0_ffn_wq, L0_ffn_wk, L0_ffn_wv, L0_ffn_wo, L0_ffn_router_w, L0_ffn_sh_gate, L0_ffn_sh_up, L0_ffn_sh_down, L0_ffn_e_gate, L0_ffn_e_up, L0_ffn_e_down, L1_xattn_w_sim, L1_xattn_b_sim, L1_xattn_W_qv, L1_xattn_b_qv, L1_ffn_Wg, L1_ffn_We_gate, L1_ffn_We_up, L1_ffn_We_down, L1_ffn_Ws_gate, L1_ffn_Ws_up, L1_ffn_Ws_down, L1_ffn_Wsg):
    import jax
    import jax.numpy as jnp

    def _L0_xattn_ref(q, k, v, Wq, bq, Wk, bk, Wv, bv, Wo, bo):
        import math
        import jax, jax.numpy as jnp
        import numpy as np
        B, TQ, TK, D = (4, 256, 1024, 128)
        N_HEAD = 16
        STRIDE = 16
        Bb, Tq, Dd = q.shape
        Tk = k.shape[1]
        H, dh, s = (N_HEAD, Dd // N_HEAD, STRIDE)
        Q = (q @ Wq.T + bq).reshape(Bb, Tq, H, dh).transpose(0, 2, 1, 3)
        K = (k @ Wk.T + bk).reshape(Bb, Tk, H, dh).transpose(0, 2, 1, 3)
        V = (v @ Wv.T + bv).reshape(Bb, Tk, H, dh).transpose(0, 2, 1, 3)
        L = Tk // s
        idx = jnp.arange(H)[:, None] + s * jnp.arange(L)[None, :]
        Kg = jnp.take_along_axis(K, idx[None, :, :, None], axis=2)
        Vg = jnp.take_along_axis(V, idx[None, :, :, None], axis=2)
        scores = jnp.einsum('bhqd,bhld->bhql', Q, Kg) / math.sqrt(dh)
        attn = jax.nn.softmax(scores, axis=-1)
        out = jnp.einsum('bhql,bhld->bhqd', attn, Vg)
        out = out.transpose(0, 2, 1, 3).reshape(Bb, Tq, Dd)
        return out @ Wo.T + bo

    def _L0_ffn_ref(X, norm1_w, norm2_w, wq, wk, wv, wo, router_w, sh_gate, sh_up, sh_down, e_gate, e_up, e_down):
        import jax, jax.numpy as jnp
        import numpy as np
        D_MODEL = 128
        N_HEADS = 16
        D_HEAD = D_MODEL // N_HEADS
        N_EXPERTS = 8
        TOP_K = 2
        D_FF = 256
        EPS = 1e-06

        def rmsnorm(x, w):
            return x * jax.lax.rsqrt(jnp.mean(x * x, axis=-1, keepdims=True) + EPS) * w

        def swiglu(x, w_gate, w_up, w_down):
            return jax.nn.silu(x @ w_gate) * (x @ w_up) @ w_down
        B, S, d = X.shape
        scale = 1.0 / jnp.sqrt(jnp.asarray(D_HEAD, X.dtype))
        h = rmsnorm(X, norm1_w)
        q = (h @ wq).reshape(B, S, N_HEADS, D_HEAD)
        k = (h @ wk).reshape(B, S, N_HEADS, D_HEAD)
        v = (h @ wv).reshape(B, S, N_HEADS, D_HEAD)
        scores = jnp.einsum('bshd,bthd->bhst', q, k) * scale
        attn = jax.nn.softmax(scores, axis=-1)
        ctx = jnp.einsum('bhst,bthd->bshd', attn, v).reshape(B, S, d)
        X = X + ctx @ wo
        h2 = rmsnorm(X, norm2_w).reshape(B * S, d)
        logits = h2 @ router_w
        probs = jax.nn.softmax(logits, axis=-1)
        topw, topi = jax.lax.top_k(probs, TOP_K)
        topw = jax.nn.softmax(topw, axis=-1)
        combine = jnp.sum(jax.nn.one_hot(topi, N_EXPERTS, dtype=h2.dtype) * topw[..., None], axis=1)
        shared = swiglu(h2, sh_gate, sh_up, sh_down)
        gate = jnp.einsum('td,edf->etf', h2, e_gate)
        up = jnp.einsum('td,edf->etf', h2, e_up)
        eout = jnp.einsum('etf,efd->etd', jax.nn.silu(gate) * up, e_down)
        spec = jnp.einsum('etd,te->td', eout, combine)
        moe_out = (shared + spec).reshape(B, S, d)
        return X + moe_out

    def _L1_xattn_ref(encoder_hc, decoder_hq, w_sim, b_sim, W_qv, b_qv):
        import jax, jax.numpy as jnp
        import numpy as np
        B, L_ENC, L_DEC, D = (16, 64, 128, 128)
        d = encoder_hc.shape[-1]
        w1, w2, w3 = (w_sim[:d], w_sim[d:2 * d], w_sim[2 * d:])
        Sim = (encoder_hc @ w1)[:, :, None] + (decoder_hq @ w2)[:, None, :] + jnp.einsum('bid,bjd->bij', encoder_hc * w3, decoder_hq) + b_sim[0]
        A = jax.nn.softmax(Sim, axis=2)
        hq_hat = jnp.einsum('bij,bjd->bid', A, decoder_hq)
        Batt = jax.nn.softmax(jnp.max(Sim, axis=2), axis=1)
        hc_bar = jnp.einsum('bi,bid->bd', Batt, encoder_hc)[:, None, :]
        hc_hat = jnp.broadcast_to(hc_bar, encoder_hc.shape)
        feats = jnp.concatenate([encoder_hc, hq_hat, encoder_hc * hq_hat, encoder_hc * hc_hat], axis=-1)
        hcq = feats @ W_qv + b_qv
        return hcq

    def _L1_ffn_ref(x, Wg, We_gate, We_up, We_down, Ws_gate, Ws_up, Ws_down, Wsg):
        import jax, jax.numpy as jnp
        import numpy as np
        DIM = 128
        MOE_HID = 64
        SHARED_HID = 256
        N_EXPERTS = 16
        TOP_K = 2
        NORM_TOPK_PROB = True
        B, S, D = x.shape
        xt = x.reshape(-1, D)
        gates = jax.nn.softmax(xt @ Wg.T, axis=-1)
        scores, inds = jax.lax.top_k(gates, TOP_K)
        if NORM_TOPK_PROB:
            scores = scores / jnp.sum(scores, axis=-1, keepdims=True)
        g = jnp.einsum('td,ehd->teh', xt, We_gate)
        u = jnp.einsum('td,ehd->teh', xt, We_up)
        h = jax.nn.silu(g) * u
        y_all = jnp.einsum('teh,edh->ted', h, We_down)
        y_sel = jnp.take_along_axis(y_all, inds[:, :, None], axis=1)
        y = jnp.sum(y_sel * scores[:, :, None], axis=1)
        shared = jax.nn.silu(xt @ Ws_gate.T) * (xt @ Ws_up.T) @ Ws_down.T
        y = y + jax.nn.sigmoid(xt @ Wsg.T) * shared
        return y.reshape(B, S, D)
    x = x + jnp.tanh(g_xattn[0]) * _L0_xattn_ref(_layernorm(x, axis=-1), ctx_1024, ctx_1024, L0_xattn_Wq, L0_xattn_bq, L0_xattn_Wk, L0_xattn_bk, L0_xattn_Wv, L0_xattn_bv, L0_xattn_Wo, L0_xattn_bo)
    x = x + jnp.tanh(g_ffn[0]) * _L0_ffn_ref(_layernorm(x, axis=-1), L0_ffn_norm1_w, L0_ffn_norm2_w, L0_ffn_wq, L0_ffn_wk, L0_ffn_wv, L0_ffn_wo, L0_ffn_router_w, L0_ffn_sh_gate, L0_ffn_sh_up, L0_ffn_sh_down, L0_ffn_e_gate, L0_ffn_e_up, L0_ffn_e_down)
    x = x + jnp.tanh(g_xattn[1]) * _L1_xattn_ref(_layernorm(x, axis=-1), ctx_1024, L1_xattn_w_sim, L1_xattn_b_sim, L1_xattn_W_qv, L1_xattn_b_qv)
    x = x + jnp.tanh(g_ffn[1]) * _L1_ffn_ref(_layernorm(x, axis=-1), L1_ffn_Wg, L1_ffn_We_gate, L1_ffn_We_up, L1_ffn_We_down, L1_ffn_Ws_gate, L1_ffn_Ws_up, L1_ffn_Ws_down, L1_ffn_Wsg)
    return x

_drawn_inputs = setup_inputs


def setup_inputs(seed=0):
    import zlib

    import numpy as np

    out = dict(_drawn_inputs(seed))
    spreads = {'g_ffn': (-1.0, 0.6),
     'L0_xattn_bq': (0.0, 0.8),
     'L0_xattn_bk': (0.0, 0.8),
     'L0_xattn_bv': (0.0, 0.404),
     'L0_xattn_bo': (0.0, 0.1),
     'L0_ffn_norm1_w': (1.0, 0.6),
     'L0_ffn_norm2_w': (1.0, 0.6)}
    factors = {'L0_xattn_Wq': 8.0,
     'L0_xattn_Wk': 8.0,
     'L0_ffn_wq': 8.0,
     'L0_ffn_wk': 8.0,
     'L0_ffn_router_w': 3.229,
     'L0_ffn_e_gate': 2.791,
     'L0_ffn_e_up': 2.792,
     'L0_ffn_e_down': 2.774,
     'L1_ffn_Wg': 8.0,
     'L1_ffn_We_gate': 8.0,
     'L1_ffn_We_up': 8.0,
     'L1_ffn_We_down': 8.0,
     'L1_ffn_Ws_gate': 6.265,
     'L1_ffn_Ws_up': 6.187,
     'L1_ffn_Ws_down': 6.189,
     'L1_ffn_Wsg': 8.0}
    for name, (base, spread) in spreads.items():
        noise = np.random.default_rng([zlib.crc32(name.encode()), seed]).standard_normal(out[name].shape)
        drawn = base * np.exp(spread * noise) if base else spread * noise
        out[name] = jnp.asarray(drawn.astype(out[name].dtype))
    for name, factor in factors.items():
        out[name] = (out[name] * factor).astype(out[name].dtype)
    return out
```

```python
from contextlib import ExitStack

import concourse.bass as bass
from concourse import mybir

F32 = mybir.dt.float32
BF16 = mybir.dt.bfloat16
I32 = mybir.dt.int32
U32 = mybir.dt.uint32
ALU = mybir.AluOpType
ACT = mybir.ActivationFunctionType
AX = mybir.AxisListType

P = 128
B = 16
D = 128
H = 16
DH = D // H
TC = 77
L = TC // H
NK = L * H
G = 4
GB = B // G
GT = GB * P
SCALE = float(DH) ** -0.5
LN_EPS = 1e-5
RMS_EPS = 1e-6
RSQRT_SEED = float(0x5F3759DF)
SLOT = 64
VW = 9
PV_N = 96
VA_W = VW * (H - 1) + PV_N
E0, F0 = 8, 256
E1, F1 = 16, 64
PIECE = 32


def build(nc, a, out):
    NC0 = E0 * F0 // P
    NC1 = E1 * F1 // P
    TURNS = [(0, 4), (4, 8), (8, 10)]
    MOE = [dict(n=NC0, s=2, per=F0 // P), dict(n=NC1, s=2, per=1)]

    with ExitStack() as ctx:
        def sb(name, shape, dt=F32):
            return ctx.enter_context(nc.sbuf_tensor(name, shape, dt))

        def sem(name):
            return ctx.enter_context(nc.semaphore(name))

        PS = ctx.enter_context(nc.psum_tensor("PS", [P, 8, 512], F32))

        X = sb("X", [P, B, D])
        Z = sb("Z", [P, B, D])
        ctx_nat = sb("ctx_nat", [TC, B, D])
        ctx_t = sb("ctx_t", [P, B, TC])
        stats = sb("stats", [P, B, 6])
        mean, var, rstd, nmr, r2 = (sb(n, [P, B]) for n in ("mean", "var", "rstd", "nmr", "r2"))
        t_a, t_b, t_c = (sb(n, [P, B]) for n in ("t_a", "t_b", "t_c"))
        identf = sb("identf", [P, P])
        identb = sb("identb", [P, P], BF16)
        hmask = sb("hmask", [P, H])
        gates = sb("gates", [P, 4])
        tg = sb("tg", [P, 4])
        bq_c, bk_c, bv_c, n1w, n2w, w2s, w3s = (sb(n, [P, 1]) for n in ("bq_c", "bk_c", "bv_c", "n1w", "n2w", "w2s", "w3s"))
        bo_r = sb("bo_r", [P, D])
        bqv_r = sb("bqv_r", [P, D])
        w1_c = sb("w1_c", [P, 1])
        bsim_c = sb("bsim_c", [P, 1])
        w_nat = sb("w_nat", [P, 4, D])
        w_t = sb("w_t", [P, 4, D])
        wqkv = sb("wqkv", [P, 3 * D])
        wo = sb("wo", [P, D])
        wqv = sb("wqv", [P, 4, D])
        wr0 = sb("wr0", [P, E0])
        wr1_nat = sb("wr1_nat", [E1 + 1, D])
        wr1 = sb("wr1", [P, E1 + 1])
        WG = [sb(f"WG{m}", [P, MOE[m]["n"] + 2, P]) for m in range(2)]
        WU = [sb(f"WU{m}", [P, MOE[m]["n"] + 2, P]) for m in range(2)]
        WD = [sb(f"WD{m}", [P, MOE[m]["n"] + 2, P]) for m in range(2)]
        w_turn = [sb(f"w_turn{k}", [P, NC1 + 2, P]) for k in range(3)]

        work = [sb(f"work{k}", [P, GT]) for k in range(8)]

        at_one = {"pe": [], "act": [], "dve": [], "pool": []}

        def stage(name, **by):
            made = {}
            for eng, names in by.items():
                for n in names.split():
                    made[n] = sem(f"{name}_{n}")
                    at_one[eng].append(made[n])
            return made

        x_in = sem("x_in")
        ctx_in = sem("ctx_in")
        small_in = sem("small_in")
        wa_in = sem("wa_in")
        wb_in = sem("wb_in")
        m0_in = sem("m0_in")
        m1_in = sem("m1_in")
        turn_in = sem("turn_in")
        turned = sem("turned")
        turn_ps = sem("turn_ps")
        consts = sem("consts")
        pool_c = sem("pool_c")
        dve_c = sem("dve_c")
        tg_ready = sem("tg_ready")
        pre_ps = sem("pre_ps")
        pre_sb = sem("pre_sb")
        out_done = sem("out_done")
        x_final = sem("x_final")
        at_one["dve"].append(x_final)

        a_sem = stage("a", pe="t kv v2 s pt y", act="xt e pt_sb", dve="xn qkv_sb v2_sb d p x")
        a_chain = sem("a_chain")
        XG = sb("XG", [P, GB, D])
        XGT = sb("XGT", [P, GT])
        QA = work[0]
        KA4 = sb("KA4", [P, GB, NK])
        VA4 = sb("VA4", [P, GB, NK])
        V2 = work[1][:, 0:2 * D].rearrange("p (b d) -> p b d", b=2)
        mxA = sb("mxA", [P, GB, H])
        PA = sb("PA", [P, GB, L, H])
        PAT = work[2][:, 0:2 * P]

        b_sem = stage("b", pe="t qkv k_t q_t s qm_t st pv ct wo", act="xt h q_sb qm_sb exp ct_sb",
                      dve="xn t32 v split k_sb max m norm z zs", pool="z0")
        b_chain = sem("b_chain")
        XNB = [sb(f"XNB{u}", [P, D]) for u in range(2)]
        XNT = [sb(f"XNT{u}", [P, D]) for u in range(2)]
        T32 = sb("T32", [P, 2, D])
        QS = [sb(f"QS{u}", [P, H, SLOT], BF16) for u in range(2)]
        KS = [sb(f"KS{u}", [P, H, SLOT], BF16) for u in range(2)]
        KT = [[sb(f"KT{u}{v}", [P, H // 2, P], BF16) for v in range(2)] for u in range(2)]
        QT = sb("QT", [P, H // 2, P], BF16)
        QM = [sb(f"QM{u}", [P, H // 2, P], BF16) for u in range(2)]
        nmax = sb("nmax", [P, H])
        EX = work[3:5]
        VAH = sb("VAH", [P, B * VA_W])
        VA = VAH[:].rearrange("p (b c) -> p b c", b=B)
        rden = sb("rden", [P, H])
        CN = sb("CN", [P, H, DH])
        CT = sb("CT", [P, D])

        r_sem = [stage(f"r{m}", pe="t lg ct", act="ht ct_sb", dve="h e1 e2 cs") for m in range(2)]
        r_chain = [sem(f"r{m}_chain") for m in range(2)]
        m_sem = [stage(f"m{m}", pe="bc g u yc y yn", act="bc_sb silu yt", dve="hid yx x", pool="scaled") for m in range(2)]
        HG, HT = XG, XGT
        H2T = VAH[:, 0:B * P]
        LG = sb("LG", [P, B, E1 + 1])
        PR = sb("PR", [P, B, E1])
        top = sb("top", [P, B, 8])
        topi = sb("topi", [P, B, 8], U32)
        topf = sb("topf", [P, B, 2])
        iota_i = sb("iota_i", [P, E1], I32)
        iota_e = sb("iota_e", [P, E1])
        wsel = sb("wsel", [P, B, 2])
        comb = sb("comb", [P, B, E1 + 1])
        combt = sb("combt", [P, B, E1 + 1])
        CS = sb("CS", [P, B, P], BF16)
        CWT = VAH[:, B * P:B * P + B * P // 2].bitcast(BF16)
        sel0 = sb("sel0", [P, E0, P], BF16)
        sel1 = sb("sel1", [P, NC1 + 1, P], BF16)
        SEL = [sel0, sel1]
        BC = work[0:2]
        SG = work[2:4]
        SC = work[4:6]
        HH = work[6:8]
        YT = sb("YT", [P, GT])
        YX = sb("YX", [P, GT])

        c_sem = stage("c", pe="t s bt at bbt hq hc o", act="xt exp bexp at_sb hq_sb",
                      dve="xn e3 mx a bb bc hcr xh x", pool="cg xb")
        c_chain = sem("c_chain")
        CG = work[0][0:TC].rearrange("p (b d) -> p b d", b=GB)
        E3T = work[1]
        AM = work[2][:, 0:GB * TC].rearrange("p (b t) -> p b t", b=GB)
        nmx, suma, rca, bt = (sb(n, [P, GB]) for n in ("nmx", "suma", "rca", "bt"))
        AMT = work[3][0:TC]
        BB = sb("BB", [P, P])
        bm, bs = sb("bm", [GB, 1]), sb("bs", [GB, 2])
        BCOL = sb("BCOL", [P, GB])
        HC = sb("HC", [P, GB])
        WB = work[4][:].rearrange("p (b d) -> p b d", b=GB)
        HQ = work[5]
        XH = work[6]
        tgb = sb("tgb", [P, D])
        ln_chain = sem("ln_chain")
        phase_x = sem("phase_x")

        block = ctx.enter_context(nc.Block())

        def have(eng, s, n):
            eng.wait_ge(s, n + 1)

        def row(ap, n):
            return ap.rearrange("(a n) -> a n", a=1).broadcast_to([n, ap.shape[0]])

        def col(ap):
            return ap.rearrange("(n a) -> n a", a=1)

        @block.sync
        def _(sp):
            sp.dma_start(X[:], a["x"].rearrange("b s d -> s b d")).then_inc(x_in, 16)
            sp.dma_start(ctx_nat[:], a["ctx_1024"].rearrange("b s d -> s b d")).then_inc(ctx_in, 16)
            for i, n in enumerate(("Wq", "Wk", "Wv", "Wo")):
                sp.dma_start(w_nat[:, i, :], a["L0_xattn_" + n]).then_inc(wa_in, 16)
            for i, n in enumerate(("wq", "wk", "wv")):
                sp.dma_start(wqkv[:, i * D:(i + 1) * D], a["L0_ffn_" + n]).then_inc(wb_in, 16)
            sp.dma_start(wo[:], a["L0_ffn_wo"]).then_inc(wb_in, 16)
            sp.dma_start(wr0[:], a["L0_ffn_router_w"]).then_inc(m0_in, 16)
            for W, n in ((WG, "gate"), (WU, "up")):
                sp.dma_start(W[0][:, 0:NC0, :].rearrange("d (e f) c -> d e (f c)", e=E0),
                             a["L0_ffn_e_" + n].rearrange("e d f -> d e f")).then_inc(m0_in, 16)
                sp.dma_start(W[0][:, NC0:NC0 + 2, :].rearrange("d a c -> d (a c)"), a["L0_ffn_sh_" + n]).then_inc(m0_in, 16)
            sp.dma_start(WD[0][:, 0:NC0, :], a["L0_ffn_e_down"].rearrange("e (c f) d -> f (e c) d", c=F0 // P)).then_inc(m0_in, 16)
            sp.dma_start(WD[0][:, NC0:NC0 + 2, :], a["L0_ffn_sh_down"].rearrange("(c f) d -> f c d", f=P)).then_inc(m0_in, 16)
            sp.dma_start(wqv[:], a["L1_xattn_W_qv"].rearrange("(k d) n -> d k n", d=D)).then_inc(m1_in, 16)
            sp.dma_start(wr1_nat[0:E1, :], a["L1_ffn_Wg"]).then_inc(m1_in, 16)
            sp.dma_start(wr1_nat[E1:E1 + 1, :], a["L1_ffn_Wsg"]).then_inc(m1_in, 16)
            for k, n in enumerate(("gate", "up")):
                sp.dma_start(w_turn[k][:, 0:NC1, :],
                             a[f"L1_ffn_We_{n}"].rearrange("(c a) f d -> (a f) c d", a=2)).then_inc(turn_in, 16)
                sp.dma_start(w_turn[k][:, NC1:NC1 + 2, :],
                             a[f"L1_ffn_Ws_{n}"].rearrange("(c f) d -> f c d", f=P)).then_inc(turn_in, 16)
            sp.dma_start(w_turn[2][:, 0:NC1, :].rearrange("d c (a f) -> d (c a) f", a=2),
                         a["L1_ffn_We_down"].rearrange("e d f -> d e f")).then_inc(turn_in, 16)
            sp.dma_start(w_turn[2][:, NC1:NC1 + 2, :].rearrange("d a f -> d (a f)"), a["L1_ffn_Ws_down"]).then_inc(turn_in, 16)
            for g in range(G):
                have(sp, x_final, g + 1)
                sp.dma_start(out[g * GB:(g + 1) * GB].rearrange("b s d -> s b d"), X[:, g * GB:(g + 1) * GB, :]).then_inc(out_done, 16)
            sp.wait_ge(out_done, 16 * G)

        @block.gpsimd
        def _(pool):
            for s in at_one["pool"]:
                pool.sem_inc(s, 1)
            n = [0]

            def step(ins):
                n[0] += 1
                ins.then_inc(pool_c, 1)
                pool.wait_ge(pool_c, n[0])

            step(pool.memset(identf[:], 0.0))
            step(pool.affine_select(out=identf[:], in_=identf[:], compare_op=ALU.not_equal, fill=1.0, base=0,
                                    pattern=[[-1, P]], channel_multiplier=1))
            step(pool.tensor_copy(identb[:], identf[:]))
            step(pool.memset(hmask[:], 1.0))
            step(pool.affine_select(out=hmask[:], in_=hmask[:], compare_op=ALU.is_ge, fill=0.0, base=0,
                                    pattern=[[-DH, H]], channel_multiplier=1))
            step(pool.affine_select(out=hmask[:], in_=hmask[:], compare_op=ALU.is_ge, fill=0.0, base=DH - 1,
                                    pattern=[[DH, H]], channel_multiplier=-1))
            pool.memset(VA, 1.0)
            pool.memset(BB[:], 0.0)
            for u in range(2):
                pool.memset(QS[u][:].bitcast(F32), 0.0)
                step(pool.memset(KS[u][:].bitcast(F32), 0.0))
                pool.memset(KS[u][:, :, 48:50], 1.0)
                pool.memset(KT[u][0][:].bitcast(F32), 0.0)
                pool.memset(KT[u][1][:].bitcast(F32), 0.0)
            step(pool.memset(CS[:].bitcast(F32), 0.0))
            pool.memset(bm[:], 0.0).then_inc(consts, 1)
            pool.iota(iota_i[:], pattern=[[1, E1]], base=0, channel_multiplier=0).then_inc(pool_c, 1)
            n[0] += 1
            pool.memset(sel0[:].bitcast(F32), 0.0)
            step(pool.memset(sel1[:].bitcast(F32), 0.0))
            step(pool.tensor_copy(iota_e[:], iota_i[:]))
            for p in range(3):
                step(pool.affine_select(out=sel0[:], in_=sel0[:], compare_op=ALU.not_equal, fill=1.0,
                                        base=-PIECE * p, pattern=[[-1, E0], [0, P]], channel_multiplier=1))
                step(pool.affine_select(out=sel1[:, 0:NC1, :].rearrange("p c (a f) -> p c a f", a=2),
                                        in_=sel1[:, 0:NC1, :].rearrange("p c (a f) -> p c a f", a=2),
                                        compare_op=ALU.not_equal, fill=1.0, base=-PIECE * p,
                                        pattern=[[-2, NC1], [-1, 2], [0, F1]], channel_multiplier=1))
                step(pool.affine_select(out=sel1[:, NC1, :], in_=sel1[:, NC1, :],
                                        compare_op=ALU.not_equal, fill=1.0, base=-PIECE * p - E1,
                                        pattern=[[0, P]], channel_multiplier=1))
            pool.memset(bm[:], 0.0).then_inc(consts, 1)
            with pool.Fori(0, B // 2) as i:
                for u in range(2):
                    b = i * 2 + u
                    have(pool, b_sem["xn"], b + 1)
                    pool.tensor_copy(Z[:, b, :], XNB[u][:]).then_inc(b_sem["z0"], 1)

            def scale_hidden(m):
                M = MOE[m]
                with pool.Fori(0, G) as g:
                    k = 0
                    for c in range(M["n"] + M["s"]):
                        if m == 0 and c >= M["n"]:
                            continue
                        e = min(c // M["per"], M["n"] // M["per"])
                        ne = M["n"] // M["per"] + (m == 1)
                        have(pool, m_sem[m]["silu"], g * (M["n"] + 2) + c + 1)
                        have(pool, m_sem[m]["bc_sb"], g * ne + e + 1)
                        if c >= 2:
                            have(pool, m_sem[m]["hid"], g * (M["n"] + 2) + c - 1)
                        else:
                            have(pool, m_sem[m]["hid"], g * (M["n"] + 2))
                        pool.tensor_tensor(SC[c % 2][:], SG[c % 2][:], BC[e % 2][:], ALU.mult).then_inc(m_sem[m]["scaled"], 1)
                        k += 1

            scale_hidden(0)
            have(pool, m_sem[0]["x"], 2 * G)
            with pool.Fori(0, G) as g:
                have(pool, c_sem["hq"], g)
                pool.tensor_copy(CG, ctx_nat[:, bass.ds(g * GB, GB), :]).then_inc(c_sem["cg"], 1)
                have(pool, c_sem["xn"], g + 1)
                Xg = X[:, bass.ds(g * GB, GB), :]
                pool.tensor_tensor(Xg, Xg, tgb[:].unsqueeze(1).broadcast_to([P, GB, D]), ALU.add).then_inc(c_sem["xb"], 1)
            scale_hidden(1)

        @block.scalar
        def _(act):
            smalls = [(gates[:, 0:2], row(a["g_xattn"], P)), (gates[:, 2:4], row(a["g_ffn"], P)),
                      (bq_c[:], col(a["L0_xattn_bq"])), (bk_c[:], col(a["L0_xattn_bk"])), (bv_c[:], col(a["L0_xattn_bv"])),
                      (bo_r[:], row(a["L0_xattn_bo"], P)), (n1w[:], col(a["L0_ffn_norm1_w"])), (n2w[:], col(a["L0_ffn_norm2_w"])),
                      (w1_c[:], col(a["L1_xattn_w_sim"][0:D])), (w2s[:], col(a["L1_xattn_w_sim"][D:2 * D])),
                      (w3s[:], col(a["L1_xattn_w_sim"][2 * D:3 * D])), (bsim_c[:], row(a["L1_xattn_b_sim"], P)),
                      (bqv_r[:], row(a["L1_xattn_b_qv"], P))]
            for dst, src in smalls:
                act.dma_start(dst, src).then_inc(small_in, 16)
            for s in at_one["act"]:
                act.sem_inc(s, 1)
            act.wait_ge(small_in, 16 * len(smalls))
            act.activation(tg[:], gates[:], ACT.Tanh).then_inc(tg_ready, 1)
            act.wait_ge(pre_ps, 1)
            act.activation(w_t[:].rearrange("p a b -> p (a b)"), PS[:, 0, :], ACT.Copy).then_inc(pre_sb, 1)
            for k in range(4):
                act.wait_ge(pre_ps, 2 + k)
                act.activation(ctx_t[:, 4 * k:4 * k + 4, :], PS[:, 1 + k, 0:4 * TC].rearrange("p (a b) -> p a b", a=4),
                               ACT.Copy).then_inc(pre_sb, 1)

            with act.Fori(0, G) as g:
                have(act, a_sem["t"], g + 1)
                have(act, a_sem["kv"], g)
                act.activation(XGT[:], PS[:, 0, :], ACT.Copy).then_inc(a_sem["xt"], 1)
                have(act, a_sem["d"], g + 1)
                act.activation(PA[:], PA[:], ACT.Exp, scale=SCALE).then_inc(a_sem["e"], 1)
                have(act, a_sem["pt"], g + 1)
                have(act, a_sem["y"], g)
                act.activation(PAT, PS[:, 5, 0:2 * P], ACT.Copy).then_inc(a_sem["pt_sb"], 1)

            def slot(s, u0):
                def batch(k):
                    return s + k, (u0 + k) % 2

                def ok(k):
                    return not isinstance(s, int) or 0 <= s + k < B

                def exp(k, j):
                    b, u = batch(k)
                    have(act, b_sem["st"], b * 4 + (j + 1))
                    if not (isinstance(b, int) and 4 * b + j < 2):
                        have(act, b_sem["pv"], b * 4 + (j - 1))
                    act.activation(EX[j % 2][:], PS[:, 2 + j % 2, :], ACT.Exp, scale=SCALE).then_inc(b_sem["exp"], 1)

                if ok(2):
                    b, u = batch(2)
                    have(act, b_sem["t"], b + 1)
                    act.activation(XNT[u][:], PS[:, 4, 3 * D:4 * D], ACT.Copy, scale=n1w[:]).then_inc(b_sem["xt"], 1)
                if ok(0):
                    exp(0, 1)
                    exp(0, 2)
                if ok(2):
                    b, u = batch(2)
                    have(act, b_sem["t32"], b + 1)
                    if not (isinstance(b, int) and b < 2):
                        have(act, b_sem["qm_t"], b - 1)
                    act.activation(QS[u][:, :, 0:24].rearrange("p h (c d) -> p h c d", c=3),
                                   T32[:, 0, :].rearrange("p (h d) -> p h d", h=H).unsqueeze(2).broadcast_to([P, H, 3, DH]),
                                   ACT.Copy).then_inc(b_sem["h"], 1)
                    act.activation(KS[u][:, :, 16:40].rearrange("p h (c d) -> p h c d", c=3),
                                   T32[:, 1, :].rearrange("p (h d) -> p h d", h=H).unsqueeze(2).broadcast_to([P, H, 3, DH]),
                                   ACT.Copy).then_inc(b_sem["h"], 1)
                if ok(0):
                    exp(0, 3)
                if ok(1):
                    b, u = batch(1)
                    have(act, b_sem["qm_t"], b + 1)
                    act.activation(QM[u][:].rearrange("p c s -> p (c s)"), PS[:, 5, :].bitcast(BF16), ACT.Copy).then_inc(b_sem["qm_sb"], 1)
                if ok(0):
                    b, u = batch(0)
                    have(act, b_sem["ct"], b + 1)
                    act.activation(CT[:], PS[:, 7, 232:360], ACT.Copy).then_inc(b_sem["ct_sb"], 1)
                if ok(2):
                    b, u = batch(2)
                    have(act, b_sem["q_t"], b + 1)
                    act.activation(QT[:].rearrange("p c s -> p (c s)"), PS[:, 5, :].bitcast(BF16), ACT.Copy).then_inc(b_sem["q_sb"], 1)
                if ok(1):
                    exp(1, 0)

            for s in range(-3, 0):
                slot(s, s % 2)
            with act.Fori(0, (B - 4) // 2) as i:
                for u in range(2):
                    slot(i * 2 + u, u)
            for s in range(B - 4, B):
                slot(s, s % 2)

            def router(m):
                R = r_sem[m]
                with act.Fori(0, G) as g:
                    have(act, R["t"], g + 1)
                    have(act, R["lg"], g)
                    scale = {"scale": n2w[:]} if m == 0 else {}
                    act.activation(HT[:], PS[:, 0, :], ACT.Copy, **scale).then_inc(R["ht"], 1)
                    act.activation(H2T[:, bass.ds(g * GT, GT)], PS[:, 0, :], ACT.Copy, **scale).then_inc(R["ht"], 1)
                have(act, R["e1"], 1)
                act.activation(LG[:], LG[:], ACT.Exp).then_inc(R["e1"], 1)
                if m == 0:
                    have(act, R["e2"], 1)
                    act.activation(wsel[:, :, 1], wsel[:, :, 1], ACT.Exp).then_inc(R["e2"], 1)
                for k in range(2):
                    have(act, R["ct"], k + 1)
                    act.activation(CWT[:, k * 1024:(k + 1) * 1024], PS[:, 2 + k, :].bitcast(BF16), ACT.Copy).then_inc(R["ct_sb"], 1)

            def mixture(m):
                M, S = MOE[m], m_sem[m]
                nch = M["n"] + M["s"]
                ne = M["n"] // M["per"] + (m == 1)
                with act.Fori(0, G) as g:
                    for c in range(nch):
                        e = min(c // M["per"], ne)
                        first = c % M["per"] == 0 if c < M["n"] else (m == 1 and c == M["n"])
                        if first:
                            have(act, S["bc"], g * ne + e + 1)
                            nsc = nch if m else M["n"]
                            done = max((e - 1) * M["per"], 0)
                            have(act, S["scaled"], g * nsc + done)
                            act.activation(BC[e % 2][:], PS[:, 4 + e % 2, :], ACT.Copy).then_inc(S["bc_sb"], 1)
                        have(act, S["g"], g * nch + c + 1)
                        have(act, S["hid"], g * nch + max(c - 1, 0))
                        act.activation(SG[c % 2][:], PS[:, c % 2, :], ACT.Silu).then_inc(S["silu"], 1)
                    have(act, S["y"], g + 1)
                    have(act, S["yn"], g)
                    act.activation(YT[:], PS[:, 6, :], ACT.Copy).then_inc(S["yt"], 1)

            router(0)
            mixture(0)

            for k, W in enumerate((WG[1], WU[1], WD[1])):
                for t, (c0, c1) in enumerate(TURNS):
                    act.wait_ge(turn_ps, 3 * k + t + 1)
                    act.activation(W[:, c0:c1, :], PS[:, (3 * k + t) % 8, 0:(c1 - c0) * P].rearrange("p (c f) -> p c f", f=P),
                                   ACT.Copy).then_inc(turned, 1)
            act.wait_ge(turn_ps, 10)
            act.activation(wr1[:], PS[:, 1, 0:E1 + 1], ACT.Copy).then_inc(turned, 1)

            with act.Fori(0, G) as g:
                have(act, c_sem["t"], g + 1)
                have(act, c_sem["o"], g)
                act.activation(XGT[:], PS[:, 0, :], ACT.Copy).then_inc(c_sem["xt"], 1)
                have(act, c_sem["mx"], g + 1)
                for j in range(GB):
                    act.activation(AM[:, j, :], PS[:, 1, j * TC:(j + 1) * TC], ACT.Exp, bias=nmx[:, j:j + 1],
                                   accum_out=suma[:, j:j + 1]).then_inc(c_sem["exp"], 1)
                have(act, c_sem["bt"], g * 2 + 2)
                act.activation(BB[0:GB, :], PS[0:GB, 3, 0:P], ACT.Exp, bias=bm[:], accum_out=bs[:, 0:1]).then_inc(c_sem["bexp"], 1)
                have(act, c_sem["at"], g + 1)
                act.activation(AMT, PS[0:TC, 2, :], ACT.Copy).then_inc(c_sem["at_sb"], 1)
                have(act, c_sem["hq"], g + 1)
                act.activation(HQ[:], PS[:, 4, :], ACT.Copy).then_inc(c_sem["hq_sb"], 1)

            router(1)
            mixture(1)

        @block.vector
        def _(dve):
            class Chain:

                def __init__(self, s, per):
                    self.s, self.per, self.k, self.base = s, per, 0, 0

                def begin(self, i):
                    self.base, self.k = i * self.per, 0

                def __call__(self, ins):
                    self.k += 1
                    ins.then_inc(self.s, 1)
                    dve.wait_ge(self.s, self.base + self.k)

                def end(self):
                    assert self.k == self.per, (self.k, self.per)

            lnc = Chain(ln_chain, 0)

            def rsqrt(dst, src, eps):
                lnc(dve.tensor_scalar(t_a[:], src, eps, None, ALU.add))
                lnc(dve.tensor_scalar(dst.bitcast(I32), t_a[:].bitcast(I32), -0.5, RSQRT_SEED, ALU.mult, ALU.add))
                for _ in range(3):
                    lnc(dve.scalar_tensor_tensor(out=t_b[:], in0=dst, scalar=-0.5, in1=dst, op0=ALU.mult, op1=ALU.mult))
                    lnc(dve.tensor_tensor(t_b[:], t_b[:], t_a[:], ALU.mult))
                    lnc(dve.scalar_tensor_tensor(out=dst, in0=t_b[:], scalar=1.5, in1=dst, op0=ALU.add, op1=ALU.mult))

            def moments():
                lnc(dve.tensor_tensor(t_a[:], stats[:, :, 1], stats[:, :, 4], ALU.add))
                lnc(dve.tensor_scalar(mean[:], t_a[:], 0.5, None, ALU.mult))
                lnc(dve.tensor_tensor(t_b[:], stats[:, :, 1], stats[:, :, 4], ALU.subtract))
                lnc(dve.scalar_tensor_tensor(out=t_c[:], in0=t_b[:], scalar=0.25, in1=t_b[:], op0=ALU.mult, op1=ALU.mult))
                lnc(dve.tensor_tensor(t_a[:], stats[:, :, 2], stats[:, :, 5], ALU.add))
                lnc(dve.scalar_tensor_tensor(out=var[:], in0=t_a[:], scalar=1.0 / D, in1=t_c[:], op0=ALU.mult, op1=ALU.add))

            def layernorm_scales():
                moments()
                rsqrt(rstd[:], var[:], LN_EPS)
                lnc(dve.scalar_tensor_tensor(out=nmr[:], in0=mean[:], scalar=-1.0, in1=rstd[:], op0=ALU.mult, op1=ALU.mult))

            def normalise(dst, b):
                return dve.tensor_scalar(dst, X[:, b, :], rstd[:, bass.ds(b, 1)], nmr[:, bass.ds(b, 1)], ALU.mult, ALU.add)

            for s in at_one["dve"]:
                dve.sem_inc(s, 1)
            dve.wait_ge(x_in, 16)
            with dve.Fori(0, B) as b:
                dve.bn_stats(stats[:, b, :], X[:, b, :]).then_inc(dve_c, 1)
            dve.wait_ge(dve_c, B)
            layernorm_scales()
            dve.wait_ge(small_in, 16 * 13)
            lnc(dve.tensor_scalar(bo_r[:], bo_r[:], 1.0 / H, None, ALU.mult))
            dve.wait_ge(tg_ready, 1)
            lnc(dve.tensor_scalar(tgb[:], bqv_r[:], tg[:, 1:2], None, ALU.mult))
            dve.wait_ge(consts, 1)

            A = Chain(a_chain, 4)
            with dve.Fori(0, G) as g:
                A.begin(g)
                have(dve, a_sem["t"], g)
                for j in range(GB):
                    ins = normalise(XG[:, j, :], g * GB + j)
                ins.then_inc(a_sem["xn"], 1)
                have(dve, a_sem["kv"], g + 1)
                have(dve, a_sem["s"], g)
                dve.tensor_scalar(QA[:], PS[:, 1, :], bq_c[:], None, ALU.add)
                mask = hmask[:].unsqueeze(1).broadcast_to([P, GB * L, H])
                for dst, off, bias in ((KA4, 0, bk_c), (VA4, GB * NK, bv_c)):
                    ins = dve.scalar_tensor_tensor(
                        out=dst[:].rearrange("p b (l h) -> p (b l) h", h=H),
                        in0=PS[:, 2, off:off + GB * NK].rearrange("p (a h) -> p a h", h=H),
                        scalar=bias[:], in1=mask, op0=ALU.add, op1=ALU.mult)
                ins.then_inc(a_sem["qkv_sb"], 1)
                have(dve, a_sem["v2"], g + 1)
                have(dve, a_sem["y"], g)
                dve.tensor_tensor(V2, PS[:, 3, 0:2 * D].rearrange("p (b d) -> p b d", b=2),
                                  bo_r[:].unsqueeze(1).broadcast_to([P, 2, D]), ALU.add).then_inc(a_sem["v2_sb"], 1)
                have(dve, a_sem["s"], g + 1)
                S4 = PS[:, 4, 0:GB * NK]
                A(dve.tensor_reduce(mxA[:], S4.rearrange("p (b l h) -> p b h l", b=GB, h=H), AX.X, ALU.max))
                have(dve, a_sem["pt"], g)
                dve.tensor_tensor(PA[:], S4.rearrange("p (b l h) -> p b l h", b=GB, h=H),
                                  mxA[:].unsqueeze(2).broadcast_to([P, GB, L, H]), ALU.subtract).then_inc(a_sem["d"], 1)
                have(dve, a_sem["e"], g + 1)
                A(dve.tensor_reduce(mxA[:], PA[:].rearrange("p b l h -> p b h l"), AX.X, ALU.add))
                A(dve.reciprocal(mxA[:], mxA[:]))
                dve.tensor_tensor(PA[:], PA[:], mxA[:].unsqueeze(2).broadcast_to([P, GB, L, H]), ALU.mult).then_inc(a_sem["p"], 1)
                have(dve, a_sem["y"], g + 1)
                Xg = X[:, bass.ds(g * GB, GB), :]
                for u in range(2):
                    Xu = Xg.rearrange("p (k u) d -> p k u d", u=2)[:, :, u, :]
                    ins = dve.scalar_tensor_tensor(out=Xu, in0=PS[:, 6 + u, 0:2 * D].rearrange("p (b d) -> p b d", b=2),
                                                   scalar=tg[:, 0:1], in1=Xu, op0=ALU.mult, op1=ALU.add)
                A(ins)
                for j in range(GB):
                    ins = dve.bn_stats(stats[:, g * GB + j, :], X[:, g * GB + j, :])
                ins.then_inc(a_sem["x"], 1)
                A.end()
            have(dve, a_sem["x"], G)
            layernorm_scales()
            lnc(dve.tensor_tensor(t_a[:], rstd[:], rstd[:], ALU.mult))
            lnc(dve.tensor_tensor(t_c[:], t_a[:], var[:], ALU.mult))
            rsqrt(r2[:], t_c[:], RMS_EPS)

            PER = 6
            Bc = Chain(b_chain, PER)

            def slot(s, u0):
                def batch(k):
                    return s + k, (u0 + k) % 2

                def ok(k):
                    return not isinstance(s, int) or 0 <= s + k < B

                def rowmax(j):
                    b, u = batch(1)
                    have(dve, b_sem["s"], b * 4 + (j + 1))
                    dve.tensor_reduce(nmax[:, 4 * j:4 * j + 4], PS[:, j % 2, :].rearrange("p (h t) -> p h t", h=4),
                                      AX.X, ALU.max, negate=True).then_inc(b_sem["max"], 1)

                if ok(1):
                    rowmax(0)
                    rowmax(1)
                    rowmax(2)
                if ok(2):
                    b, u = batch(2)
                    Bc.begin(b)
                    have(dve, b_sem["qkv"], b + 1)
                    dve.tensor_scalar(T32[:], PS[:, 4, 0:2 * D].rearrange("p (a d) -> p a d", a=2), r2[:, bass.ds(b, 1)], None,
                                      ALU.mult).then_inc(b_sem["t32"], 1)
                    dve.tensor_scalar(VA[:, b, 0:VW * H].rearrange("p (h d) -> p h d", h=H)[:, :, 0:DH],
                                      PS[:, 4, 2 * D:3 * D].rearrange("p (h d) -> p h d", h=H), r2[:, bass.ds(b, 1)], None,
                                      ALU.mult).then_inc(b_sem["v"], 1)
                if ok(1):
                    rowmax(3)
                    b, u = batch(1)
                    have(dve, b_sem["max"], b * 4 + 4)
                    have(dve, b_sem["q_t"], b + 1)
                    dve.tensor_copy(QS[u][:, :, 48], nmax[:]).then_inc(b_sem["m"], 1)
                    have(dve, b_sem["m"], b * 2 + 1)
                    dve.tensor_tensor(QS[u][:, :, 49], nmax[:], QS[u][:, :, 48], ALU.subtract).then_inc(b_sem["m"], 1)
                if ok(2):
                    b, u = batch(2)
                    have(dve, b_sem["h"], b * 2 + 2)
                    q, k = T32[:, 0, :].rearrange("p (h d) -> p h d", h=H), T32[:, 1, :].rearrange("p (h d) -> p h d", h=H)
                    Bc(dve.tensor_tensor(q, q, QS[u][:, :, 0:8], ALU.subtract))
                    Bc(dve.tensor_tensor(k, k, KS[u][:, :, 16:24], ALU.subtract))
                    Bc(dve.tensor_copy(QS[u][:, :, 32:48].rearrange("p h (c d) -> p h c d", c=2),
                                       q.unsqueeze(2).broadcast_to([P, H, 2, DH])))
                    Bc(dve.tensor_copy(KS[u][:].rearrange("p h (c d) -> p h c d", c=2)[:, :, :, 8:16],
                                       k.unsqueeze(2).broadcast_to([P, H, 2, DH])))
                    Bc(dve.memset(QS[u][:, :, 48:50], 0.0))
                    Bc(dve.tensor_tensor(QS[u][:, :, 24:32], q, QS[u][:, :, 32:40], ALU.subtract))
                    dve.tensor_tensor(KS[u][:, :, 0:8], k, KS[u][:, :, 8:16], ALU.subtract).then_inc(b_sem["split"], 1)
                    Bc.end()
                if ok(0):
                    b, u = batch(0)
                    O = PS[:, 7, 0:VW * H].rearrange("p (h d) -> p h d", h=H)
                    have(dve, b_sem["pv"], b * 4 + 4)
                    dve.reciprocal(rden[:], O[:, :, DH]).then_inc(b_sem["norm"], 1)
                    have(dve, b_sem["norm"], b * 2 + 1)
                    dve.tensor_tensor(CN[:], O[:, :, 0:DH], rden[:].unsqueeze(2).broadcast_to([P, H, DH]),
                                      ALU.mult).then_inc(b_sem["norm"], 1)
                if ok(2):
                    b, u = batch(2)
                    have(dve, b_sem["k_t"], b + 1)
                    src = PS[:, 6, :].bitcast(BF16)
                    dve.tensor_copy(KT[u][0][0:64].rearrange("p c s -> p (c s)"), src[0:64, :])
                    dve.tensor_copy(KT[u][1][64:128].rearrange("p c s -> p (c s)"), src[64:128, :]).then_inc(b_sem["k_sb"], 1)
                if ok(0):
                    b, u = batch(0)
                    have(dve, b_sem["wo"], b + 1)
                    have(dve, b_sem["z0"], b + 1)
                    dve.tensor_tensor(Z[:, b, :], PS[:, 7, 360:488], Z[:, b, :], ALU.add).then_inc(b_sem["z"], 1)
                    have(dve, b_sem["z"], b + 1)
                    dve.bn_stats(stats[:, b, :], Z[:, b, :]).then_inc(b_sem["zs"], 1)
                if ok(3):
                    b, u = batch(3)
                    if not (isinstance(b, int) and b < 2):
                        have(dve, b_sem["t"], b - 1)
                        have(dve, b_sem["z0"], b - 1)
                    normalise(XNB[u][:], b).then_inc(b_sem["xn"], 1)

            for s in range(-3, 0):
                slot(s, s % 2)
            with dve.Fori(0, (B - 4) // 2) as i:
                for u in range(2):
                    slot(i * 2 + u, u)
            for s in range(B - 4, B):
                slot(s, s % 2)
            have(dve, b_sem["zs"], B)
            moments()
            lnc(dve.tensor_tensor(t_c[:], mean[:], mean[:], ALU.mult))
            lnc(dve.tensor_tensor(t_c[:], t_c[:], var[:], ALU.add))
            rsqrt(r2[:], t_c[:], RMS_EPS)

            def router(m):
                R, E = r_sem[m], (E0, E1)[m]
                C = Chain(r_chain[m], 0)
                with dve.Fori(0, G) as g:
                    have(dve, R["t"], g)
                    for j in range(GB):
                        b = g * GB + j
                        if m == 0:
                            ins = dve.tensor_scalar(HG[:, j, :], Z[:, b, :], r2[:, bass.ds(b, 1)], None, ALU.mult)
                        else:
                            ins = normalise(HG[:, j, :], b)
                    ins.then_inc(R["h"], 1)
                EW = E + m
                have(dve, R["lg"], G)
                LGm = LG[:, :, 0:E]
                C(dve.tensor_copy(LG[:, :, 0:EW], PS[:, 1, 0:B * EW].rearrange("p (b e) -> p b e", b=B)))
                if m == 0:
                    C(dve.memset(LG[:, :, E:E1 + 1], 0.0))
                C(dve.tensor_reduce(t_b[:], LGm, AX.X, ALU.max))
                if m == 1:
                    C(dve.tensor_scalar(LG[:, :, E1:E1 + 1], LG[:, :, E1:E1 + 1], -1.0, None, ALU.mult))
                dve.tensor_tensor(LGm, LGm, t_b[:].unsqueeze(2).broadcast_to([P, B, E]), ALU.subtract).then_inc(R["e1"], 1)
                have(dve, R["e1"], 2)
                C(dve.tensor_reduce(t_b[:], LGm, AX.X, ALU.add))
                C(dve.reciprocal(t_b[:], t_b[:]))
                PRm = PR[:, :, 0:E]
                C(dve.tensor_tensor(PRm, LGm, t_b[:].unsqueeze(2).broadcast_to([P, B, E]), ALU.mult))
                for b in range(B):
                    ins = dve.max(top[:, b, :], PR[:, b, 0:E])
                C(ins)
                for b in range(B):
                    ins = dve.max_index(topi[:, b, :], top[:, b, :], PR[:, b, 0:E])
                C(ins)
                C(dve.tensor_copy(topf[:], topi[:, :, 0:2]))
                w0, w1 = wsel[:, :, 0], wsel[:, :, 1]
                if m == 0:
                    dve.tensor_tensor(w1, top[:, :, 1], top[:, :, 0], ALU.subtract).then_inc(R["e2"], 1)
                    have(dve, R["e2"], 2)
                    C(dve.tensor_scalar(t_b[:], w1, 1.0, None, ALU.add))
                    C(dve.reciprocal(w0, t_b[:]))
                    C(dve.tensor_tensor(w1, w1, w0, ALU.mult))
                else:
                    C(dve.tensor_tensor(t_b[:], top[:, :, 0], top[:, :, 1], ALU.add))
                    C(dve.reciprocal(t_b[:], t_b[:]))
                    C(dve.tensor_tensor(w0, top[:, :, 0], t_b[:], ALU.mult))
                    C(dve.tensor_tensor(w1, top[:, :, 1], t_b[:], ALU.mult))
                dve.wait_ge(consts, 2)
                io = iota_e[:, 0:E].unsqueeze(1).broadcast_to([P, B, E])
                cm, ct = comb[:, :, 0:E], combt[:, :, 0:E]
                C(dve.tensor_tensor(cm, io, topf[:, :, 0:1].broadcast_to([P, B, E]), ALU.is_equal))
                C(dve.tensor_tensor(cm, cm, wsel[:, :, 0:1].broadcast_to([P, B, E]), ALU.mult))
                C(dve.tensor_tensor(ct, io, topf[:, :, 1:2].broadcast_to([P, B, E]), ALU.is_equal))
                C(dve.tensor_tensor(ct, ct, wsel[:, :, 1:2].broadcast_to([P, B, E]), ALU.mult))
                C(dve.tensor_tensor(cm, cm, ct, ALU.add))
                if m == 1:
                    C(dve.tensor_scalar(comb[:, :, E1:E1 + 1], LG[:, :, E1:E1 + 1], 1.0, None, ALU.add))
                    C(dve.reciprocal(comb[:, :, E1:E1 + 1], comb[:, :, E1:E1 + 1]))
                cf = comb[:, :, 0:EW]
                for p in range(3):
                    piece = CS[:, :, p * PIECE:p * PIECE + EW]
                    ins = dve.tensor_copy(piece, cf)
                    if p == 2:
                        ins.then_inc(R["cs"], 1)
                    else:
                        C(ins)
                        C(dve.tensor_tensor(cf, cf, piece, ALU.subtract))

            def mixture(m):
                M, S = MOE[m], m_sem[m]
                nch = M["n"] + M["s"]
                nsc = nch if m else M["n"]
                with dve.Fori(0, G) as g:
                    for c in range(nch):
                        have(dve, S["u"], g * nch + c + 1)
                        if c < nsc:
                            have(dve, S["scaled"], g * nsc + c + 1)
                            act_part = SC[c % 2]
                        else:
                            have(dve, S["silu"], g * nch + c + 1)
                            act_part = SG[c % 2]
                        have(dve, S["y"], g) if c < 2 else have(dve, S["yc"], g * (nch - 1) + c - 1)
                        dve.tensor_tensor(HH[c % 2][:], PS[:, 2 + c % 2, :], act_part[:], ALU.mult).then_inc(S["hid"], 1)
                    have(dve, S["yn"], g + 1)
                    Xg, Zg = X[:, bass.ds(g * GB, GB), :], Z[:, bass.ds(g * GB, GB), :]
                    y = PS[:, 7, :].rearrange("p (b d) -> p b d", b=GB)
                    if m == 0:
                        dve.tensor_tensor(YX[:].rearrange("p (b d) -> p b d", b=GB), y, Zg, ALU.add).then_inc(S["yx"], 1)
                        have(dve, S["yx"], g + 1)
                        y = YX[:].rearrange("p (b d) -> p b d", b=GB)
                    dve.scalar_tensor_tensor(out=Xg, in0=y, scalar=tg[:, 2 + m:3 + m], in1=Xg, op0=ALU.mult, op1=ALU.add)\
                       .then_inc(S["x"] if m == 0 else x_final, 1)
                    if m == 0:
                        have(dve, S["x"], g * 2 + 1)
                        for j in range(GB):
                            ins = dve.bn_stats(stats[:, g * GB + j, :], X[:, g * GB + j, :])
                        ins.then_inc(S["x"], 1)

            router(0)
            mixture(0)
            have(dve, m_sem[0]["x"], 2 * G)
            layernorm_scales()

            CC = Chain(c_chain, 5)
            with dve.Fori(0, G) as g:
                CC.begin(g)
                have(dve, c_sem["hc"], g)
                for j in range(GB):
                    ins = normalise(XG[:, j, :], g * GB + j)
                ins.then_inc(c_sem["xn"], 1)
                have(dve, c_sem["xt"], g + 1)
                have(dve, c_sem["s"], g)
                dve.tensor_scalar(E3T[:], XGT[:], w3s[:], w2s[:], ALU.mult, ALU.add).then_inc(c_sem["e3"], 1)
                have(dve, c_sem["s"], g + 1)
                have(dve, c_sem["exp"], g * GB)
                CC(dve.tensor_reduce(nmx[:], PS[:, 1, 0:GB * TC].rearrange("p (b t) -> p b t", b=GB), AX.X, ALU.max, negate=True))
                dve.scalar_tensor_tensor(out=bt[:], in0=PS[:, 1, GB * TC:GB * TC + GB], scalar=bsim_c[:], in1=nmx[:],
                                         op0=ALU.add, op1=ALU.subtract).then_inc(c_sem["mx"], 1)
                have(dve, c_sem["exp"], g * GB + GB)
                CC(dve.reciprocal(rca[:], suma[:]))
                dve.tensor_tensor(AM, AM, rca[:].unsqueeze(2).broadcast_to([P, GB, TC]), ALU.mult).then_inc(c_sem["a"], 1)
                have(dve, c_sem["bt"], g * 2 + 1)
                dve.tensor_reduce(bm[:], PS[0:GB, 3, 0:P], AX.X, ALU.max, negate=True).then_inc(c_sem["bt"], 1)
                have(dve, c_sem["bexp"], g + 1)
                CC(dve.reciprocal(bs[:, 1:2], bs[:, 0:1]))
                dve.tensor_scalar(BB[0:GB, :], BB[0:GB, :], bs[:, 1:2], None, ALU.mult).then_inc(c_sem["bb"], 1)
                have(dve, c_sem["bbt"], g + 1)
                dve.tensor_copy(BCOL[:], PS[:, 3, P:P + GB]).then_inc(c_sem["bc"], 1)
                have(dve, c_sem["hc"], g + 1)
                dve.tensor_copy(HC[:], PS[:, 3, 2 * P:2 * P + GB]).then_inc(c_sem["hcr"], 1)
                have(dve, c_sem["hcr"], g + 1)
                have(dve, c_sem["o"], g)
                for j in range(GB):
                    ins = dve.scalar_tensor_tensor(out=WB[:, j, :], in0=wqv[:, 3, :], scalar=HC[:, j:j + 1], in1=wqv[:, 0, :],
                                                   op0=ALU.mult, op1=ALU.add)
                CC(ins)
                have(dve, c_sem["hq_sb"], g + 1)
                dve.tensor_tensor(XH[:], PS[:, 4, :], XGT[:], ALU.mult).then_inc(c_sem["xh"], 1)
                have(dve, c_sem["o"], g + 1)
                have(dve, c_sem["xb"], g + 1)
                Xg = X[:, bass.ds(g * GB, GB), :]
                CC(dve.scalar_tensor_tensor(out=Xg, in0=PS[:, 5, :].rearrange("p (b d) -> p b d", b=GB), scalar=tg[:, 1:2],
                                            in1=Xg, op0=ALU.mult, op1=ALU.add))
                for j in range(GB):
                    ins = dve.bn_stats(stats[:, g * GB + j, :], X[:, g * GB + j, :])
                ins.then_inc(c_sem["x"], 1)
                CC.end()
            have(dve, c_sem["x"], G)
            layernorm_scales()
            router(1)
            mixture(1)

        @block.tensor
        def _(pe):
            for s in at_one["pe"]:
                pe.sem_inc(s, 1)
            pe.wait_ge(consts, 1)
            pe.wait_ge(wa_in, 16 * 4)
            for i in range(4):
                ins = pe.transpose(PS[:, 0, i * D:(i + 1) * D], w_nat[:, i, :], identf[:])
            ins.then_inc(pre_ps, 1)
            pe.wait_ge(ctx_in, 16)
            for k in range(4):
                for j in range(4):
                    ins = pe.transpose(PS[:, 1 + k, j * TC:(j + 1) * TC], ctx_nat[:, 4 * k + j, :], identf[0:TC, 0:TC])
                ins.then_inc(pre_ps, 1)
            pe.wait_ge(pre_sb, 5)

            with pe.Fori(0, G) as g:
                have(pe, a_sem["xn"], g + 1)
                have(pe, a_sem["xt"], g)
                for j in range(GB):
                    ins = pe.transpose(PS[:, 0, j * P:(j + 1) * P], XG[:, j, :], identf[:])
                ins.then_inc(a_sem["t"], 1)
                have(pe, a_sem["xt"], g + 1)
                have(pe, a_sem["qkv_sb"], g)
                pe.matmul(PS[:, 1, :], w_t[:, 0, :], XGT[:], start=True, stop=True)
                keys = ctx_t[:, bass.ds(g * GB, GB), 0:NK]
                pe.matmul(PS[:, 2, 0:GB * NK], w_t[:, 1, :], keys, start=True, stop=True)
                pe.matmul(PS[:, 2, GB * NK:2 * GB * NK], w_t[:, 2, :], keys, start=True, stop=True).then_inc(a_sem["kv"], 1)
                have(pe, a_sem["qkv_sb"], g + 1)
                have(pe, a_sem["v2_sb"], g)
                for j in range(2):
                    ins = pe.matmul(PS[:, 3, j * D:(j + 1) * D], VA4[:, 2 * j:2 * j + 2, :].rearrange("p b k -> p (b k)"), w_t[:, 3, :],
                                    start=True, stop=True)
                ins.then_inc(a_sem["v2"], 1)
                have(pe, a_sem["p"], g)
                for j in range(GB):
                    ins = pe.matmul(PS[:, 4, j * NK:(j + 1) * NK], QA[:, j * P:(j + 1) * P], KA4[:, j, :], start=True, stop=True)
                ins.then_inc(a_sem["s"], 1)
                have(pe, a_sem["p"], g + 1)
                have(pe, a_sem["pt_sb"], g)
                for j in range(2):
                    ins = pe.transpose(PS[:, 5, j * P:(j + 1) * P], PA[:, 2 * j:2 * j + 2, :, :].rearrange("p b l h -> p (b l h)"),
                                       identf[:])
                ins.then_inc(a_sem["pt"], 1)
                have(pe, a_sem["pt_sb"], g + 1)
                have(pe, a_sem["v2_sb"], g + 1)
                have(pe, a_sem["x"], g)
                for j in range(GB):
                    k, r = j // 2, slice(NK * (j % 2), NK * (j % 2 + 1))
                    ins = pe.matmul(PS[:, 6 + j % 2, k * D:(k + 1) * D], PAT[r, k * P:(k + 1) * P], V2[r, k, :], start=True, stop=True)
                ins.then_inc(a_sem["y"], 1)

            have(pe, a_sem["x"], G)
            pe.wait_ge(wb_in, 16 * 4)

            def slot(s, u0):
                def batch(k):
                    return s + k, (u0 + k) % 2

                def ok(k):
                    return not isinstance(s, int) or 0 <= s + k < B

                def scores(j):
                    b, u = batch(1)
                    if j == 0:
                        have(pe, b_sem["k_sb"], b + 1)
                        have(pe, b_sem["q_sb"], b + 1)
                    if not (isinstance(b, int) and 4 * b + j < 2):
                        have(pe, b_sem["max"], b * 4 + (j - 1))
                    for h in range(4 * j, 4 * j + 4):
                        ins = pe.matmul(PS[:, j % 2, (h % 4) * P:(h % 4 + 1) * P], QT[:, h // 2, :], KT[u][h % 2][:, h // 2, :],
                                        start=True, stop=True)
                    ins.then_inc(b_sem["s"], 1)

                def scores_t(k, j):
                    b, u = batch(k)
                    if j == 0:
                        have(pe, b_sem["qm_sb"], b + 1)
                    if not (isinstance(b, int) and 4 * b + j < 2):
                        have(pe, b_sem["exp"], b * 4 + (j - 1))
                    for h in range(4 * j, 4 * j + 4):
                        ins = pe.matmul(PS[:, 2 + j % 2, (h % 4) * P:(h % 4 + 1) * P], KT[u][h % 2][:, h // 2, :], QM[u][:, h // 2, :],
                                        start=True, stop=True)
                    ins.then_inc(b_sem["st"], 1)

                def values(j):
                    b, u = batch(0)
                    have(pe, b_sem["exp"], b * 4 + (j + 1))
                    if j == 0 and not (isinstance(b, int) and b == 0):
                        have(pe, b_sem["z"], b)
                    for h in range(4 * j, 4 * j + 4):
                        ins = pe.matmul(PS[:, 7, VW * h:VW * h + PV_N], EX[j % 2][:, (h % 4) * P:(h % 4 + 1) * P],
                                        VA[:, b, VW * h:VW * h + PV_N], start=True, stop=True)
                    ins.then_inc(b_sem["pv"], 1)

                if ok(1):
                    scores(0)
                    scores(1)
                if ok(2):
                    b, u = batch(2)
                    have(pe, b_sem["xn"], b + 1)
                    if not (isinstance(b, int) and b == 0):
                        have(pe, b_sem["xt"], b)
                        have(pe, b_sem["v"], b)
                    pe.transpose(PS[:, 4, 3 * D:4 * D], XNB[u][:], identf[:]).then_inc(b_sem["t"], 1)
                if ok(0):
                    scores_t(0, 1)
                    values(0)
                if ok(1):
                    scores(2)
                if ok(0):
                    scores_t(0, 2)
                    values(1)
                if ok(2):
                    b, u = batch(2)
                    have(pe, b_sem["xt"], b + 1)
                    if not (isinstance(b, int) and b == 0):
                        have(pe, b_sem["v"], b)
                    pe.matmul(PS[:, 4, 0:3 * D], XNT[u][:], wqkv[:], start=True, stop=True).then_inc(b_sem["qkv"], 1)
                if ok(1):
                    scores(3)
                if ok(0):
                    scores_t(0, 3)
                    values(2)
                    values(3)
                if ok(1):
                    b, u = batch(1)
                    have(pe, b_sem["m"], b * 2 + 2)
                    have(pe, b_sem["q_sb"], b + 1)
                    for c in range(H // 2):
                        ins = pe.transpose(PS[:, 5, :].bitcast(BF16)[:, c * P:(c + 1) * P],
                                           QS[u][:, 2 * c:2 * c + 2, :].rearrange("p h d -> p (h d)"), identb[:])
                    ins.then_inc(b_sem["qm_t"], 1)
                if ok(0):
                    b, u = batch(0)
                    have(pe, b_sem["norm"], b * 2 + 2)
                    pe.transpose(PS[:, 7, 232:360], CN[:].rearrange("p h d -> p (h d)"), identf[:]).then_inc(b_sem["ct"], 1)
                if ok(2):
                    b, u = batch(2)
                    have(pe, b_sem["split"], b + 1)
                    if not (isinstance(b, int) and b == 0):
                        have(pe, b_sem["k_sb"], b)
                    for c in range(H // 2):
                        ins = pe.transpose(PS[:, 6, :].bitcast(BF16)[:, c * P:(c + 1) * P],
                                           KS[u][:, 2 * c:2 * c + 2, :].rearrange("p h d -> p (h d)"), identb[:])
                    ins.then_inc(b_sem["k_t"], 1)
                if ok(0):
                    b, u = batch(0)
                    have(pe, b_sem["ct_sb"], b + 1)
                    pe.matmul(PS[:, 7, 360:488], CT[:], wo[:], start=True, stop=True).then_inc(b_sem["wo"], 1)
                if ok(2):
                    b, u = batch(2)
                    if not (isinstance(b, int) and b == 0):
                        have(pe, b_sem["qm_sb"], b)
                    for c in range(H // 2):
                        ins = pe.transpose(PS[:, 5, :].bitcast(BF16)[:, c * P:(c + 1) * P],
                                           QS[u][:, 2 * c:2 * c + 2, :].rearrange("p h d -> p (h d)"), identb[:])
                    ins.then_inc(b_sem["q_t"], 1)
                if ok(1):
                    scores_t(1, 0)

            for s in range(-3, 0):
                slot(s, s % 2)
            with pe.Fori(0, (B - 4) // 2) as i:
                for u in range(2):
                    slot(i * 2 + u, u)
            for s in range(B - 4, B):
                slot(s, s % 2)

            def router(m):
                R, EW, w = r_sem[m], (E0, E1 + 1)[m], (wr0, wr1)[m]
                with pe.Fori(0, G) as g:
                    have(pe, R["h"], g + 1)
                    have(pe, R["ht"], g * 2)
                    for j in range(GB):
                        ins = pe.transpose(PS[:, 0, j * P:(j + 1) * P], HG[:, j, :], identf[:])
                    ins.then_inc(R["t"], 1)
                    have(pe, R["ht"], g * 2 + 1)
                    for j in range(GB):
                        ins = pe.matmul(PS[:, 1, bass.ds((g * GB + j) * EW, EW)], HT[:, j * P:(j + 1) * P], w[:],
                                        start=True, stop=True)
                    ins.then_inc(R["lg"], 1)
                have(pe, R["cs"], 1)
                for b in range(B):
                    ins = pe.transpose(PS[:, 2 + b // 8, :].bitcast(BF16)[:, (b % 8) * P:(b % 8 + 1) * P], CS[:, b, :], identb[:])
                    if b % 8 == 7:
                        ins.then_inc(R["ct"], 1)
                have(pe, R["ct_sb"], 2)

            def mixture(m):
                M, S = MOE[m], m_sem[m]
                nch = M["n"] + M["s"]
                ne = M["n"] // M["per"] + (m == 1)
                with pe.Fori(0, G) as g:
                    h2 = H2T[:, bass.ds(g * GT, GT)]

                    def down(c):
                        have(pe, S["hid"], g * nch + c + 1)
                        if c == 0:
                            have(pe, S["yt"], g)
                        pe.matmul(PS[:, 6, :], WD[m][:, c, :], HH[c % 2][:], start=(c == 0), stop=(c == nch - 1))\
                          .then_inc(S["y"] if c == nch - 1 else S["yc"], 1)

                    for c in range(nch):
                        first = c % M["per"] == 0 if c < M["n"] else (m == 1 and c == M["n"])
                        if first:
                            e = c // M["per"]
                            have(pe, S["bc_sb"], g * ne + max(e - 1, 0))
                            pe.matmul(PS[:, 4 + e % 2, :], SEL[m][:, e, :], CWT[:, bass.ds(g * GT, GT)], start=True, stop=True)\
                              .then_inc(S["bc"], 1)
                        have(pe, S["silu"], g * nch + max(c - 1, 0))
                        pe.matmul(PS[:, c % 2, :], WG[m][:, c, :], h2, start=True, stop=True).then_inc(S["g"], 1)
                        have(pe, S["hid"], g * nch + max(c - 1, 0))
                        pe.matmul(PS[:, 2 + c % 2, :], WU[m][:, c, :], h2, start=True, stop=True).then_inc(S["u"], 1)
                        if c:
                            down(c - 1)
                    down(nch - 1)
                    have(pe, S["yt"], g + 1)
                    have(pe, S["x"] if m == 0 else x_final, g * 2 if m == 0 else g)
                    for j in range(GB):
                        ins = pe.transpose(PS[:, 7, j * P:(j + 1) * P], YT[:, j * P:(j + 1) * P], identf[:])
                    ins.then_inc(S["yn"], 1)

            have(pe, b_sem["z"], B)
            pe.wait_ge(m0_in, 16 * 7)
            router(0)
            mixture(0)
            have(pe, m_sem[0]["x"], 2 * G)

            pe.wait_ge(turn_in, 16 * 6)
            pe.wait_ge(m1_in, 16 * 3)
            for k in range(3):
                for t, (c0, c1) in enumerate(TURNS):
                    if 3 * k + t >= 8:
                        pe.wait_ge(turned, 3 * k + t - 7)
                    for c in range(c0, c1):
                        ins = pe.transpose(PS[:, (3 * k + t) % 8, (c - c0) * P:(c - c0 + 1) * P], w_turn[k][:, c, :], identf[:])
                    ins.then_inc(turn_ps, 1)
            pe.wait_ge(turned, 2)
            pe.transpose(PS[:, 1, 0:E1 + 1], wr1_nat[:], identf[0:E1 + 1, 0:E1 + 1]).then_inc(turn_ps, 1)
            pe.wait_ge(turned, 10)

            with pe.Fori(0, G) as g:
                have(pe, c_sem["xn"], g + 1)
                have(pe, c_sem["e3"], g)
                have(pe, c_sem["xt"], g)
                for j in range(GB):
                    ins = pe.transpose(PS[:, 0, j * P:(j + 1) * P], XG[:, j, :], identf[:])
                ins.then_inc(c_sem["t"], 1)
                have(pe, c_sem["e3"], g + 1)
                have(pe, c_sem["xt"], g + 1)
                have(pe, c_sem["exp"], g * GB)
                for j in range(GB):
                    pe.matmul(PS[:, 1, j * TC:(j + 1) * TC], E3T[:, j * P:(j + 1) * P], ctx_t[:, g * GB + j, :], start=True, stop=True)
                    ins = pe.matmul(PS[:, 1, GB * TC + j:GB * TC + j + 1], XGT[:, j * P:(j + 1) * P], w1_c[:], start=True, stop=True)
                ins.then_inc(c_sem["s"], 1)
                have(pe, c_sem["mx"], g + 1)
                have(pe, c_sem["hcr"], g)
                pe.transpose(PS[0:GB, 3, 0:P], bt[:], identf[:]).then_inc(c_sem["bt"], 1)
                have(pe, c_sem["a"], g + 1)
                have(pe, c_sem["at_sb"], g)
                for j in range(GB):
                    ins = pe.transpose(PS[0:TC, 2, j * P:(j + 1) * P], AM[:, j, :], identf[:])
                ins.then_inc(c_sem["at"], 1)
                have(pe, c_sem["bb"], g + 1)
                pe.transpose(PS[:, 3, P:2 * P], BB[:], identf[:]).then_inc(c_sem["bbt"], 1)
                have(pe, c_sem["at_sb"], g + 1)
                have(pe, c_sem["cg"], g + 1)
                have(pe, c_sem["xh"], g)
                for j in range(GB):
                    ins = pe.matmul(PS[:, 4, j * P:(j + 1) * P], CG[:, j, :], AMT[:, j * P:(j + 1) * P], start=True, stop=True)
                ins.then_inc(c_sem["hq"], 1)
                have(pe, c_sem["bc"], g + 1)
                for j in range(GB):
                    ins = pe.matmul(PS[:, 3, 2 * P + j:2 * P + j + 1], XG[:, j, :], BCOL[:, j:j + 1], start=True, stop=True)
                ins.then_inc(c_sem["hc"], 1)
                have(pe, c_sem["xh"], g + 1)
                have(pe, c_sem["x"], g)
                for j in range(GB):
                    o = PS[:, 5, j * D:(j + 1) * D]
                    pe.matmul(o, XGT[:, j * P:(j + 1) * P], WB[:, j, :], start=True, stop=False)
                    pe.matmul(o, HQ[:, j * P:(j + 1) * P], wqv[:, 1, :], start=False, stop=False)
                    ins = pe.matmul(o, XH[:, j * P:(j + 1) * P], wqv[:, 2, :], start=False, stop=True)
                ins.then_inc(c_sem["o"], 1)

            have(pe, c_sem["x"], G)
            router(1)
            mixture(1)


_INS = ['x', 'ctx_1024', 'g_xattn', 'g_ffn', 'L0_xattn_Wq', 'L0_xattn_bq', 'L0_xattn_Wk', 'L0_xattn_bk', 'L0_xattn_Wv',
        'L0_xattn_bv', 'L0_xattn_Wo', 'L0_xattn_bo', 'L0_ffn_norm1_w', 'L0_ffn_norm2_w', 'L0_ffn_wq', 'L0_ffn_wk',
        'L0_ffn_wv', 'L0_ffn_wo', 'L0_ffn_router_w', 'L0_ffn_sh_gate', 'L0_ffn_sh_up', 'L0_ffn_sh_down', 'L0_ffn_e_gate',
        'L0_ffn_e_up', 'L0_ffn_e_down', 'L1_xattn_w_sim', 'L1_xattn_b_sim', 'L1_xattn_W_qv', 'L1_xattn_b_qv', 'L1_ffn_Wg',
        'L1_ffn_We_gate', 'L1_ffn_We_up', 'L1_ffn_We_down', 'L1_ffn_Ws_gate', 'L1_ffn_Ws_up', 'L1_ffn_Ws_down', 'L1_ffn_Wsg']


def kernel(**inputs):
    import numpy as _np
    import concourse.bacc as _bacc
    from concourse import mybir as _mybir
    from concourse.bass_utils import run_bass_kernel_spmd as _run

    nc = _bacc.Bacc("TRN2", target_bir_lowering=False, num_devices=1)
    arrays, args = {}, {}
    for name in _INS:
        v = _np.ascontiguousarray(inputs[name])
        arrays[f"in_{name}_dram"] = v
        args[name] = nc.dram_tensor(f"in_{name}_dram", v.shape, _mybir.dt.from_np(v.dtype), kind="ExternalInput").ap()
    out = nc.dram_tensor("out_0_dram", (B, P, D), _mybir.dt.float32, kind="ExternalOutput").ap()
    build(nc, args, out)
    r = _run(nc, [arrays], core_ids=[0])
    return r.results[0]["out_0_dram"]
```

```python
from contextlib import ExitStack

import concourse.bass as bass
from concourse import mybir

F32 = mybir.dt.float32
BF16 = mybir.dt.bfloat16
F32R = mybir.dt.float32r
I32 = mybir.dt.int32
U32 = mybir.dt.uint32
ALU = mybir.AluOpType
ACT = mybir.ActivationFunctionType
AX = mybir.AxisListType

P = 128
B = 16
D = 128
H = 16
DH = D // H
TC = 77
L = TC // H
NK = L * H
G = 4
GB = B // G
GT = GB * P
SCALE = float(DH) ** -0.5
LN_EPS = 1e-5
RMS_EPS = 1e-6
RSQRT_SEED = float(0x5F3759DF)
SLOT = 64
VW = 9
PV_N = 96
VA_W = VW * (H - 1) + PV_N
E0, F0 = 8, 256
E1, F1 = 16, 64
KINDS = ("gate", "up", "down")
PIECE = 32
LAG = 3


def build(nc, a, out):
    NC0 = E0 * F0 // P
    NC1 = E1 * F1 // P
    TURNS = [(0, 4), (4, 8), (8, 10)]
    TURN_AT = [2, 3, 4, 5, 6, 7, 12, 13, 14, 15]
    TB, RB, LB = (5, 7), (0, 5), (1, 5)
    MOE = [dict(n=NC0, s=2, per=F0 // P), dict(n=NC1, s=2, per=1)]
    NCH, NSC, NBC = (NC0 + 2, NC1 + 2), (NC0, NC1 + 2), (E0, NC1 + 1)
    OFF = [(0, 0, 0), (G * NCH[0], G * NSC[0], G * NBC[0])]

    with ExitStack() as ctx:
        def sb(name, shape, dt=F32):
            return ctx.enter_context(nc.sbuf_tensor(name, shape, dt))

        def sem(name):
            return ctx.enter_context(nc.semaphore(name))

        PS = ctx.enter_context(nc.psum_tensor("PS", [P, 8, 512], F32))

        X = sb("X", [P, B, D])
        Z = sb("Z", [P, B, D])
        ctx_nat = sb("ctx_nat", [TC, B, D])
        ctx_t = sb("ctx_t", [P, B, TC])
        stats = sb("stats", [P, B, 6])
        mean, var, rstd, nmr, r2 = (sb(n, [P, B]) for n in ("mean", "var", "rstd", "nmr", "r2"))
        t_a, t_b, t_c = (sb(n, [P, B]) for n in ("t_a", "t_b", "t_c"))
        identf = sb("identf", [P, P])
        identb = sb("identb", [P, P], BF16)
        hmask = sb("hmask", [P, H])
        gates = sb("gates", [P, 4])
        tg = sb("tg", [P, 4])
        bq_c, bk_c, bv_c, n1w, n2w, w1_c, w2s, w3s = (
            sb(n, [P, 1]) for n in ("bq_c", "bk_c", "bv_c", "n1w", "n2w", "w1_c", "w2s", "w3s"))
        bo_r = sb("bo_r", [P, D])
        bqv_r = sb("bqv_r", [P, D])
        tgb = sb("tgb", [P, D])
        bsim_c = sb("bsim_c", [P, 1])
        wqv = sb("wqv", [P, 4, D])
        wr0 = sb("wr0", [P, E0])
        wr1_nat = sb("wr1_nat", [E1 + 1, D])
        wr1 = sb("wr1", [P, E1 + 1])
        raw = [sb(f"raw{k}", [P, NC0 + 2, P]) for k in range(2)]
        W0H = [sb(f"W0H_{k}", [P, NC0 + 2, P], F32R) for k in KINDS]
        W0L = [sb(f"W0L_{k}", [P, NC0 + 2, P], F32R) for k in KINDS]
        XG = sb("XG", [P, GB, D])
        XGT = sb("XGT", [P, GT])
        HG1 = sb("HG1", [P, GB, D])
        work = [sb(f"work{k}", [P, GT]) for k in range(6)]
        gstats = sb("gstats", [P, 2 * GB, 6])
        grstd, gnmr = sb("grstd", [P, 2 * GB]), sb("gnmr", [P, 2 * GB])
        LG = sb("LG", [P, B, E1 + 1])
        PR = sb("PR", [P, B, E1])
        top = sb("top", [P, B, 8])
        topi = sb("topi", [P, B, 8], U32)
        topf = sb("topf", [P, B, 2])
        iota_i = sb("iota_i", [P, E1], I32)
        iota_e = sb("iota_e", [P, E1])
        wsel = sb("wsel", [P, B, 2])
        comb = sb("comb", [P, B, E1 + 1])
        combt = sb("combt", [P, B, E1 + 1])
        CS = sb("CS", [P, B, P], BF16)
        sel0 = sb("sel0", [P, E0, P], BF16)
        sel1 = sb("sel1", [P, NC1 + 1, P], BF16)
        SEL = [sel0, sel1]
        nmx, suma, rca, bt = (sb(n, [P, GB]) for n in ("nmx", "suma", "rca", "bt"))
        BB = sb("BB", [P, P])
        bm, bs = sb("bm", [GB, 1]), sb("bs", [GB, 2])
        BCOL = sb("BCOL", [P, GB])
        HC = sb("HC", [P, GB])
        pad = sb("pad", [P, 1])

        with ExitStack() as early:
            def sbe(name, shape, dt=F32):
                return early.enter_context(nc.sbuf_tensor(name, shape, dt))

            w_nat = sbe("w_nat", [P, 4, D])
            w_t = sbe("w_t", [P, 4, D])
            QA = work[0]
            KA4 = sbe("KA4", [P, GB, NK])
            VA4 = sbe("VA4", [P, GB, NK])
            V2 = work[1][:, 0:2 * D].rearrange("p (b d) -> p b d", b=2)
            mxA = sbe("mxA", [P, GB, H])
            PA = sbe("PA", [P, GB, L, H])
            PAT = work[2][:, 0:2 * P]
            wqkv = sbe("wqkv", [P, 3 * D])
            wo = sbe("wo", [P, D])
            XNB = [sbe(f"XNB{u}", [P, D]) for u in range(2)]
            XNT = [sbe(f"XNT{u}", [P, D]) for u in range(2)]
            T32 = sbe("T32", [P, 2, D])
            QS = [sbe(f"QS{u}", [P, H, SLOT], BF16) for u in range(2)]
            KS = [sbe(f"KS{u}", [P, H, SLOT], BF16) for u in range(2)]
            KT = [[sbe(f"KT{u}{v}", [P, H // 2, P], BF16) for v in range(2)] for u in range(2)]
            QT = sbe("QT", [P, H // 2, P], BF16)
            QM = [sbe(f"QM{u}", [P, H // 2, P], BF16) for u in range(2)]
            nmax = sbe("nmax", [P, H])
            EX = work[3:5]
            VA = sbe("VA", [P, B, VA_W])[:]
            rden = sbe("rden", [P, H])
            CN = sbe("CN", [P, H, DH])
            CT = sbe("CT", [P, D])

        H2H = sb("H2H", [P, B * P], F32R)
        H2L = sb("H2L", [P, B * P], F32R)
        CWT = sb("CWT", [P, B * P], BF16)
        W1H = [sb(f"W1H_{k}", [P, NC1 + 2, P], F32R) for k in KINDS]
        W1L = [sb(f"W1L_{k}", [P, NC1 + 2, P], F32R) for k in KINDS]
        WH, WL = [W0H, W1H], [W0L, W1L]
        BC, SG, HH = work[0:2], work[2:4], work[4:6]
        HHI = [sb(f"HHI{u}", [P, GT], F32R) for u in range(LAG)]
        HLO = [sb(f"HLO{u}", [P, GT], F32R) for u in range(LAG)]
        YT = sb("YT", [P, GT])
        spare = [raw[k][:, c:c + GB, :].rearrange("p c d -> p (c d)") for k, c in ((0, NC1 + 2), (0, NC1 + 6), (1, NC1 + 2), (1, NC1 + 6))]
        HG, HT = [XG, HG1], [XGT, spare[3]]
        HQ, AMT, CG = spare[0], spare[1][0:TC], spare[2][0:TC].rearrange("p (b d) -> p b d", b=GB)
        E3T = sb("E3T", [P, GT])
        XH = E3T
        AMW = sb("AMW", [P, GT])
        AM = AMW[:, 0:GB * TC].rearrange("p (b t) -> p b t", b=GB)
        WB = AMW[:].rearrange("p (b d) -> p b d", b=GB)

        at_one = {"pe": [], "act": [], "dve": [], "pool": []}

        def stage(name, **by):
            made = {}
            for eng, names in by.items():
                for n in names.split():
                    made[n] = sem(f"{name}_{n}")
                    at_one[eng].append(made[n])
            return made

        x_in, ctx_in, small_in, wa_in, wb_in, wr_in, wqv_in = (
            sem(n) for n in ("x_in", "ctx_in", "small_in", "wa_in", "wb_in", "wr_in", "wqv_in"))
        raw_in = [sem(f"raw_in{k}") for k in range(6)]
        halved = sem("halved")
        turn_ps, turn_hi, turn_lo = sem("turn_ps"), sem("turn_hi"), sem("turn_lo")
        consts, pool_c, dve_c = sem("consts"), sem("pool_c"), sem("dve_c")
        tg_ready, pre_ps, pre_sb = sem("tg_ready"), sem("pre_ps"), sem("pre_sb")
        out_done = sem("out_done")
        a_sem = stage("a", pe="t kv v2 s pt y", act="xt e pt_sb", dve="xn qkv_sb v2_sb d p x")
        a_chain = sem("a_chain")
        b_sem = stage("b", pe="t qkv k_t q_t s qm_t st pv ct wo", act="xt h q_sb qm_sb exp ct_sb",
                      dve="xn t32 v split k_sb max m norm z zs", pool="z0")
        b_chain = sem("b_chain")
        r_sem = [stage(f"r{m}", pe="t lg ct", act="ht ct_sb", dve="h e1 e2 cs", pool="low") for m in range(2)]
        r_chain = [sem(f"r{m}_chain") for m in range(2)]
        m_sem = stage("m", pe="bc g u down yn", act="bc_sb silu hi yt", dve="hid lo yx x st", pool="scaled")
        c_sem = stage("c", pe="t s bt at bbt hq hc o", act="xt exp bexp at_sb hq_sb",
                      dve="xn e3 mx a bb bc hcr xh wb xu x", pool="cg xb")
        c_chain = sem("c_chain")
        ln_chain, m_ln = sem("ln_chain"), sem("m_ln")

        block = ctx.enter_context(nc.Block())

        def have(eng, s, n):
            eng.wait_ge(s, n + 1)

        def turn_of(m, g, c):
            assert NCH[0] % LAG == 0
            return (c if m == 0 else g * NCH[1] + c) % LAG

        def first_of_expert(m, c):
            return c % MOE[m]["per"] == 0 if c < MOE[m]["n"] else (m == 1 and c == MOE[m]["n"])

        def mixtures(eng, chunks, first_steps, matching):
            n0, n1 = NCH

            def pick(*parts):
                return {c: [f for steps, lo, hi in parts if lo + c < hi for f in steps.get(lo + c, ())] for c in range(n0)}

            chunks(0, 0, first_steps)
            chunks(0, 1, pick((matching(0), 0, n0)))
            with eng.Fori(0, G - 2) as i:
                chunks(0, i + 2, pick((matching(i), n0, 2 * n0), (matching(i + 1), 0, n0)))
            before, last = matching(G - 2), matching(G - 1)
            chunks(1, 0, pick((before, n0, n0 + n1), (last, 0, n1)))
            chunks(1, 1, pick((before, n0 + n1, 2 * n0), (last, n1, 2 * n1)))
            chunks(1, 2, pick((last, 2 * n1, 3 * n1)))
            chunks(1, 3, {})

        def is_last(g):
            return isinstance(g, int) and g == G - 1

        def by_chunk(*steps):
            made = {}
            for c, f in steps:
                made.setdefault(c, []).append(f)
            return made

        def row(ap, n):
            return ap.rearrange("(a n) -> a n", a=1).broadcast_to([n, ap.shape[0]])

        def col(ap):
            return ap.rearrange("(n a) -> n a", a=1)

        @block.sync
        def _(sp):
            sp.dma_start(X[:], a["x"].rearrange("b s d -> s b d")).then_inc(x_in, 16)
            sp.dma_start(ctx_nat[:], a["ctx_1024"].rearrange("b s d -> s b d")).then_inc(ctx_in, 16)
            for i, n in enumerate(("Wq", "Wk", "Wv", "Wo")):
                sp.dma_start(w_nat[:, i, :], a["L0_xattn_" + n]).then_inc(wa_in, 16)
            for i, n in enumerate(("wq", "wk", "wv")):
                sp.dma_start(wqkv[:, i * D:(i + 1) * D], a["L0_ffn_" + n]).then_inc(wb_in, 16)
            sp.dma_start(wo[:], a["L0_ffn_wo"]).then_inc(wb_in, 16)
            sp.dma_start(wr0[:], a["L0_ffn_router_w"]).then_inc(wr_in, 16)
            for k, n in enumerate(KINDS):
                r = raw[k % 2]
                if k == 2:
                    sp.wait_ge(halved, 1)
                if n == "down":
                    sp.dma_start(r[:, 0:NC0, :], a["L0_ffn_e_down"].rearrange("e (c f) d -> f (e c) d", c=F0 // P)).then_inc(raw_in[k], 16)
                    sp.dma_start(r[:, NC0:NC0 + 2, :], a["L0_ffn_sh_down"].rearrange("(c f) d -> f c d", f=P)).then_inc(raw_in[k], 16)
                else:
                    sp.dma_start(r[:, 0:NC0, :].rearrange("d (e f) c -> d e (f c)", e=E0),
                                 a["L0_ffn_e_" + n].rearrange("e d f -> d e f")).then_inc(raw_in[k], 16)
                    sp.dma_start(r[:, NC0:NC0 + 2, :].rearrange("d a c -> d (a c)"), a["L0_ffn_sh_" + n]).then_inc(raw_in[k], 16)
            sp.dma_start(wr1_nat[0:E1, :], a["L1_ffn_Wg"]).then_inc(wr_in, 16)
            sp.dma_start(wr1_nat[E1:E1 + 1, :], a["L1_ffn_Wsg"]).then_inc(wr_in, 16)
            sp.dma_start(wqv[:], a["L1_xattn_W_qv"].rearrange("(k d) n -> d k n", d=D)).then_inc(wqv_in, 16)
            for k, n in enumerate(KINDS):
                r = raw[(k + 1) % 2]
                if k < 2:
                    sp.wait_ge(halved, k + 2)
                else:
                    sp.wait_ge(turn_ps, 3)
                if n == "down":
                    sp.dma_start(r[:, 0:NC1, :].rearrange("d c (a f) -> d (c a) f", a=2),
                                 a["L1_ffn_We_down"].rearrange("e d f -> d e f")).then_inc(raw_in[3 + k], 16)
                    sp.dma_start(r[:, NC1:NC1 + 2, :].rearrange("d a f -> d (a f)"), a["L1_ffn_Ws_down"]).then_inc(raw_in[3 + k], 16)
                else:
                    sp.dma_start(r[:, 0:NC1, :], a[f"L1_ffn_We_{n}"].rearrange("(c a) f d -> (a f) c d", a=2)).then_inc(raw_in[3 + k], 16)
                    sp.dma_start(r[:, NC1:NC1 + 2, :], a[f"L1_ffn_Ws_{n}"].rearrange("(c f) d -> f c d", f=P)).then_inc(raw_in[3 + k], 16)
            for g in range(G):
                have(sp, m_sem["x"], G + g + 1)
                sp.dma_start(out[g * GB:(g + 1) * GB].rearrange("b s d -> s b d"), X[:, g * GB:(g + 1) * GB, :]).then_inc(out_done, 16)
            sp.wait_ge(out_done, 16 * G)

        @block.gpsimd
        def _(pool):
            for s in at_one["pool"]:
                pool.sem_inc(s, 1)
            n = [0]

            def step(ins):
                n[0] += 1
                ins.then_inc(pool_c, 1)
                pool.wait_ge(pool_c, n[0])

            step(pool.memset(identf[:], 0.0))
            step(pool.affine_select(out=identf[:], in_=identf[:], compare_op=ALU.not_equal, fill=1.0, base=0,
                                    pattern=[[-1, P]], channel_multiplier=1))
            step(pool.tensor_copy(identb[:], identf[:]))
            step(pool.memset(hmask[:], 1.0))
            step(pool.affine_select(out=hmask[:], in_=hmask[:], compare_op=ALU.is_ge, fill=0.0, base=0,
                                    pattern=[[-DH, H]], channel_multiplier=1))
            step(pool.affine_select(out=hmask[:], in_=hmask[:], compare_op=ALU.is_ge, fill=0.0, base=DH - 1,
                                    pattern=[[DH, H]], channel_multiplier=-1))
            pool.memset(VA, 1.0)
            pool.memset(BB[:], 0.0)
            for u in range(2):
                pool.memset(QS[u][:].bitcast(F32), 0.0)
                step(pool.memset(KS[u][:].bitcast(F32), 0.0))
                pool.memset(KS[u][:, :, 48:50], 1.0)
                pool.memset(KT[u][0][:].bitcast(F32), 0.0)
                pool.memset(KT[u][1][:].bitcast(F32), 0.0)
            step(pool.memset(CS[:].bitcast(F32), 0.0))
            pool.memset(bm[:], 0.0).then_inc(consts, 1)
            pool.iota(iota_i[:], pattern=[[1, E1]], base=0, channel_multiplier=0).then_inc(pool_c, 1)
            n[0] += 1
            pool.memset(sel0[:].bitcast(F32), 0.0)
            step(pool.memset(sel1[:].bitcast(F32), 0.0))
            step(pool.tensor_copy(iota_e[:], iota_i[:]))
            for p in range(3):
                step(pool.affine_select(out=sel0[:], in_=sel0[:], compare_op=ALU.not_equal, fill=1.0,
                                        base=-PIECE * p, pattern=[[-1, E0], [0, P]], channel_multiplier=1))
                step(pool.affine_select(out=sel1[:, 0:NC1, :].rearrange("p c (a f) -> p c a f", a=2),
                                        in_=sel1[:, 0:NC1, :].rearrange("p c (a f) -> p c a f", a=2),
                                        compare_op=ALU.not_equal, fill=1.0, base=-PIECE * p,
                                        pattern=[[-2, NC1], [-1, 2], [0, F1]], channel_multiplier=1))
                step(pool.affine_select(out=sel1[:, NC1, :], in_=sel1[:, NC1, :],
                                        compare_op=ALU.not_equal, fill=1.0, base=-PIECE * p - E1,
                                        pattern=[[0, P]], channel_multiplier=1))
            pool.memset(bm[:], 0.0).then_inc(consts, 1)
            for k in range(3):
                pool.wait_ge(raw_in[k], 32)
                step(pool.tensor_copy(W0H[k][:], raw[k % 2][:]))
                pool.tensor_tensor(W0L[k][:], raw[k % 2][:], W0H[k][:].bitcast(F32), ALU.subtract).then_inc(halved, 1)
            with pool.Fori(0, B // 2) as i:
                for u in range(2):
                    b = i * 2 + u
                    have(pool, b_sem["xn"], b + 1)
                    pool.tensor_copy(Z[:, b, :], XNB[u][:]).then_inc(b_sem["z0"], 1)

            def low_tokens(m, g):
                have(pool, r_sem[m]["ht"], g * 2 + 2)
                at = bass.ds(g * GT, GT)
                pool.tensor_tensor(H2L[:, at], HT[m][:], H2H[:, at].bitcast(F32), ALU.subtract).then_inc(r_sem[m]["low"], 1)

            with pool.Fori(0, G) as g:
                low_tokens(0, g)

            def chunks(m, g, inserts):
                n, per = NCH[m], MOE[m]["per"]
                base = g * n + OFF[m][0]
                for c in range(n):
                    if c < NSC[m]:
                        e = min(c // per, (n - 2) // per)
                        have(pool, m_sem["silu"], base + c + 1)
                        have(pool, m_sem["bc_sb"], g * NBC[m] + OFF[m][2] + e + 1)
                        pool.tensor_tensor(SG[c % 2][:], SG[c % 2][:], BC[e % 2][:], ALU.mult).then_inc(m_sem["scaled"], 1)
                    for f in inserts.get(c, ()):
                        f()

            def matching(g):
                def context(j):
                    have(pool, c_sem["hq"], g)
                    pool.tensor_copy(CG[:, j:j + 2, :], ctx_nat[:, bass.ds(g * GB + j, 2), :]).then_inc(c_sem["cg"], 1)

                def bias(j):
                    have(pool, c_sem["xn"], g + 1)
                    Xg = X[:, bass.ds(g * GB + j, 2), :]
                    pool.tensor_tensor(Xg, Xg, tgb[:].unsqueeze(1).broadcast_to([P, 2, D]), ALU.add).then_inc(c_sem["xb"], 1)

                return by_chunk((2, lambda: context(0)), (4, lambda: context(2)), (8, lambda: bias(0)), (10, lambda: bias(2)),
                                (23 if is_last(g) else 27, lambda: low_tokens(1, g)))

            mixtures(pool, chunks, {}, matching)

        @block.scalar
        def _(act):
            smalls = [(gates[:, 0:2], row(a["g_xattn"], P)), (gates[:, 2:4], row(a["g_ffn"], P)),
                      (bq_c[:], col(a["L0_xattn_bq"])), (bk_c[:], col(a["L0_xattn_bk"])), (bv_c[:], col(a["L0_xattn_bv"])),
                      (bo_r[:], row(a["L0_xattn_bo"], P)), (n1w[:], col(a["L0_ffn_norm1_w"])), (n2w[:], col(a["L0_ffn_norm2_w"])),
                      (w1_c[:], col(a["L1_xattn_w_sim"][0:D])), (w2s[:], col(a["L1_xattn_w_sim"][D:2 * D])),
                      (w3s[:], col(a["L1_xattn_w_sim"][2 * D:3 * D])), (bsim_c[:], row(a["L1_xattn_b_sim"], P)),
                      (bqv_r[:], row(a["L1_xattn_b_qv"], P))]
            for dst, src in smalls:
                act.dma_start(dst, src).then_inc(small_in, 16)
            for s in at_one["act"]:
                act.sem_inc(s, 1)
            act.wait_ge(small_in, 16 * len(smalls))
            act.activation(tg[:], gates[:], ACT.Tanh).then_inc(tg_ready, 1)
            act.wait_ge(pre_ps, 1)
            act.activation(w_t[:].rearrange("p a b -> p (a b)"), PS[:, 0, :], ACT.Copy).then_inc(pre_sb, 1)
            for k in range(4):
                act.wait_ge(pre_ps, 2 + k)
                act.activation(ctx_t[:, 4 * k:4 * k + 4, :], PS[:, 1 + k, 0:4 * TC].rearrange("p (a b) -> p a b", a=4),
                               ACT.Copy).then_inc(pre_sb, 1)

            with act.Fori(0, G) as g:
                have(act, a_sem["t"], g + 1)
                have(act, a_sem["kv"], g)
                act.activation(XGT[:], PS[:, 0, :], ACT.Copy).then_inc(a_sem["xt"], 1)
                have(act, a_sem["d"], g + 1)
                act.activation(PA[:], PA[:], ACT.Exp, scale=SCALE).then_inc(a_sem["e"], 1)
                have(act, a_sem["pt"], g + 1)
                have(act, a_sem["y"], g)
                act.activation(PAT, PS[:, 5, 0:2 * P], ACT.Copy).then_inc(a_sem["pt_sb"], 1)

            def slot(s, u0):
                def batch(k):
                    return s + k, (u0 + k) % 2

                def ok(k):
                    return not isinstance(s, int) or 0 <= s + k < B

                def exp(k, j):
                    b, u = batch(k)
                    have(act, b_sem["st"], b * 4 + (j + 1))
                    if not (isinstance(b, int) and 4 * b + j < 2):
                        have(act, b_sem["pv"], b * 4 + (j - 1))
                    act.activation(EX[j % 2][:], PS[:, 2 + j % 2, :], ACT.Exp, scale=SCALE).then_inc(b_sem["exp"], 1)

                if ok(2):
                    b, u = batch(2)
                    have(act, b_sem["t"], b + 1)
                    act.activation(XNT[u][:], PS[:, 4, 3 * D:4 * D], ACT.Copy, scale=n1w[:]).then_inc(b_sem["xt"], 1)
                if ok(0):
                    exp(0, 1)
                    exp(0, 2)
                if ok(2):
                    b, u = batch(2)
                    have(act, b_sem["t32"], b + 1)
                    if not (isinstance(b, int) and b < 2):
                        have(act, b_sem["qm_t"], b - 1)
                    act.activation(QS[u][:, :, 0:24].rearrange("p h (c d) -> p h c d", c=3),
                                   T32[:, 0, :].rearrange("p (h d) -> p h d", h=H).unsqueeze(2).broadcast_to([P, H, 3, DH]),
                                   ACT.Copy).then_inc(b_sem["h"], 1)
                    act.activation(KS[u][:, :, 16:40].rearrange("p h (c d) -> p h c d", c=3),
                                   T32[:, 1, :].rearrange("p (h d) -> p h d", h=H).unsqueeze(2).broadcast_to([P, H, 3, DH]),
                                   ACT.Copy).then_inc(b_sem["h"], 1)
                if ok(0):
                    exp(0, 3)
                if ok(1):
                    b, u = batch(1)
                    have(act, b_sem["qm_t"], b + 1)
                    act.activation(QM[u][:].rearrange("p c s -> p (c s)"), PS[:, 5, :].bitcast(BF16), ACT.Copy).then_inc(b_sem["qm_sb"], 1)
                if ok(0):
                    b, u = batch(0)
                    have(act, b_sem["ct"], b + 1)
                    act.activation(CT[:], PS[:, 7, 232:360], ACT.Copy).then_inc(b_sem["ct_sb"], 1)
                if ok(2):
                    b, u = batch(2)
                    have(act, b_sem["q_t"], b + 1)
                    act.activation(QT[:].rearrange("p c s -> p (c s)"), PS[:, 5, :].bitcast(BF16), ACT.Copy).then_inc(b_sem["q_sb"], 1)
                if ok(1):
                    exp(1, 0)

            for s in range(-3, 0):
                slot(s, s % 2)
            with act.Fori(0, (B - 4) // 2) as i:
                for u in range(2):
                    slot(i * 2 + u, u)
            for s in range(B - 4, B):
                slot(s, s % 2)

            def turned_tokens(m, g):
                R = r_sem[m]
                have(act, R["t"], g + 1)
                have(act, R["lg"], g)
                have(act, R["low"], g)
                scale = {"scale": n2w[:]} if m == 0 else {}
                act.activation(HT[m][:], PS[:, RB[m], :], ACT.Copy, **scale).then_inc(R["ht"], 1)
                act.activation(H2H[:, bass.ds(g * GT, GT)], PS[:, RB[m], :], ACT.Copy, **scale).then_inc(R["ht"], 1)

            R = r_sem[0]
            with act.Fori(0, G) as g:
                turned_tokens(0, g)
            have(act, R["e1"], 1)
            act.activation(LG[:, :, 0:E0], LG[:, :, 0:E0], ACT.Exp).then_inc(R["e1"], 1)
            have(act, R["e2"], 1)
            act.activation(wsel[:, :, 1], wsel[:, :, 1], ACT.Exp).then_inc(R["e2"], 1)
            for k in range(2):
                have(act, R["ct"], k + 1)
                act.activation(CWT[:, k * 1024:(k + 1) * 1024], PS[:, 2 + k, :].bitcast(BF16), ACT.Copy).then_inc(R["ct_sb"], 1)

            S = m_sem

            def chunks(m, g, inserts):
                n, per = NCH[m], MOE[m]["per"]
                base = g * n + OFF[m][0]
                start = isinstance(g, int) and m == 0 and g == 0

                def leading(k):
                    have(act, S["hid"], base + k + 1)
                    if not (start and k < LAG):
                        have(act, S["down"], base + k - (LAG - 1))
                    act.activation(HHI[turn_of(m, g, k)][:], HH[k % 2][:], ACT.Copy).then_inc(S["hi"], 1)

                for c in range(n):
                    if first_of_expert(m, c):
                        e = c // per
                        have(act, S["bc"], g * NBC[m] + OFF[m][2] + e + 1)
                        have(act, S["scaled"], g * NSC[m] + OFF[m][1] + max((e - 1) * per, 0))
                        act.activation(BC[e % 2][:], PS[:, 4, :], ACT.Copy).then_inc(S["bc_sb"], 1)
                    if c == LAG and not start:
                        out_t(m, g)
                    have(act, S["g"], base + c + 1)
                    have(act, S["hid"], base + max(c - 1, 0))
                    act.activation(SG[c % 2][:], PS[:, c % 2, :], ACT.Silu).then_inc(S["silu"], 1)
                    if not (start and c == 0):
                        leading(c - 1)
                    for f in inserts.get(c, ()):
                        f()

            def out_t(m, g):
                q = g + m * G
                have(act, S["down"], g * NCH[m] + OFF[m][0])
                have(act, S["yn"], q - 1)
                act.activation(YT[:], PS[:, 6, :], ACT.Copy).then_inc(S["yt"], 1)

            def turn(t):
                def go():
                    act.wait_ge(turn_ps, t + 1)
                    if t == 9:
                        act.activation(wr1[:], PS[:, TB[t % 2], 0:E1 + 1], ACT.Copy).then_inc(turn_hi, 1)
                    else:
                        c0, c1 = TURNS[t % 3]
                        act.activation(W1H[t // 3][:, c0:c1, :], PS[:, TB[t % 2], 0:(c1 - c0) * P].rearrange("p (c f) -> p c f", f=P),
                                       ACT.Copy).then_inc(turn_hi, 1)
                return go

            def matching(g):
                def xt():
                    have(act, c_sem["t"], g + 1)
                    have(act, c_sem["o"], g)
                    act.activation(XGT[:], PS[:, 7, :], ACT.Copy).then_inc(c_sem["xt"], 1)

                def exps():
                    have(act, c_sem["mx"], g + 1)
                    for j in range(GB):
                        act.activation(AM[:, j, :], PS[:, 7, j * TC:(j + 1) * TC], ACT.Exp, bias=nmx[:, j:j + 1],
                                       accum_out=suma[:, j:j + 1]).then_inc(c_sem["exp"], 1)

                def bexp():
                    have(act, c_sem["bt"], g * 2 + 2)
                    act.activation(BB[0:GB, :], PS[0:GB, 5, 0:P], ACT.Exp, bias=bm[:], accum_out=bs[:, 0:1]).then_inc(c_sem["bexp"], 1)

                def at_sb():
                    have(act, c_sem["at"], g + 1)
                    act.activation(AMT, PS[0:TC, 7, :], ACT.Copy).then_inc(c_sem["at_sb"], 1)

                def hq_sb():
                    have(act, c_sem["hq"], g + 1)
                    act.activation(HQ, PS[:, 7, :], ACT.Copy).then_inc(c_sem["hq_sb"], 1)

                def rexp():
                    have(act, r_sem[1]["e1"], g * 2 + 1)
                    act.activation(LG[:, 0:GB, :], LG[:, 0:GB, :], ACT.Exp).then_inc(r_sem[1]["e1"], 1)

                def ct_sb():
                    have(act, r_sem[1]["ct"], g + 1)
                    act.activation(CWT[:, bass.ds(g * GT, GT)], PS[:, 5, 0:GT // 2].bitcast(BF16), ACT.Copy).then_inc(r_sem[1]["ct_sb"], 1)

                r = (23, 25, 28) if is_last(g) else (27, 31, 35)
                return by_chunk((9, xt), (13, exps), (13, bexp), (16, at_sb), (17, hq_sb), (r[0], lambda: turned_tokens(1, g)),
                                (r[1], rexp), (r[2], ct_sb))

            mixtures(act, chunks, by_chunk(*((c, turn(t)) for t, c in enumerate(TURN_AT))), matching)
            every = G * NCH[1] + OFF[1][0]
            have(act, S["hid"], every)
            have(act, S["down"], every - LAG)
            act.activation(HHI[(every - 1) % LAG][:], HH[1][:], ACT.Copy).then_inc(S["hi"], 1)
            out_t(1, G)

        @block.vector
        def _(dve):
            class Chain:

                def __init__(self, s, per):
                    self.s, self.per, self.k, self.base = s, per, 0, 0

                def begin(self, i):
                    self.base, self.k = i * self.per, 0

                def __call__(self, ins):
                    self.k += 1
                    ins.then_inc(self.s, 1)
                    dve.wait_ge(self.s, self.base + self.k)

                def end(self):
                    assert self.k == self.per, (self.k, self.per)

            def take_wait():
                dve.memset(pad[:], 0.0)

            lnc = Chain(ln_chain, 0)

            def first(t, n):
                return t[:, 0:n]

            def rsqrt(dst, src, eps, chain=lnc, n=B):
                ta, tb = first(t_a, n), first(t_b, n)
                chain(dve.tensor_scalar(ta, src, eps, None, ALU.add))
                chain(dve.tensor_scalar(dst.bitcast(I32), ta.bitcast(I32), -0.5, RSQRT_SEED, ALU.mult, ALU.add))
                for _ in range(3):
                    chain(dve.scalar_tensor_tensor(out=tb, in0=dst, scalar=-0.5, in1=dst, op0=ALU.mult, op1=ALU.mult))
                    chain(dve.tensor_tensor(tb, tb, ta, ALU.mult))
                    chain(dve.scalar_tensor_tensor(out=dst, in0=tb, scalar=1.5, in1=dst, op0=ALU.add, op1=ALU.mult))

            def moments(st=stats, chain=lnc, n=B):
                ta, tb, tc, mn, vr = (first(t, n) for t in (t_a, t_b, t_c, mean, var))
                chain(dve.tensor_tensor(ta, st[:, :, 1], st[:, :, 4], ALU.add))
                chain(dve.tensor_scalar(mn, ta, 0.5, None, ALU.mult))
                chain(dve.tensor_tensor(tb, st[:, :, 1], st[:, :, 4], ALU.subtract))
                chain(dve.scalar_tensor_tensor(out=tc, in0=tb, scalar=0.25, in1=tb, op0=ALU.mult, op1=ALU.mult))
                chain(dve.tensor_tensor(ta, st[:, :, 2], st[:, :, 5], ALU.add))
                chain(dve.scalar_tensor_tensor(out=vr, in0=ta, scalar=1.0 / D, in1=tc, op0=ALU.mult, op1=ALU.add))

            def scales(rs=rstd, nm=nmr, chain=lnc, n=B):
                rsqrt(rs[:], first(var, n), LN_EPS, chain, n)
                chain(dve.scalar_tensor_tensor(out=nm[:], in0=first(mean, n), scalar=-1.0, in1=rs[:], op0=ALU.mult, op1=ALU.mult))

            def normalise(dst, b):
                return dve.tensor_scalar(dst, X[:, b, :], rstd[:, bass.ds(b, 1)], nmr[:, bass.ds(b, 1)], ALU.mult, ALU.add)

            for s in at_one["dve"]:
                dve.sem_inc(s, 1)
            dve.wait_ge(x_in, 16)
            with dve.Fori(0, B) as b:
                dve.bn_stats(stats[:, b, :], X[:, b, :]).then_inc(dve_c, 1)
            dve.wait_ge(dve_c, B)
            moments()
            scales()
            dve.wait_ge(small_in, 16 * 13)
            lnc(dve.tensor_scalar(bo_r[:], bo_r[:], 1.0 / H, None, ALU.mult))
            dve.wait_ge(tg_ready, 1)
            lnc(dve.tensor_scalar(tgb[:], bqv_r[:], tg[:, 1:2], None, ALU.mult))
            dve.wait_ge(consts, 1)

            A = Chain(a_chain, 4)
            with dve.Fori(0, G) as g:
                A.begin(g)
                have(dve, a_sem["t"], g)
                for j in range(GB):
                    ins = normalise(XG[:, j, :], g * GB + j)
                ins.then_inc(a_sem["xn"], 1)
                have(dve, a_sem["kv"], g + 1)
                have(dve, a_sem["s"], g)
                dve.tensor_scalar(QA[:], PS[:, 1, :], bq_c[:], None, ALU.add)
                mask = hmask[:].unsqueeze(1).broadcast_to([P, GB * L, H])
                for dst, off, bias in ((KA4, 0, bk_c), (VA4, GB * NK, bv_c)):
                    ins = dve.scalar_tensor_tensor(
                        out=dst[:].rearrange("p b (l h) -> p (b l) h", h=H),
                        in0=PS[:, 2, off:off + GB * NK].rearrange("p (a h) -> p a h", h=H),
                        scalar=bias[:], in1=mask, op0=ALU.add, op1=ALU.mult)
                ins.then_inc(a_sem["qkv_sb"], 1)
                have(dve, a_sem["v2"], g + 1)
                have(dve, a_sem["y"], g)
                dve.tensor_tensor(V2, PS[:, 3, 0:2 * D].rearrange("p (b d) -> p b d", b=2),
                                  bo_r[:].unsqueeze(1).broadcast_to([P, 2, D]), ALU.add).then_inc(a_sem["v2_sb"], 1)
                have(dve, a_sem["s"], g + 1)
                S4 = PS[:, 4, 0:GB * NK]
                A(dve.tensor_reduce(mxA[:], S4.rearrange("p (b l h) -> p b h l", b=GB, h=H), AX.X, ALU.max))
                have(dve, a_sem["pt"], g)
                dve.tensor_tensor(PA[:], S4.rearrange("p (b l h) -> p b l h", b=GB, h=H),
                                  mxA[:].unsqueeze(2).broadcast_to([P, GB, L, H]), ALU.subtract).then_inc(a_sem["d"], 1)
                have(dve, a_sem["e"], g + 1)
                A(dve.tensor_reduce(mxA[:], PA[:].rearrange("p b l h -> p b h l"), AX.X, ALU.add))
                A(dve.reciprocal(mxA[:], mxA[:]))
                dve.tensor_tensor(PA[:], PA[:], mxA[:].unsqueeze(2).broadcast_to([P, GB, L, H]), ALU.mult).then_inc(a_sem["p"], 1)
                have(dve, a_sem["y"], g + 1)
                Xg = X[:, bass.ds(g * GB, GB), :]
                for u in range(2):
                    Xu = Xg.rearrange("p (k u) d -> p k u d", u=2)[:, :, u, :]
                    ins = dve.scalar_tensor_tensor(out=Xu, in0=PS[:, 6 + u, 0:2 * D].rearrange("p (b d) -> p b d", b=2),
                                                   scalar=tg[:, 0:1], in1=Xu, op0=ALU.mult, op1=ALU.add)
                A(ins)
                for j in range(GB):
                    ins = dve.bn_stats(stats[:, g * GB + j, :], X[:, g * GB + j, :])
                ins.then_inc(a_sem["x"], 1)
                A.end()
            have(dve, a_sem["x"], G)
            moments()
            scales()
            lnc(dve.tensor_tensor(t_a[:], rstd[:], rstd[:], ALU.mult))
            lnc(dve.tensor_tensor(t_c[:], t_a[:], var[:], ALU.mult))
            rsqrt(r2[:], t_c[:], RMS_EPS)

            PER = 6
            Bc = Chain(b_chain, PER)

            def slot(s, u0):
                def batch(k):
                    return s + k, (u0 + k) % 2

                def ok(k):
                    return not isinstance(s, int) or 0 <= s + k < B

                def rowmax(j):
                    b, u = batch(1)
                    have(dve, b_sem["s"], b * 4 + (j + 1))
                    dve.tensor_reduce(nmax[:, 4 * j:4 * j + 4], PS[:, j % 2, :].rearrange("p (h t) -> p h t", h=4),
                                      AX.X, ALU.max, negate=True).then_inc(b_sem["max"], 1)

                if ok(1):
                    rowmax(0)
                    rowmax(1)
                    rowmax(2)
                if ok(2):
                    b, u = batch(2)
                    Bc.begin(b)
                    have(dve, b_sem["qkv"], b + 1)
                    dve.tensor_scalar(T32[:], PS[:, 4, 0:2 * D].rearrange("p (a d) -> p a d", a=2), r2[:, bass.ds(b, 1)], None,
                                      ALU.mult).then_inc(b_sem["t32"], 1)
                    dve.tensor_scalar(VA[:, b, 0:VW * H].rearrange("p (h d) -> p h d", h=H)[:, :, 0:DH],
                                      PS[:, 4, 2 * D:3 * D].rearrange("p (h d) -> p h d", h=H), r2[:, bass.ds(b, 1)], None,
                                      ALU.mult).then_inc(b_sem["v"], 1)
                if ok(1):
                    rowmax(3)
                    b, u = batch(1)
                    have(dve, b_sem["max"], b * 4 + 4)
                    have(dve, b_sem["q_t"], b + 1)
                    dve.tensor_copy(QS[u][:, :, 48], nmax[:]).then_inc(b_sem["m"], 1)
                    have(dve, b_sem["m"], b * 2 + 1)
                    dve.tensor_tensor(QS[u][:, :, 49], nmax[:], QS[u][:, :, 48], ALU.subtract).then_inc(b_sem["m"], 1)
                if ok(2):
                    b, u = batch(2)
                    have(dve, b_sem["h"], b * 2 + 2)
                    q, k = T32[:, 0, :].rearrange("p (h d) -> p h d", h=H), T32[:, 1, :].rearrange("p (h d) -> p h d", h=H)
                    Bc(dve.tensor_tensor(q, q, QS[u][:, :, 0:8], ALU.subtract))
                    Bc(dve.tensor_tensor(k, k, KS[u][:, :, 16:24], ALU.subtract))
                    Bc(dve.tensor_copy(QS[u][:, :, 32:48].rearrange("p h (c d) -> p h c d", c=2),
                                       q.unsqueeze(2).broadcast_to([P, H, 2, DH])))
                    Bc(dve.tensor_copy(KS[u][:].rearrange("p h (c d) -> p h c d", c=2)[:, :, :, 8:16],
                                       k.unsqueeze(2).broadcast_to([P, H, 2, DH])))
                    Bc(dve.memset(QS[u][:, :, 48:50], 0.0))
                    Bc(dve.tensor_tensor(QS[u][:, :, 24:32], q, QS[u][:, :, 32:40], ALU.subtract))
                    dve.tensor_tensor(KS[u][:, :, 0:8], k, KS[u][:, :, 8:16], ALU.subtract).then_inc(b_sem["split"], 1)
                    Bc.end()
                if ok(0):
                    b, u = batch(0)
                    O = PS[:, 7, 0:VW * H].rearrange("p (h d) -> p h d", h=H)
                    have(dve, b_sem["pv"], b * 4 + 4)
                    dve.reciprocal(rden[:], O[:, :, DH]).then_inc(b_sem["norm"], 1)
                    have(dve, b_sem["norm"], b * 2 + 1)
                    dve.tensor_tensor(CN[:], O[:, :, 0:DH], rden[:].unsqueeze(2).broadcast_to([P, H, DH]),
                                      ALU.mult).then_inc(b_sem["norm"], 1)
                if ok(2):
                    b, u = batch(2)
                    have(dve, b_sem["k_t"], b + 1)
                    src = PS[:, 6, :].bitcast(BF16)
                    dve.tensor_copy(KT[u][0][0:64].rearrange("p c s -> p (c s)"), src[0:64, :])
                    dve.tensor_copy(KT[u][1][64:128].rearrange("p c s -> p (c s)"), src[64:128, :]).then_inc(b_sem["k_sb"], 1)
                if ok(0):
                    b, u = batch(0)
                    have(dve, b_sem["wo"], b + 1)
                    have(dve, b_sem["z0"], b + 1)
                    dve.tensor_tensor(Z[:, b, :], PS[:, 7, 360:488], Z[:, b, :], ALU.add).then_inc(b_sem["z"], 1)
                    have(dve, b_sem["z"], b + 1)
                    dve.bn_stats(stats[:, b, :], Z[:, b, :]).then_inc(b_sem["zs"], 1)
                if ok(3):
                    b, u = batch(3)
                    if not (isinstance(b, int) and b < 2):
                        have(dve, b_sem["t"], b - 1)
                        have(dve, b_sem["z0"], b - 1)
                    normalise(XNB[u][:], b).then_inc(b_sem["xn"], 1)

            for s in range(-3, 0):
                slot(s, s % 2)
            with dve.Fori(0, (B - 4) // 2) as i:
                for u in range(2):
                    slot(i * 2 + u, u)
            for s in range(B - 4, B):
                slot(s, s % 2)
            have(dve, b_sem["zs"], B)
            moments()
            lnc(dve.tensor_tensor(t_c[:], mean[:], mean[:], ALU.mult))
            lnc(dve.tensor_tensor(t_c[:], t_c[:], var[:], ALU.add))
            rsqrt(r2[:], t_c[:], RMS_EPS)

            def less_maximum(m, C, nb):
                R, E = r_sem[m], (E0, E1)[m]
                EW = E + m
                LGb, LGm, tb = LG[:, 0:nb, 0:EW], LG[:, 0:nb, 0:E], first(t_b, nb)
                wide = tb.unsqueeze(2).broadcast_to([P, nb, E])
                C(dve.tensor_copy(LGb, PS[:, LB[m], 0:nb * EW].rearrange("p (b e) -> p b e", b=nb)))
                C(dve.tensor_reduce(tb, LGm, AX.X, ALU.max))
                if m == 1:
                    C(dve.tensor_scalar(LG[:, 0:nb, E1:E1 + 1], LG[:, 0:nb, E1:E1 + 1], -1.0, None, ALU.mult))
                dve.tensor_tensor(LGm, LGm, wide, ALU.subtract).then_inc(R["e1"], 1)

            def two_largest(m, g, C, nb):
                R, E = r_sem[m], (E0, E1)[m]
                EW = E + m
                LGm, PRm, tb = LG[:, 0:nb, 0:E], PR[:, 0:nb, 0:E], first(t_b, nb)
                wide = tb.unsqueeze(2).broadcast_to([P, nb, E])
                have(dve, R["e1"], g * 2 + 2)
                C(dve.tensor_reduce(tb, LGm, AX.X, ALU.add))
                C(dve.reciprocal(tb, tb))
                C(dve.tensor_tensor(PRm, LGm, wide, ALU.mult))
                take_wait()
                for b in range(nb):
                    ins = dve.max(top[:, b, :], PR[:, b, 0:E])
                C(ins)
                take_wait()
                for b in range(nb):
                    ins = dve.max_index(topi[:, b, :], top[:, b, :], PR[:, b, 0:E])
                C(ins)
                C(dve.tensor_copy(topf[:, 0:nb, :], topi[:, 0:nb, 0:2]))

            def weights_of_two(m, g, C, nb):
                R, E = r_sem[m], (E0, E1)[m]
                tb = first(t_b, nb)
                w0, w1, p0, p1 = wsel[:, 0:nb, 0], wsel[:, 0:nb, 1], top[:, 0:nb, 0], top[:, 0:nb, 1]
                if m == 0:
                    dve.tensor_tensor(w1, p1, p0, ALU.subtract).then_inc(R["e2"], 1)
                    have(dve, R["e2"], g * 2 + 2)
                    C(dve.tensor_scalar(tb, w1, 1.0, None, ALU.add))
                    C(dve.reciprocal(w0, tb))
                    C(dve.tensor_tensor(w1, w1, w0, ALU.mult))
                else:
                    C(dve.tensor_tensor(tb, p0, p1, ALU.add))
                    C(dve.reciprocal(tb, tb))
                    C(dve.tensor_tensor(w0, p0, tb, ALU.mult))
                    C(dve.tensor_tensor(w1, p1, tb, ALU.mult))
                dve.wait_ge(consts, 2)
                io = iota_e[:, 0:E].unsqueeze(1).broadcast_to([P, nb, E])
                cm, ct = comb[:, 0:nb, 0:E], combt[:, 0:nb, 0:E]
                C(dve.tensor_tensor(cm, io, topf[:, 0:nb, 0:1].broadcast_to([P, nb, E]), ALU.is_equal))
                C(dve.tensor_tensor(cm, cm, wsel[:, 0:nb, 0:1].broadcast_to([P, nb, E]), ALU.mult))
                C(dve.tensor_tensor(ct, io, topf[:, 0:nb, 1:2].broadcast_to([P, nb, E]), ALU.is_equal))
                C(dve.tensor_tensor(ct, ct, wsel[:, 0:nb, 1:2].broadcast_to([P, nb, E]), ALU.mult))
                C(dve.tensor_tensor(cm, cm, ct, ALU.add))

            def in_pieces(m, g, C, nb):
                R, E = r_sem[m], (E0, E1)[m]
                EW = E + m
                if m == 1:
                    sg = comb[:, 0:nb, E1:E1 + 1]
                    C(dve.tensor_scalar(sg, LG[:, 0:nb, E1:E1 + 1], 1.0, None, ALU.add))
                    C(dve.reciprocal(sg, sg))
                have(dve, R["ct"], g)
                cf = comb[:, 0:nb, 0:EW]
                for p in range(3):
                    piece = CS[:, 0:nb, p * PIECE:p * PIECE + EW]
                    ins = dve.tensor_copy(piece, cf)
                    if p == 2:
                        ins.then_inc(R["cs"], 1)
                    else:
                        C(ins)
                        C(dve.tensor_tensor(cf, cf, piece, ALU.subtract))
                C.end()

            R = r_sem[0]
            with dve.Fori(0, G) as g:
                have(dve, R["t"], g)
                for j in range(GB):
                    b = g * GB + j
                    ins = dve.tensor_scalar(HG[0][:, j, :], Z[:, b, :], r2[:, bass.ds(b, 1)], None, ALU.mult)
                ins.then_inc(R["h"], 1)
            have(dve, R["lg"], G)
            C0 = Chain(r_chain[0], 20)
            C0.begin(0)
            less_maximum(0, C0, B)
            two_largest(0, 0, C0, B)
            weights_of_two(0, 0, C0, B)
            in_pieces(0, 0, C0, B)

            S = m_sem

            def chunks(m, g, inserts):
                n, per = NCH[m], MOE[m]["per"]
                base = g * n + OFF[m][0]
                start = isinstance(g, int) and m == 0 and g == 0

                def rest(k):
                    have(dve, S["hi"], base + k + 1)
                    if not (start and k < LAG):
                        have(dve, S["down"], base + k - (LAG - 1))
                    t = turn_of(m, g, k)
                    dve.tensor_tensor(HLO[t][:], HH[k % 2][:], HHI[t][:].bitcast(F32), ALU.subtract).then_inc(S["lo"], 1)

                for c in range(n):
                    have(dve, S["u"], base + c + 1)
                    if c < NSC[m]:
                        have(dve, S["scaled"], g * NSC[m] + OFF[m][1] + c + 1)
                    else:
                        have(dve, S["silu"], base + c + 1)
                    if not (start and c < 2):
                        have(dve, S["lo"], base + c - 1)
                    dve.tensor_tensor(HH[c % 2][:], PS[:, 2 + c % 2, :], SG[c % 2][:], ALU.mult).then_inc(S["hid"], 1)
                    if not (start and c == 0):
                        rest(c - 1)
                    if c == LAG + 1 and not start:
                        residual(m, g)
                    for f in inserts.get(c, ()):
                        f()

            def ffn_input(g):
                Xg = X[:, g * GB:(g + 1) * GB, :]
                dve.scalar_tensor_tensor(out=Xg, in0=Z[:, g * GB:(g + 1) * GB, :], scalar=tg[:, 2:3], in1=Xg,
                                         op0=ALU.mult, op1=ALU.add).then_inc(S["yx"], 1)

            def residual(m, g):
                q = g + m * G
                of_first = m == 0 or (isinstance(g, int) and g == 0)
                have(dve, S["yn"], q)
                have(dve, S["yx"], G)
                at = (g - 1) * GB if not (m == 1 and of_first) else (G - 1) * GB
                Xg = X[:, bass.ds(at, GB), :]
                dve.scalar_tensor_tensor(out=Xg, in0=PS[:, 7, :].rearrange("p (b d) -> p b d", b=GB),
                                         scalar=tg[:, 2:3] if of_first else tg[:, 3:4], in1=Xg,
                                         op0=ALU.mult, op1=ALU.add).then_inc(S["x"], 1)
                if of_first:
                    have(dve, S["x"], q)
                    take_wait()
                    for j in range(GB):
                        ins = dve.bn_stats(gstats[:, j, :], X[:, at + j, :])
                    ins.then_inc(S["st"], 1)

            def turn(t):
                def go():
                    dve.wait_ge(turn_hi, t + 1)
                    c0, c1 = TURNS[t % 3]
                    dve.tensor_tensor(W1L[t // 3][:, c0:c1, :], PS[:, TB[t % 2], 0:(c1 - c0) * P].rearrange("p (c f) -> p c f", f=P),
                                      W1H[t // 3][:, c0:c1, :].bitcast(F32), ALU.subtract).then_inc(turn_lo, 1)
                return go

            CC = Chain(c_chain, 3)
            G_LN = Chain(m_ln, 18)
            CR = Chain(r_chain[1], 24)

            def matching(g):
                def norm_group(dst, k, signal):
                    for j in range(GB):
                        ins = dve.tensor_scalar(dst[:, j, :], X[:, g * GB + j, :], grstd[:, k + j:k + j + 1], gnmr[:, k + j:k + j + 1],
                                                ALU.mult, ALU.add)
                    ins.then_inc(signal, 1)

                def norm_a(i=g):
                    have(dve, S["st"], min(i + 1, G) if isinstance(i, int) else i + 1)
                    have(dve, c_sem["x"], i)
                    G_LN.begin(i)
                    moments(gstats, G_LN, 2 * GB)

                def norm_b():
                    scales(grstd, gnmr, G_LN, 2 * GB)
                    G_LN.end()

                def xn():
                    have(dve, c_sem["hc"], g)
                    norm_group(XG, 0, c_sem["xn"])

                def e3():
                    have(dve, c_sem["xt"], g + 1)
                    have(dve, c_sem["s"], g)
                    have(dve, c_sem["o"], g)
                    dve.tensor_scalar(E3T[:], XGT[:], w3s[:], w2s[:], ALU.mult, ALU.add).then_inc(c_sem["e3"], 1)

                def mx():
                    CC.begin(g)
                    have(dve, c_sem["s"], g + 1)
                    CC(dve.tensor_reduce(nmx[:], PS[:, 7, 0:GB * TC].rearrange("p (b t) -> p b t", b=GB), AX.X, ALU.max,
                                         negate=True))
                    dve.scalar_tensor_tensor(out=bt[:], in0=PS[:, 7, GB * TC:GB * TC + GB], scalar=bsim_c[:], in1=nmx[:],
                                             op0=ALU.add, op1=ALU.subtract).then_inc(c_sem["mx"], 1)

                def bmax():
                    have(dve, c_sem["bt"], g * 2 + 1)
                    dve.tensor_reduce(bm[:], PS[0:GB, 5, 0:P], AX.X, ALU.max, negate=True).then_inc(c_sem["bt"], 1)

                def soft():
                    have(dve, c_sem["exp"], g * GB + GB)
                    CC(dve.reciprocal(rca[:], suma[:]))
                    dve.tensor_tensor(AM, AM, rca[:].unsqueeze(2).broadcast_to([P, GB, TC]), ALU.mult).then_inc(c_sem["a"], 1)
                    have(dve, c_sem["bexp"], g + 1)
                    CC(dve.reciprocal(bs[:, 1:2], bs[:, 0:1]))
                    dve.tensor_scalar(BB[0:GB, :], BB[0:GB, :], bs[:, 1:2], None, ALU.mult).then_inc(c_sem["bb"], 1)
                    CC.end()

                def bcol():
                    have(dve, c_sem["bbt"], g + 1)
                    dve.tensor_copy(BCOL[:], PS[:, 5, P:P + GB]).then_inc(c_sem["bc"], 1)

                def product():
                    have(dve, c_sem["hq_sb"], g + 1)
                    dve.tensor_tensor(XH[:], PS[:, 7, :], XGT[:], ALU.mult).then_inc(c_sem["xh"], 1)

                def weights():
                    have(dve, c_sem["hc"], g + 1)
                    dve.tensor_copy(HC[:], PS[:, 5, 2 * P:2 * P + GB]).then_inc(c_sem["hcr"], 1)
                    have(dve, c_sem["hcr"], g + 1)
                    for j in range(GB):
                        ins = dve.scalar_tensor_tensor(out=WB[:, j, :], in0=wqv[:, 3, :], scalar=HC[:, j:j + 1], in1=wqv[:, 0, :],
                                                       op0=ALU.mult, op1=ALU.add)
                    ins.then_inc(c_sem["wb"], 1)

                def update():
                    have(dve, c_sem["o"], g + 1)
                    have(dve, c_sem["xb"], g * 2 + 2)
                    Xg = X[:, bass.ds(g * GB, GB), :]
                    dve.scalar_tensor_tensor(out=Xg, in0=PS[:, 5, :].rearrange("p (b d) -> p b d", b=GB), scalar=tg[:, 1:2],
                                             in1=Xg, op0=ALU.mult, op1=ALU.add).then_inc(c_sem["xu"], 1)
                    have(dve, c_sem["xu"], g + 1)
                    take_wait()
                    for j in range(GB):
                        ins = dve.bn_stats(gstats[:, GB + j, :], X[:, g * GB + j, :])
                    ins.then_inc(c_sem["x"], 1)

                def hn():
                    norm_group(HG1, GB, r_sem[1]["h"])

                def route_a():
                    have(dve, r_sem[1]["lg"], g + 1)
                    CR.begin(g)
                    less_maximum(1, CR, GB)

                steps = [(5, norm_a), (6, norm_b), (7, xn), (9, e3), (11, mx), (12, bmax), (14, soft), (16, bcol), (18, product),
                         (18, weights), (20, update)]
                if is_last(g):
                    steps += [(21, lambda: norm_a(G)), (21, norm_b)]
                r = (22, 24, 25, 25, 26) if is_last(g) else (25, 28, 32, 33, 34)
                steps += [(r[0], hn), (r[1], route_a), (r[2], lambda: two_largest(1, g, CR, GB)),
                          (r[3], lambda: weights_of_two(1, g, CR, GB)), (r[4], lambda: in_pieces(1, g, CR, GB))]
                return by_chunk(*steps)

            dve.memset(gstats[:], 0.0)
            mixtures(dve, chunks, by_chunk(*((c, turn(t)) for t, c in enumerate(TURN_AT[:9])),
                                           *((8 + g, lambda g=g: ffn_input(g)) for g in range(G))), matching)
            every = G * NCH[1] + OFF[1][0]
            have(dve, S["hi"], every)
            have(dve, S["down"], every - LAG)
            t = (every - 1) % LAG
            dve.tensor_tensor(HLO[t][:], HH[1][:], HHI[t][:].bitcast(F32), ALU.subtract).then_inc(S["lo"], 1)
            residual(1, G)

        @block.tensor
        def _(pe):
            for s in at_one["pe"]:
                pe.sem_inc(s, 1)
            pe.wait_ge(consts, 1)
            pe.wait_ge(wa_in, 16 * 4)
            for i in range(4):
                ins = pe.transpose(PS[:, 0, i * D:(i + 1) * D], w_nat[:, i, :], identf[:])
            ins.then_inc(pre_ps, 1)
            pe.wait_ge(ctx_in, 16)
            for k in range(4):
                for j in range(4):
                    ins = pe.transpose(PS[:, 1 + k, j * TC:(j + 1) * TC], ctx_nat[:, 4 * k + j, :], identf[0:TC, 0:TC])
                ins.then_inc(pre_ps, 1)
            pe.wait_ge(pre_sb, 5)

            with pe.Fori(0, G) as g:
                have(pe, a_sem["xn"], g + 1)
                have(pe, a_sem["xt"], g)
                for j in range(GB):
                    ins = pe.transpose(PS[:, 0, j * P:(j + 1) * P], XG[:, j, :], identf[:])
                ins.then_inc(a_sem["t"], 1)
                have(pe, a_sem["xt"], g + 1)
                have(pe, a_sem["qkv_sb"], g)
                pe.matmul(PS[:, 1, :], w_t[:, 0, :], XGT[:], start=True, stop=True)
                keys = ctx_t[:, bass.ds(g * GB, GB), 0:NK]
                pe.matmul(PS[:, 2, 0:GB * NK], w_t[:, 1, :], keys, start=True, stop=True)
                pe.matmul(PS[:, 2, GB * NK:2 * GB * NK], w_t[:, 2, :], keys, start=True, stop=True).then_inc(a_sem["kv"], 1)
                have(pe, a_sem["qkv_sb"], g + 1)
                have(pe, a_sem["v2_sb"], g)
                for j in range(2):
                    ins = pe.matmul(PS[:, 3, j * D:(j + 1) * D], VA4[:, 2 * j:2 * j + 2, :].rearrange("p b k -> p (b k)"), w_t[:, 3, :],
                                    start=True, stop=True)
                ins.then_inc(a_sem["v2"], 1)
                have(pe, a_sem["p"], g)
                for j in range(GB):
                    ins = pe.matmul(PS[:, 4, j * NK:(j + 1) * NK], QA[:, j * P:(j + 1) * P], KA4[:, j, :], start=True, stop=True)
                ins.then_inc(a_sem["s"], 1)
                have(pe, a_sem["p"], g + 1)
                have(pe, a_sem["pt_sb"], g)
                for j in range(2):
                    ins = pe.transpose(PS[:, 5, j * P:(j + 1) * P], PA[:, 2 * j:2 * j + 2, :, :].rearrange("p b l h -> p (b l h)"),
                                       identf[:])
                ins.then_inc(a_sem["pt"], 1)
                have(pe, a_sem["pt_sb"], g + 1)
                have(pe, a_sem["v2_sb"], g + 1)
                have(pe, a_sem["x"], g)
                for j in range(GB):
                    k, r = j // 2, slice(NK * (j % 2), NK * (j % 2 + 1))
                    ins = pe.matmul(PS[:, 6 + j % 2, k * D:(k + 1) * D], PAT[r, k * P:(k + 1) * P], V2[r, k, :], start=True, stop=True)
                ins.then_inc(a_sem["y"], 1)

            have(pe, a_sem["x"], G)
            pe.wait_ge(wb_in, 16 * 4)

            def slot(s, u0):
                def batch(k):
                    return s + k, (u0 + k) % 2

                def ok(k):
                    return not isinstance(s, int) or 0 <= s + k < B

                def scores(j):
                    b, u = batch(1)
                    if j == 0:
                        have(pe, b_sem["k_sb"], b + 1)
                        have(pe, b_sem["q_sb"], b + 1)
                    if not (isinstance(b, int) and 4 * b + j < 2):
                        have(pe, b_sem["max"], b * 4 + (j - 1))
                    for h in range(4 * j, 4 * j + 4):
                        ins = pe.matmul(PS[:, j % 2, (h % 4) * P:(h % 4 + 1) * P], QT[:, h // 2, :], KT[u][h % 2][:, h // 2, :],
                                        start=True, stop=True)
                    ins.then_inc(b_sem["s"], 1)

                def scores_t(k, j):
                    b, u = batch(k)
                    if j == 0:
                        have(pe, b_sem["qm_sb"], b + 1)
                    if not (isinstance(b, int) and 4 * b + j < 2):
                        have(pe, b_sem["exp"], b * 4 + (j - 1))
                    for h in range(4 * j, 4 * j + 4):
                        ins = pe.matmul(PS[:, 2 + j % 2, (h % 4) * P:(h % 4 + 1) * P], KT[u][h % 2][:, h // 2, :], QM[u][:, h // 2, :],
                                        start=True, stop=True)
                    ins.then_inc(b_sem["st"], 1)

                def values(j):
                    b, u = batch(0)
                    have(pe, b_sem["exp"], b * 4 + (j + 1))
                    if j == 0 and not (isinstance(b, int) and b == 0):
                        have(pe, b_sem["z"], b)
                    for h in range(4 * j, 4 * j + 4):
                        ins = pe.matmul(PS[:, 7, VW * h:VW * h + PV_N], EX[j % 2][:, (h % 4) * P:(h % 4 + 1) * P],
                                        VA[:, b, VW * h:VW * h + PV_N], start=True, stop=True)
                    ins.then_inc(b_sem["pv"], 1)

                if ok(1):
                    scores(0)
                    scores(1)
                if ok(2):
                    b, u = batch(2)
                    have(pe, b_sem["xn"], b + 1)
                    if not (isinstance(b, int) and b == 0):
                        have(pe, b_sem["xt"], b)
                        have(pe, b_sem["v"], b)
                    pe.transpose(PS[:, 4, 3 * D:4 * D], XNB[u][:], identf[:]).then_inc(b_sem["t"], 1)
                if ok(0):
                    scores_t(0, 1)
                    values(0)
                if ok(1):
                    scores(2)
                if ok(0):
                    scores_t(0, 2)
                    values(1)
                if ok(2):
                    b, u = batch(2)
                    have(pe, b_sem["xt"], b + 1)
                    if not (isinstance(b, int) and b == 0):
                        have(pe, b_sem["v"], b)
                    pe.matmul(PS[:, 4, 0:3 * D], XNT[u][:], wqkv[:], start=True, stop=True).then_inc(b_sem["qkv"], 1)
                if ok(1):
                    scores(3)
                if ok(0):
                    scores_t(0, 3)
                    values(2)
                    values(3)
                if ok(1):
                    b, u = batch(1)
                    have(pe, b_sem["m"], b * 2 + 2)
                    have(pe, b_sem["q_sb"], b + 1)
                    for c in range(H // 2):
                        ins = pe.transpose(PS[:, 5, :].bitcast(BF16)[:, c * P:(c + 1) * P],
                                           QS[u][:, 2 * c:2 * c + 2, :].rearrange("p h d -> p (h d)"), identb[:])
                    ins.then_inc(b_sem["qm_t"], 1)
                if ok(0):
                    b, u = batch(0)
                    have(pe, b_sem["norm"], b * 2 + 2)
                    pe.transpose(PS[:, 7, 232:360], CN[:].rearrange("p h d -> p (h d)"), identf[:]).then_inc(b_sem["ct"], 1)
                if ok(2):
                    b, u = batch(2)
                    have(pe, b_sem["split"], b + 1)
                    if not (isinstance(b, int) and b == 0):
                        have(pe, b_sem["k_sb"], b)
                    for c in range(H // 2):
                        ins = pe.transpose(PS[:, 6, :].bitcast(BF16)[:, c * P:(c + 1) * P],
                                           KS[u][:, 2 * c:2 * c + 2, :].rearrange("p h d -> p (h d)"), identb[:])
                    ins.then_inc(b_sem["k_t"], 1)
                if ok(0):
                    b, u = batch(0)
                    have(pe, b_sem["ct_sb"], b + 1)
                    pe.matmul(PS[:, 7, 360:488], CT[:], wo[:], start=True, stop=True).then_inc(b_sem["wo"], 1)
                if ok(2):
                    b, u = batch(2)
                    if not (isinstance(b, int) and b == 0):
                        have(pe, b_sem["qm_sb"], b)
                    for c in range(H // 2):
                        ins = pe.transpose(PS[:, 5, :].bitcast(BF16)[:, c * P:(c + 1) * P],
                                           QS[u][:, 2 * c:2 * c + 2, :].rearrange("p h d -> p (h d)"), identb[:])
                    ins.then_inc(b_sem["q_t"], 1)
                if ok(1):
                    scores_t(1, 0)

            for s in range(-3, 0):
                slot(s, s % 2)
            with pe.Fori(0, (B - 4) // 2) as i:
                for u in range(2):
                    slot(i * 2 + u, u)
            for s in range(B - 4, B):
                slot(s, s % 2)

            def logits(m, g, at):
                R, EW, w = r_sem[m], (E0, E1 + 1)[m], (wr0, wr1)[m]
                have(pe, R["ht"], g * 2 + 2)
                for j in range(GB):
                    ins = pe.matmul(PS[:, LB[m], bass.ds((at + j) * EW, EW)], HT[m][:, j * P:(j + 1) * P], w[:], start=True, stop=True)
                ins.then_inc(R["lg"], 1)

            def turn_tokens(m, g):
                R = r_sem[m]
                have(pe, R["h"], g + 1)
                have(pe, R["ht"], g * 2)
                for j in range(GB):
                    ins = pe.transpose(PS[:, RB[m], j * P:(j + 1) * P], HG[m][:, j, :], identf[:])
                ins.then_inc(R["t"], 1)

            have(pe, b_sem["z"], B)
            pe.wait_ge(wr_in, 16 * 3)
            with pe.Fori(0, G) as g:
                turn_tokens(0, g)
                logits(0, g, g * GB)
            have(pe, r_sem[0]["cs"], 1)
            for b in range(B):
                ins = pe.transpose(PS[:, 2 + b // 8, :].bitcast(BF16)[:, (b % 8) * P:(b % 8 + 1) * P], CS[:, b, :], identb[:])
                if b % 8 == 7:
                    ins.then_inc(r_sem[0]["ct"], 1)
            have(pe, r_sem[0]["ct_sb"], 2)
            have(pe, r_sem[0]["low"], G)
            pe.wait_ge(halved, 3)

            S = m_sem

            def split_product(bank, high, low, x_high, x_low, start=True, stop=True):
                pe.matmul(PS[:, bank, :], high, x_high, start=start, stop=False)
                pe.matmul(PS[:, bank, :], high, x_low, start=False, stop=False)
                return pe.matmul(PS[:, bank, :], low, x_high, start=False, stop=stop)

            def down(m, g, base, k, q):
                have(pe, S["lo"], base + k + 1)
                if k == 0:
                    have(pe, S["yt"], q)
                t = turn_of(m, g, k)
                split_product(6, WH[m][2][:, k, :], WL[m][2][:, k, :], HHI[t][:], HLO[t][:],
                              start=(k == 0), stop=(k == NCH[m] - 1)).then_inc(S["down"], 1)

            def turn_out(q):
                have(pe, S["yt"], q)
                have(pe, S["x"], q - 1)
                if not isinstance(q, int):
                    have(pe, c_sem["xh"], q - 1)
                elif q > 1:
                    have(pe, c_sem["xh"], {4: 3, 5: 3}.get(q, G))
                if isinstance(q, int) and q == 5:
                    have(pe, c_sem["exp"], G * GB)
                for j in range(GB):
                    ins = pe.transpose(PS[:, 7, j * P:(j + 1) * P], YT[:, j * P:(j + 1) * P], identf[:])
                ins.then_inc(S["yn"], 1)

            def chunks(m, g, inserts):
                n, per = NCH[m], MOE[m]["per"]
                base = g * n + OFF[m][0]
                start = isinstance(g, int) and m == 0 and g == 0
                q = g + m * G
                xh, xl = H2H[:, bass.ds(g * GT, GT)], H2L[:, bass.ds(g * GT, GT)]
                before = 0 if m == 1 and isinstance(g, int) and g == 0 else m
                if m == 1:
                    have(pe, r_sem[1]["low"], g + 1)
                    have(pe, r_sem[1]["ct_sb"], g + 1)
                for c in range(n):
                    if first_of_expert(m, c):
                        e = c // per
                        have(pe, S["bc_sb"], g * NBC[m] + OFF[m][2] + e)
                        pe.matmul(PS[:, 4, :], SEL[m][:, e, :], CWT[:, bass.ds(g * GT, GT)], start=True, stop=True).then_inc(S["bc"], 1)
                    if not (start and c < 2):
                        have(pe, S["silu"], base + c - 1)
                    split_product(c % 2, WH[m][0][:, c, :], WL[m][0][:, c, :], xh, xl).then_inc(S["g"], 1)
                    if not (start and c < 2):
                        have(pe, S["hid"], base + c - 1)
                    split_product(2 + c % 2, WH[m][1][:, c, :], WL[m][1][:, c, :], xh, xl).then_inc(S["u"], 1)
                    if c >= LAG:
                        down(m, g, base, c - LAG, q)
                    elif not start:
                        down(before, g - 1, base - NCH[before], NCH[before] + c - LAG, q)
                    if c == LAG + 1 and not start:
                        turn_out(q)
                    for f in inserts.get(c, ()):
                        f()

            def turn(t):
                def go():
                    bank = TB[t % 2]
                    if t == 9:
                        pe.wait_ge(turn_lo, 8)
                        pe.transpose(PS[:, bank, 0:E1 + 1], wr1_nat[:], identf[0:E1 + 1, 0:E1 + 1]).then_inc(turn_ps, 1)
                        pe.wait_ge(turn_lo, 9)
                        pe.wait_ge(turn_hi, 10)
                        return
                    if t % 3 == 0:
                        pe.wait_ge(raw_in[3 + t // 3], 32)
                    if t >= 2:
                        pe.wait_ge(turn_lo, t - 1)
                    c0, c1 = TURNS[t % 3]
                    for c in range(c0, c1):
                        ins = pe.transpose(PS[:, bank, (c - c0) * P:(c - c0 + 1) * P], raw[(t // 3 + 1) % 2][:, c, :], identf[:])
                    ins.then_inc(turn_ps, 1)
                return go

            def matching(g):
                def t():
                    have(pe, c_sem["xn"], g + 1)
                    for j in range(GB):
                        ins = pe.transpose(PS[:, 7, j * P:(j + 1) * P], XG[:, j, :], identf[:])
                    ins.then_inc(c_sem["t"], 1)

                def sims():
                    have(pe, c_sem["e3"], g + 1)
                    have(pe, c_sem["xt"], g + 1)
                    for j in range(GB):
                        pe.matmul(PS[:, 7, j * TC:(j + 1) * TC], E3T[:, j * P:(j + 1) * P], ctx_t[:, g * GB + j, :], start=True, stop=True)
                        ins = pe.matmul(PS[:, 7, GB * TC + j:GB * TC + j + 1], XGT[:, j * P:(j + 1) * P], w1_c[:], start=True, stop=True)
                    ins.then_inc(c_sem["s"], 1)

                def bts():
                    have(pe, c_sem["mx"], g + 1)
                    pe.transpose(PS[0:GB, 5, 0:P], bt[:], identf[:]).then_inc(c_sem["bt"], 1)

                def ats():
                    have(pe, c_sem["a"], g + 1)
                    if is_last(g):
                        have(pe, S["x"], G + 1)
                    for j in range(GB):
                        ins = pe.transpose(PS[0:TC, 7, j * P:(j + 1) * P], AM[:, j, :], identf[:])
                    ins.then_inc(c_sem["at"], 1)

                def bbts():
                    have(pe, c_sem["bb"], g + 1)
                    pe.transpose(PS[:, 5, P:2 * P], BB[:], identf[:]).then_inc(c_sem["bbt"], 1)

                def hqs():
                    have(pe, c_sem["at_sb"], g + 1)
                    have(pe, c_sem["cg"], g * 2 + 2)
                    for j in range(GB):
                        ins = pe.matmul(PS[:, 7, j * P:(j + 1) * P], CG[:, j, :], AMT[:, j * P:(j + 1) * P], start=True, stop=True)
                    ins.then_inc(c_sem["hq"], 1)

                def hcs():
                    have(pe, c_sem["bc"], g + 1)
                    have(pe, r_sem[1]["ct_sb"], g)
                    for j in range(GB):
                        ins = pe.matmul(PS[:, 5, 2 * P + j:2 * P + j + 1], XG[:, j, :], BCOL[:, j:j + 1], start=True, stop=True)
                    ins.then_inc(c_sem["hc"], 1)

                def outs():
                    have(pe, c_sem["xh"], g + 1)
                    have(pe, c_sem["wb"], g + 1)
                    for j in range(GB):
                        o = PS[:, 5, j * D:(j + 1) * D]
                        pe.matmul(o, XGT[:, j * P:(j + 1) * P], WB[:, j, :], start=True, stop=False)
                        pe.matmul(o, HQ[:, j * P:(j + 1) * P], wqv[:, 1, :], start=False, stop=False)
                        ins = pe.matmul(o, XH[:, j * P:(j + 1) * P], wqv[:, 2, :], start=False, stop=True)
                    ins.then_inc(c_sem["o"], 1)

                def ct():
                    have(pe, r_sem[1]["cs"], g + 1)
                    if not is_last(g):
                        have(pe, c_sem["bc"], g + 2)
                    for j in range(GB):
                        ins = pe.transpose(PS[:, 5, :].bitcast(BF16)[:, j * P:(j + 1) * P], CS[:, j, :], identb[:])
                    ins.then_inc(r_sem[1]["ct"], 1)

                r = (23, 24, 28) if is_last(g) else (27, 28, 35)
                return by_chunk((9, t), (11, sims), (12, bts), (16, ats), (16, bbts), (17, hqs), (18, hcs), (20, outs),
                                (r[0], lambda: turn_tokens(1, g)), (r[1], lambda: logits(1, g, 0)), (r[2], ct))

            pe.wait_ge(wqv_in, 16)
            mixtures(pe, chunks, by_chunk(*((c, turn(t)) for t, c in enumerate(TURN_AT))), matching)
            last_base = (G - 1) * NCH[1] + OFF[1][0]
            for k in range(NCH[1] - LAG, NCH[1]):
                down(1, G - 1, last_base, k, 2 * G - 1)
            turn_out(2 * G)


_INS = ['x', 'ctx_1024', 'g_xattn', 'g_ffn', 'L0_xattn_Wq', 'L0_xattn_bq', 'L0_xattn_Wk', 'L0_xattn_bk', 'L0_xattn_Wv',
        'L0_xattn_bv', 'L0_xattn_Wo', 'L0_xattn_bo', 'L0_ffn_norm1_w', 'L0_ffn_norm2_w', 'L0_ffn_wq', 'L0_ffn_wk',
        'L0_ffn_wv', 'L0_ffn_wo', 'L0_ffn_router_w', 'L0_ffn_sh_gate', 'L0_ffn_sh_up', 'L0_ffn_sh_down', 'L0_ffn_e_gate',
        'L0_ffn_e_up', 'L0_ffn_e_down', 'L1_xattn_w_sim', 'L1_xattn_b_sim', 'L1_xattn_W_qv', 'L1_xattn_b_qv', 'L1_ffn_Wg',
        'L1_ffn_We_gate', 'L1_ffn_We_up', 'L1_ffn_We_down', 'L1_ffn_Ws_gate', 'L1_ffn_Ws_up', 'L1_ffn_Ws_down', 'L1_ffn_Wsg']


def kernel(**inputs):
    import numpy as _np
    import concourse.bacc as _bacc
    from concourse import mybir as _mybir
    from concourse.bass_utils import run_bass_kernel_spmd as _run

    nc = _bacc.Bacc("TRN2", target_bir_lowering=False, num_devices=1)
    arrays, args = {}, {}
    for name in _INS:
        v = _np.ascontiguousarray(inputs[name])
        arrays[f"in_{name}_dram"] = v
        args[name] = nc.dram_tensor(f"in_{name}_dram", v.shape, _mybir.dt.from_np(v.dtype), kind="ExternalInput").ap()
    out = nc.dram_tensor("out_0_dram", (B, P, D), _mybir.dt.float32, kind="ExternalOutput").ap()
    build(nc, args, out)
    r = _run(nc, [arrays], core_ids=[0])
    return r.results[0]["out_0_dram"]
```

```python
from contextlib import ExitStack

import concourse.bass as bass
from concourse import mybir

F32 = mybir.dt.float32
BF16 = mybir.dt.bfloat16
F32R = mybir.dt.float32r
I32 = mybir.dt.int32
U32 = mybir.dt.uint32
ALU = mybir.AluOpType
ACT = mybir.ActivationFunctionType
AX = mybir.AxisListType

P = 128
B = 16
D = 128
H = 16
DH = D // H
TC = 77
L = TC // H
NK = L * H
G = 4
GB = B // G
GT = GB * P
SCALE = float(DH) ** -0.5
LN_EPS = 1e-5
RMS_EPS = 1e-6
RSQRT_SEED = float(0x5F3759DF)
SLOT = 64
VW = 9
PV_N = 96
VA_W = VW * (H - 1) + PV_N
E0, F0 = 8, 256
E1, F1 = 16, 64
KINDS = ("gate", "up", "down")
PIECE = 32
LAG = 3


def build(nc, a, out):
    NC0 = E0 * F0 // P
    NC1 = E1 * F1 // P
    TURNS = [(0, 4), (4, 8), (8, 10)]
    TURN_AT = [2, 3, 4, 5, 6, 7, 12, 13, 14, 15]
    TB, RB, LB = (5, 7), ((0, 7), (5, 5)), (1, 5)
    MOE = [dict(n=NC0, s=2, per=F0 // P), dict(n=NC1, s=2, per=1)]
    NCH, NSC, NBC = (NC0 + 2, NC1 + 2), (NC0, NC1 + 2), (E0, NC1 + 1)
    OFF = [(0, 0, 0), (G * NCH[0], G * NSC[0], G * NBC[0])]

    with ExitStack() as ctx:
        def sb(name, shape, dt=F32):
            return ctx.enter_context(nc.sbuf_tensor(name, shape, dt))

        def sem(name):
            return ctx.enter_context(nc.semaphore(name))

        PS = ctx.enter_context(nc.psum_tensor("PS", [P, 8, 512], F32))

        X = sb("X", [P, B, D])
        Z = sb("Z", [P, B, D])
        ctx_nat = sb("ctx_nat", [TC, B, D])
        ctx_t = sb("ctx_t", [P, B, TC])
        stats = sb("stats", [P, B, 6])
        mean, var, rstd, nmr, r2 = (sb(n, [P, B]) for n in ("mean", "var", "rstd", "nmr", "r2"))
        t_a, t_b, t_c = (sb(n, [P, B]) for n in ("t_a", "t_b", "t_c"))
        identf = sb("identf", [P, P])
        identb = sb("identb", [P, P], BF16)
        hmask = sb("hmask", [P, H])
        gates = sb("gates", [P, 4])
        tg = sb("tg", [P, 4])
        bq_c, bk_c, bv_c, n1w, n2w, w1_c, w2s, w3s = (
            sb(n, [P, 1]) for n in ("bq_c", "bk_c", "bv_c", "n1w", "n2w", "w1_c", "w2s", "w3s"))
        bo_r = sb("bo_r", [P, D])
        bqv_r = sb("bqv_r", [P, D])
        tgb = sb("tgb", [P, D])
        bsim_c = sb("bsim_c", [P, 1])
        wqv = sb("wqv", [P, 4, D])
        wr0 = sb("wr0", [P, E0])
        wr1_nat = sb("wr1_nat", [E1 + 1, D])
        wr1 = sb("wr1", [P, E1 + 1])
        raw = [sb(f"raw{k}", [P, NC0 + 2, P]) for k in range(2)]
        W0H = [sb(f"W0H_{k}", [P, NC0 + 2, P], F32R) for k in KINDS]
        W0L = [sb(f"W0L_{k}", [P, NC0 + 2, P], F32R) for k in KINDS]
        XG = sb("XG", [P, GB, D])
        XGT = sb("XGT", [P, GT])
        HG1 = sb("HG1", [P, GB, D])
        work = [sb(f"work{k}", [P, GT]) for k in range(6)]
        gstats = sb("gstats", [P, 2 * GB, 6])
        grstd, gnmr = sb("grstd", [P, 2 * GB]), sb("gnmr", [P, 2 * GB])
        LG = sb("LG", [P, B, E1 + 1])
        PR = sb("PR", [P, B, E1])
        top = sb("top", [P, B, 8])
        topi = sb("topi", [P, B, 8], U32)
        topf = sb("topf", [P, B, 2])
        iota_i = sb("iota_i", [P, E1], I32)
        iota_e = sb("iota_e", [P, E1])
        wsel = sb("wsel", [P, B, 2])
        comb = sb("comb", [P, B, E1 + 1])
        combt = sb("combt", [P, B, E1 + 1])
        CS = sb("CS", [P, B, P], BF16)
        sel0 = sb("sel0", [P, E0, P], BF16)
        sel1 = sb("sel1", [P, NC1 + 1, P], BF16)
        SEL = [sel0, sel1]
        nmx, suma, rca, bt = (sb(n, [P, GB]) for n in ("nmx", "suma", "rca", "bt"))
        BB = sb("BB", [P, P])
        bm, bs = sb("bm", [GB, 1]), sb("bs", [GB, 2])
        BCOL = sb("BCOL", [P, GB])
        HC = sb("HC", [P, GB])
        pad = sb("pad", [P, 1])

        with ExitStack() as early:
            def sbe(name, shape, dt=F32):
                return early.enter_context(nc.sbuf_tensor(name, shape, dt))

            w_nat = sbe("w_nat", [P, 4, D])
            w_t = sbe("w_t", [P, 4, D])
            QA = work[0]
            KA4 = sbe("KA4", [P, GB, NK])
            VA4 = sbe("VA4", [P, GB, NK])
            V2 = work[1][:, 0:2 * D].rearrange("p (b d) -> p b d", b=2)
            mxA = sbe("mxA", [P, GB, H])
            PA = sbe("PA", [P, GB, L, H])
            PAT = work[2][:, 0:2 * P]
            wqkv = sbe("wqkv", [P, 3 * D])
            wo = sbe("wo", [P, D])
            XNB = [sbe(f"XNB{u}", [P, D]) for u in range(2)]
            XNT = [sbe(f"XNT{u}", [P, D]) for u in range(2)]
            T32 = sbe("T32", [P, 2, D])
            QS = [sbe(f"QS{u}", [P, H, SLOT], BF16) for u in range(2)]
            KS = [sbe(f"KS{u}", [P, H, SLOT], BF16) for u in range(2)]
            KT = [[sbe(f"KT{u}{v}", [P, H // 2, P], BF16) for v in range(2)] for u in range(2)]
            QT = sbe("QT", [P, H // 2, P], BF16)
            QM = [sbe(f"QM{u}", [P, H // 2, P], BF16) for u in range(2)]
            nmax = sbe("nmax", [P, H])
            EX = work[3:5]
            VA = sbe("VA", [P, B, VA_W])[:]
            rden = sbe("rden", [P, H])
            CN = sbe("CN", [P, H, DH])
            CT = sbe("CT", [P, D])

        H2H = sb("H2H", [P, B * P], F32R)
        H2L = sb("H2L", [P, B * P], F32R)
        CWT = sb("CWT", [P, B * P], BF16)
        W1H = [sb(f"W1H_{k}", [P, NC1 + 2, P], F32R) for k in KINDS]
        W1L = [sb(f"W1L_{k}", [P, NC1 + 2, P], F32R) for k in KINDS]
        WH, WL = [W0H, W1H], [W0L, W1L]
        BC, SG, HH = work[0:2], work[2:4], work[4:6]
        HHI = [sb(f"HHI{u}", [P, GT], F32R) for u in range(LAG)]
        HLO = [sb(f"HLO{u}", [P, GT], F32R) for u in range(LAG)]
        YT = sb("YT", [P, GT])
        spare = [raw[k][:, c:c + GB, :].rearrange("p c d -> p (c d)") for k, c in ((0, NC1 + 2), (0, NC1 + 6), (1, NC1 + 2), (1, NC1 + 6))]
        HG, HT = ((XG, HG1), (HG1, HG1)), ((XGT, spare[3]), (spare[3], spare[3]))
        HQ, AMT, CG = spare[0], spare[1][0:TC], spare[2][0:TC].rearrange("p (b d) -> p b d", b=GB)
        E3T = sb("E3T", [P, GT])
        XH = E3T
        AMW = sb("AMW", [P, GT])
        AM = AMW[:, 0:GB * TC].rearrange("p (b t) -> p b t", b=GB)
        WB = AMW[:].rearrange("p (b d) -> p b d", b=GB)

        at_one = {"pe": [], "act": [], "dve": [], "pool": []}

        def stage(name, **by):
            made = {}
            for eng, names in by.items():
                for n in names.split():
                    made[n] = sem(f"{name}_{n}")
                    at_one[eng].append(made[n])
            return made

        x_in, ctx_in, small_in, wa_in, wb_in, wr_in, wqv_in = (
            sem(n) for n in ("x_in", "ctx_in", "small_in", "wa_in", "wb_in", "wr_in", "wqv_in"))
        raw_in = [sem(f"raw_in{k}") for k in range(6)]
        halved = sem("halved")
        turn_ps, turn_hi, turn_lo = sem("turn_ps"), sem("turn_hi"), sem("turn_lo")
        consts, pool_c, dve_c = sem("consts"), sem("pool_c"), sem("dve_c")
        tg_ready, pre_ps, pre_sb = sem("tg_ready"), sem("pre_ps"), sem("pre_sb")
        out_done = sem("out_done")
        a_sem = stage("a", pe="t kv v2 s pt y", act="xt e pt_sb", dve="xn qkv_sb v2_sb d p x")
        a_chain = sem("a_chain")
        b_sem = stage("b", pe="t qkv k_t q_t s qm_t st pv ct wo", act="xt h q_sb qm_sb exp ct_sb",
                      dve="xn t32 v split k_sb max m norm z zs", pool="z0")
        b_chain = sem("b_chain")
        r_sem = [stage(f"r{m}", pe="t lg ct", act="ht ct_sb", dve="h e1 e2 cs", pool="low") for m in range(2)]
        r_chain = [sem(f"r{m}_chain") for m in range(2)]
        m_sem = stage("m", pe="bc g u down yn", act="bc_sb silu hi yt", dve="hid lo yx x st", pool="scaled")
        c_sem = stage("c", pe="t s bt at bbt hq hc o", act="xt exp bexp at_sb hq_sb",
                      dve="xn e3 mx a bb bc hcr xh wb xu x", pool="cg xb")
        c_chain = sem("c_chain")
        ln_chain, m_ln = sem("ln_chain"), sem("m_ln")

        block = ctx.enter_context(nc.Block())

        def turn_of(m, g, c):
            assert NCH[0] % LAG == 0
            return (c if m == 0 else g * NCH[1] + c) % LAG

        def first_of_expert(m, c):
            return c % MOE[m]["per"] == 0 if c < MOE[m]["n"] else (m == 1 and c == MOE[m]["n"])

        def mixtures(eng, chunks, first_steps, matching):
            n0, n1 = NCH

            def pick(*parts):
                return {c: [f for steps, lo, hi in parts if lo + c < hi for f in steps.get(lo + c, ())] for c in range(n0)}

            chunks(0, 0, first_steps)
            chunks(0, 1, pick((matching(0), 0, n0)))
            with eng.Fori(0, G - 2) as i:
                chunks(0, i + 2, pick((matching(i), n0, 2 * n0), (matching(i + 1), 0, n0)))
            before, last = matching(G - 2), matching(G - 1)
            chunks(1, 0, pick((before, n0, n0 + n1), (last, 0, n1)))
            chunks(1, 1, pick((before, n0 + n1, 2 * n0), (last, n1, 2 * n1)))
            chunks(1, 2, pick((last, 2 * n1, 3 * n1)))
            chunks(1, 3, {})

        def side(m, g):
            return g % 2 if m == 0 else 0

        def is_last(g):
            return isinstance(g, int) and g == G - 1

        def by_chunk(*steps):
            made = {}
            for c, f in steps:
                made.setdefault(c, []).append(f)
            return made

        def row(ap, n):
            return ap.rearrange("(a n) -> a n", a=1).broadcast_to([n, ap.shape[0]])

        def col(ap):
            return ap.rearrange("(n a) -> n a", a=1)

        @block.sync
        def _(sp):
            sp.dma_start(X[:], a["x"].rearrange("b s d -> s b d")).then_inc(x_in, 16)
            sp.dma_start(ctx_nat[:], a["ctx_1024"].rearrange("b s d -> s b d")).then_inc(ctx_in, 16)
            for i, n in enumerate(("Wq", "Wk", "Wv", "Wo")):
                sp.dma_start(w_nat[:, i, :], a["L0_xattn_" + n]).then_inc(wa_in, 16)
            for i, n in enumerate(("wq", "wk", "wv")):
                sp.dma_start(wqkv[:, i * D:(i + 1) * D], a["L0_ffn_" + n]).then_inc(wb_in, 16)
            sp.dma_start(wo[:], a["L0_ffn_wo"]).then_inc(wb_in, 16)
            sp.dma_start(wr0[:], a["L0_ffn_router_w"]).then_inc(wr_in, 16)
            for k, n in enumerate(KINDS):
                r = raw[k % 2]
                if k == 2:
                    sp.wait_ge(halved, 1)
                if n == "down":
                    sp.dma_start(r[:, 0:NC0, :], a["L0_ffn_e_down"].rearrange("e (c f) d -> f (e c) d", c=F0 // P)).then_inc(raw_in[k], 16)
                    sp.dma_start(r[:, NC0:NC0 + 2, :], a["L0_ffn_sh_down"].rearrange("(c f) d -> f c d", f=P)).then_inc(raw_in[k], 16)
                else:
                    sp.dma_start(r[:, 0:NC0, :].rearrange("d (e f) c -> d e (f c)", e=E0),
                                 a["L0_ffn_e_" + n].rearrange("e d f -> d e f")).then_inc(raw_in[k], 16)
                    sp.dma_start(r[:, NC0:NC0 + 2, :].rearrange("d a c -> d (a c)"), a["L0_ffn_sh_" + n]).then_inc(raw_in[k], 16)
            sp.dma_start(wr1_nat[0:E1, :], a["L1_ffn_Wg"]).then_inc(wr_in, 16)
            sp.dma_start(wr1_nat[E1:E1 + 1, :], a["L1_ffn_Wsg"]).then_inc(wr_in, 16)
            sp.dma_start(wqv[:], a["L1_xattn_W_qv"].rearrange("(k d) n -> d k n", d=D)).then_inc(wqv_in, 16)
            for k, n in enumerate(KINDS):
                r = raw[(k + 1) % 2]
                if k < 2:
                    sp.wait_ge(halved, k + 2)
                else:
                    sp.wait_ge(turn_ps, 3)
                if n == "down":
                    sp.dma_start(r[:, 0:NC1, :].rearrange("d c (a f) -> d (c a) f", a=2),
                                 a["L1_ffn_We_down"].rearrange("e d f -> d e f")).then_inc(raw_in[3 + k], 16)
                    sp.dma_start(r[:, NC1:NC1 + 2, :].rearrange("d a f -> d (a f)"), a["L1_ffn_Ws_down"]).then_inc(raw_in[3 + k], 16)
                else:
                    sp.dma_start(r[:, 0:NC1, :], a[f"L1_ffn_We_{n}"].rearrange("(c a) f d -> (a f) c d", a=2)).then_inc(raw_in[3 + k], 16)
                    sp.dma_start(r[:, NC1:NC1 + 2, :], a[f"L1_ffn_Ws_{n}"].rearrange("(c f) d -> f c d", f=P)).then_inc(raw_in[3 + k], 16)
            for g in range(G):
                sp.wait_ge(m_sem["x"], G + g + 2)
                sp.dma_start(out[g * GB:(g + 1) * GB].rearrange("b s d -> s b d"), X[:, g * GB:(g + 1) * GB, :]).then_inc(out_done, 16)
            sp.wait_ge(out_done, 16 * G)

        @block.gpsimd
        def _(pool):
            for s in at_one["pool"]:
                pool.sem_inc(s, 1)
            n = [0]

            def step(ins):
                n[0] += 1
                ins.then_inc(pool_c, 1)
                pool.wait_ge(pool_c, n[0])

            step(pool.memset(identf[:], 0.0))
            step(pool.affine_select(out=identf[:], in_=identf[:], compare_op=ALU.not_equal, fill=1.0, base=0,
                                    pattern=[[-1, P]], channel_multiplier=1))
            step(pool.tensor_copy(identb[:], identf[:]))
            step(pool.memset(hmask[:], 1.0))
            step(pool.affine_select(out=hmask[:], in_=hmask[:], compare_op=ALU.is_ge, fill=0.0, base=0,
                                    pattern=[[-DH, H]], channel_multiplier=1))
            step(pool.affine_select(out=hmask[:], in_=hmask[:], compare_op=ALU.is_ge, fill=0.0, base=DH - 1,
                                    pattern=[[DH, H]], channel_multiplier=-1))
            pool.memset(VA, 1.0)
            pool.memset(BB[:], 0.0)
            for u in range(2):
                pool.memset(QS[u][:].bitcast(F32), 0.0)
                step(pool.memset(KS[u][:].bitcast(F32), 0.0))
                pool.memset(KS[u][:, :, 48:50], 1.0)
                pool.memset(KT[u][0][:].bitcast(F32), 0.0)
                pool.memset(KT[u][1][:].bitcast(F32), 0.0)
            step(pool.memset(CS[:].bitcast(F32), 0.0))
            pool.memset(bm[:], 0.0).then_inc(consts, 1)
            pool.iota(iota_i[:], pattern=[[1, E1]], base=0, channel_multiplier=0).then_inc(pool_c, 1)
            n[0] += 1
            pool.memset(sel0[:].bitcast(F32), 0.0)
            step(pool.memset(sel1[:].bitcast(F32), 0.0))
            step(pool.tensor_copy(iota_e[:], iota_i[:]))
            for p in range(3):
                step(pool.affine_select(out=sel0[:], in_=sel0[:], compare_op=ALU.not_equal, fill=1.0,
                                        base=-PIECE * p, pattern=[[-1, E0], [0, P]], channel_multiplier=1))
                step(pool.affine_select(out=sel1[:, 0:NC1, :].rearrange("p c (a f) -> p c a f", a=2),
                                        in_=sel1[:, 0:NC1, :].rearrange("p c (a f) -> p c a f", a=2),
                                        compare_op=ALU.not_equal, fill=1.0, base=-PIECE * p,
                                        pattern=[[-2, NC1], [-1, 2], [0, F1]], channel_multiplier=1))
                step(pool.affine_select(out=sel1[:, NC1, :], in_=sel1[:, NC1, :],
                                        compare_op=ALU.not_equal, fill=1.0, base=-PIECE * p - E1,
                                        pattern=[[0, P]], channel_multiplier=1))
            pool.memset(bm[:], 0.0).then_inc(consts, 1)
            for k in range(3):
                pool.wait_ge(raw_in[k], 32)
                step(pool.tensor_copy(W0H[k][:], raw[k % 2][:]))
                pool.tensor_tensor(W0L[k][:], raw[k % 2][:], W0H[k][:].bitcast(F32), ALU.subtract).then_inc(halved, 1)
            with pool.Fori(0, B // 2) as i:
                for u in range(2):
                    b = i * 2 + u
                    pool.wait_ge(b_sem["xn"], b + 2)
                    pool.tensor_copy(Z[:, b, :], XNB[u][:]).then_inc(b_sem["z0"], 1)

            def low_tokens(m, g):
                pool.wait_ge(r_sem[m]["ht"], g * 2 + 3)
                at = bass.ds(g * GT, GT)
                pool.tensor_tensor(H2L[:, at], HT[m][side(m, g)][:], H2H[:, at].bitcast(F32), ALU.subtract).then_inc(r_sem[m]["low"], 1)

            for g in range(G):
                low_tokens(0, g)

            def chunks(m, g, inserts):
                n, per = NCH[m], MOE[m]["per"]
                base = g * n + OFF[m][0]
                for c in range(n):
                    if c < NSC[m]:
                        e = min(c // per, (n - 2) // per)
                        pool.wait_ge(m_sem["silu"], base + c + 2)
                        pool.wait_ge(m_sem["bc_sb"], g * NBC[m] + OFF[m][2] + e + 2)
                        pool.tensor_tensor(SG[c % 2][:], SG[c % 2][:], BC[e % 2][:], ALU.mult).then_inc(m_sem["scaled"], 1)
                    for f in inserts.get(c, ()):
                        f()

            def matching(g):
                def context(j):
                    pool.wait_ge(c_sem["hq"], g + 1)
                    pool.tensor_copy(CG[:, j:j + 2, :], ctx_nat[:, bass.ds(g * GB + j, 2), :]).then_inc(c_sem["cg"], 1)

                def bias(j):
                    pool.wait_ge(c_sem["xn"], g + 2)
                    Xg = X[:, bass.ds(g * GB + j, 2), :]
                    pool.tensor_tensor(Xg, Xg, tgb[:].unsqueeze(1).broadcast_to([P, 2, D]), ALU.add).then_inc(c_sem["xb"], 1)

                return by_chunk((2, lambda: context(0)), (4, lambda: context(2)), (8, lambda: bias(0)), (10, lambda: bias(2)),
                                (23 if is_last(g) else 27, lambda: low_tokens(1, g)))

            mixtures(pool, chunks, {}, matching)

        @block.scalar
        def _(act):
            smalls = [(gates[:, 0:2], row(a["g_xattn"], P)), (gates[:, 2:4], row(a["g_ffn"], P)),
                      (bq_c[:], col(a["L0_xattn_bq"])), (bk_c[:], col(a["L0_xattn_bk"])), (bv_c[:], col(a["L0_xattn_bv"])),
                      (bo_r[:], row(a["L0_xattn_bo"], P)), (n1w[:], col(a["L0_ffn_norm1_w"])), (n2w[:], col(a["L0_ffn_norm2_w"])),
                      (w1_c[:], col(a["L1_xattn_w_sim"][0:D])), (w2s[:], col(a["L1_xattn_w_sim"][D:2 * D])),
                      (w3s[:], col(a["L1_xattn_w_sim"][2 * D:3 * D])), (bsim_c[:], row(a["L1_xattn_b_sim"], P)),
                      (bqv_r[:], row(a["L1_xattn_b_qv"], P))]
            for dst, src in smalls:
                act.dma_start(dst, src).then_inc(small_in, 16)
            for s in at_one["act"]:
                act.sem_inc(s, 1)
            act.wait_ge(small_in, 16 * len(smalls))
            act.activation(tg[:], gates[:], ACT.Tanh).then_inc(tg_ready, 1)
            act.wait_ge(pre_ps, 1)
            act.activation(w_t[:].rearrange("p a b -> p (a b)"), PS[:, 0, :], ACT.Copy).then_inc(pre_sb, 1)
            for k in range(4):
                act.wait_ge(pre_ps, 2 + k)
                act.activation(ctx_t[:, 4 * k:4 * k + 4, :], PS[:, 1 + k, 0:4 * TC].rearrange("p (a b) -> p a b", a=4),
                               ACT.Copy).then_inc(pre_sb, 1)

            def attention_in(g):
                act.wait_ge(a_sem["t"], g + 2)
                act.wait_ge(a_sem["kv"], g + 1)
                act.activation(XGT[:], PS[:, 0, :], ACT.Copy).then_inc(a_sem["xt"], 1)

            def attention_out(g):
                act.wait_ge(a_sem["d"], g + 2)
                act.activation(PA[:], PA[:], ACT.Exp, scale=SCALE).then_inc(a_sem["e"], 1)
                act.wait_ge(a_sem["pt"], g + 2)
                act.wait_ge(a_sem["y"], g + 1)
                act.activation(PAT, PS[:, 5, 0:2 * P], ACT.Copy).then_inc(a_sem["pt_sb"], 1)

            attention_in(0)
            with act.Fori(0, G - 1) as g:
                attention_in(g + 1)
                attention_out(g)
            attention_out(G - 1)

            def slot(s, u0):
                def batch(k):
                    return s + k, (u0 + k) % 2

                def ok(k):
                    return not isinstance(s, int) or 0 <= s + k < B

                def exp(k, j):
                    b, u = batch(k)
                    act.wait_ge(b_sem["st"], b * 4 + (j + 1) + 1)
                    if not (isinstance(b, int) and 4 * b + j < 2):
                        act.wait_ge(b_sem["pv"], b * 4 + (j - 1) + 1)
                    act.activation(EX[j % 2][:], PS[:, 2 + j % 2, :], ACT.Exp, scale=SCALE).then_inc(b_sem["exp"], 1)

                if ok(0):
                    exp(0, 1)
                    exp(0, 2)
                if ok(3):
                    b, u = batch(3)
                    act.wait_ge(b_sem["t"], b + 2)
                    act.activation(XNT[u][:], PS[:, 4, 3 * D:4 * D], ACT.Copy, scale=n1w[:]).then_inc(b_sem["xt"], 1)
                if ok(0):
                    exp(0, 3)
                if ok(1):
                    b, u = batch(1)
                    act.wait_ge(b_sem["qm_t"], b + 2)
                    act.activation(QM[u][:].rearrange("p c s -> p (c s)"), PS[:, 5, :].bitcast(BF16), ACT.Copy).then_inc(b_sem["qm_sb"], 1)
                if ok(2):
                    b, u = batch(2)
                    act.wait_ge(b_sem["q_t"], b + 2)
                    act.activation(QT[:].rearrange("p c s -> p (c s)"), PS[:, 5, :].bitcast(BF16), ACT.Copy).then_inc(b_sem["q_sb"], 1)
                if ok(0):
                    b, u = batch(0)
                    act.wait_ge(b_sem["ct"], b + 2)
                    act.activation(CT[:], PS[:, 7, 232:360], ACT.Copy).then_inc(b_sem["ct_sb"], 1)
                if ok(1):
                    exp(1, 0)
                if ok(3):
                    b, u = batch(3)
                    act.wait_ge(b_sem["t32"], b + 2)
                    if not (isinstance(b, int) and b < 2):
                        act.wait_ge(b_sem["qm_t"], b)
                    act.activation(QS[u][:, :, 0:24].rearrange("p h (c d) -> p h c d", c=3),
                                   T32[:, 0, :].rearrange("p (h d) -> p h d", h=H).unsqueeze(2).broadcast_to([P, H, 3, DH]),
                                   ACT.Copy).then_inc(b_sem["h"], 1)
                    act.activation(KS[u][:, :, 16:40].rearrange("p h (c d) -> p h c d", c=3),
                                   T32[:, 1, :].rearrange("p (h d) -> p h d", h=H).unsqueeze(2).broadcast_to([P, H, 3, DH]),
                                   ACT.Copy).then_inc(b_sem["h"], 1)

            for s in range(-4, 0):
                slot(s, s % 2)
            with act.Fori(0, (B - 4) // 2) as i:
                for u in range(2):
                    slot(i * 2 + u, u)
            for s in range(B - 4, B):
                slot(s, s % 2)

            def turned_tokens(m, g):
                R = r_sem[m]
                act.wait_ge(R["t"], g + 2)
                if m == 1:
                    act.wait_ge(R["lg"], g + 1)
                    act.wait_ge(R["low"], g + 1)
                elif g >= 2:
                    act.wait_ge(R["lg"], g)
                    act.wait_ge(R["low"], g)
                scale = {"scale": n2w[:]} if m == 0 else {}
                act.activation(HT[m][side(m, g)][:], PS[:, RB[m][side(m, g)], :], ACT.Copy, **scale).then_inc(R["ht"], 1)
                act.activation(H2H[:, bass.ds(g * GT, GT)], PS[:, RB[m][side(m, g)], :], ACT.Copy, **scale).then_inc(R["ht"], 1)

            R = r_sem[0]
            act.wait_ge(halved, 2)
            for g in range(G):
                turned_tokens(0, g)
            act.wait_ge(R["e1"], 2)
            act.activation(LG[:, :, 0:E0], LG[:, :, 0:E0], ACT.Exp).then_inc(R["e1"], 1)
            act.wait_ge(R["e2"], 2)
            act.activation(wsel[:, :, 1], wsel[:, :, 1], ACT.Exp).then_inc(R["e2"], 1)
            for k in range(2):
                act.wait_ge(R["ct"], k + 2)
                act.activation(CWT[:, k * 1024:(k + 1) * 1024], PS[:, 2 + k, :].bitcast(BF16), ACT.Copy).then_inc(R["ct_sb"], 1)

            S = m_sem

            def chunks(m, g, inserts):
                n, per = NCH[m], MOE[m]["per"]
                base = g * n + OFF[m][0]
                start = isinstance(g, int) and m == 0 and g == 0

                def leading(k):
                    act.wait_ge(S["hid"], base + k + 2)
                    if not (start and k < LAG):
                        act.wait_ge(S["down"], base + k - (LAG - 1) + 1)
                    act.activation(HHI[turn_of(m, g, k)][:], HH[k % 2][:], ACT.Copy).then_inc(S["hi"], 1)

                for c in range(n):
                    if first_of_expert(m, c):
                        e = c // per
                        act.wait_ge(S["bc"], g * NBC[m] + OFF[m][2] + e + 2)
                        act.wait_ge(S["scaled"], g * NSC[m] + OFF[m][1] + max((e - 1) * per, 0) + 1)
                        act.activation(BC[e % 2][:], PS[:, 4, :], ACT.Copy).then_inc(S["bc_sb"], 1)
                    if c == LAG and not start:
                        out_t(m, g)
                    act.wait_ge(S["g"], base + c + 2)
                    act.wait_ge(S["hid"], base + max(c - 1, 0) + 1)
                    act.activation(SG[c % 2][:], PS[:, c % 2, :], ACT.Silu).then_inc(S["silu"], 1)
                    if not (start and c == 0):
                        leading(c - 1)
                    for f in inserts.get(c, ()):
                        f()

            def out_t(m, g):
                q = g + m * G
                act.wait_ge(S["down"], g * NCH[m] + OFF[m][0] + 1)
                act.wait_ge(S["yn"], q)
                act.activation(YT[:], PS[:, 6, :], ACT.Copy).then_inc(S["yt"], 1)

            def turn(t):
                def go():
                    act.wait_ge(turn_ps, t + 1)
                    if t == 9:
                        act.activation(wr1[:], PS[:, TB[t % 2], 0:E1 + 1], ACT.Copy).then_inc(turn_hi, 1)
                    else:
                        c0, c1 = TURNS[t % 3]
                        act.activation(W1H[t // 3][:, c0:c1, :], PS[:, TB[t % 2], 0:(c1 - c0) * P].rearrange("p (c f) -> p c f", f=P),
                                       ACT.Copy).then_inc(turn_hi, 1)
                return go

            def matching(g):
                def xt():
                    act.wait_ge(c_sem["t"], g + 2)
                    act.wait_ge(c_sem["o"], g + 1)
                    act.activation(XGT[:], PS[:, 7, :], ACT.Copy).then_inc(c_sem["xt"], 1)

                def exps():
                    act.wait_ge(c_sem["mx"], g + 2)
                    for j in range(GB):
                        act.activation(AM[:, j, :], PS[:, 7, j * TC:(j + 1) * TC], ACT.Exp, bias=nmx[:, j:j + 1],
                                       accum_out=suma[:, j:j + 1]).then_inc(c_sem["exp"], 1)

                def bexp():
                    act.wait_ge(c_sem["bt"], g * 2 + 3)
                    act.activation(BB[0:GB, :], PS[0:GB, 5, 0:P], ACT.Exp, bias=bm[:], accum_out=bs[:, 0:1]).then_inc(c_sem["bexp"], 1)

                def at_sb():
                    act.wait_ge(c_sem["at"], g + 2)
                    act.activation(AMT, PS[0:TC, 7, :], ACT.Copy).then_inc(c_sem["at_sb"], 1)

                def hq_sb():
                    act.wait_ge(c_sem["hq"], g + 2)
                    act.activation(HQ, PS[:, 7, :], ACT.Copy).then_inc(c_sem["hq_sb"], 1)

                def rexp():
                    act.wait_ge(r_sem[1]["e1"], g * 2 + 2)
                    act.activation(LG[:, 0:GB, :], LG[:, 0:GB, :], ACT.Exp).then_inc(r_sem[1]["e1"], 1)

                def ct_sb():
                    act.wait_ge(r_sem[1]["ct"], g + 2)
                    act.activation(CWT[:, bass.ds(g * GT, GT)], PS[:, 5, 0:GT // 2].bitcast(BF16), ACT.Copy).then_inc(r_sem[1]["ct_sb"], 1)

                r = (23, 25, 28) if is_last(g) else (27, 31, 35)
                return by_chunk((9, xt), (13, exps), (13, bexp), (16, at_sb), (17, hq_sb), (r[0], lambda: turned_tokens(1, g)),
                                (r[1], rexp), (r[2], ct_sb))

            mixtures(act, chunks, by_chunk(*((c, turn(t)) for t, c in enumerate(TURN_AT))), matching)
            every = G * NCH[1] + OFF[1][0]
            act.wait_ge(S["hid"], every + 1)
            act.wait_ge(S["down"], every - LAG + 1)
            act.activation(HHI[(every - 1) % LAG][:], HH[1][:], ACT.Copy).then_inc(S["hi"], 1)
            out_t(1, G)

        @block.vector
        def _(dve):
            class Chain:

                def __init__(self, s, per):
                    self.s, self.per, self.k, self.base = s, per, 0, 0

                def begin(self, i):
                    self.base, self.k = i * self.per, 0

                def __call__(self, ins, behind=0):
                    self.k += 1
                    ins.then_inc(self.s, 1)
                    if self.k > behind:
                        dve.wait_ge(self.s, self.base + self.k - behind)

                def end(self):
                    assert self.k == self.per, (self.k, self.per)

            def take_wait():
                dve.memset(pad[:], 0.0)

            lnc = Chain(ln_chain, 0)

            def first(t, n):
                return t[:, 0:n]

            def rsqrt(dst, src, eps, chain=lnc, n=B):
                ta, tb = first(t_a, n), first(t_b, n)
                chain(dve.tensor_scalar(ta, src, eps, None, ALU.add))
                chain(dve.tensor_scalar(dst.bitcast(I32), ta.bitcast(I32), -0.5, RSQRT_SEED, ALU.mult, ALU.add))
                for _ in range(3):
                    chain(dve.scalar_tensor_tensor(out=tb, in0=dst, scalar=-0.5, in1=dst, op0=ALU.mult, op1=ALU.mult))
                    chain(dve.tensor_tensor(tb, tb, ta, ALU.mult))
                    chain(dve.scalar_tensor_tensor(out=dst, in0=tb, scalar=1.5, in1=dst, op0=ALU.add, op1=ALU.mult))

            def moments(st=stats, chain=lnc, n=B):
                ta, tb, tc, mn, vr = (first(t, n) for t in (t_a, t_b, t_c, mean, var))
                chain(dve.tensor_tensor(ta, st[:, :, 1], st[:, :, 4], ALU.add))
                chain(dve.tensor_scalar(mn, ta, 0.5, None, ALU.mult))
                chain(dve.tensor_tensor(tb, st[:, :, 1], st[:, :, 4], ALU.subtract))
                chain(dve.scalar_tensor_tensor(out=tc, in0=tb, scalar=0.25, in1=tb, op0=ALU.mult, op1=ALU.mult))
                chain(dve.tensor_tensor(ta, st[:, :, 2], st[:, :, 5], ALU.add))
                chain(dve.scalar_tensor_tensor(out=vr, in0=ta, scalar=1.0 / D, in1=tc, op0=ALU.mult, op1=ALU.add))

            def scales(rs=rstd, nm=nmr, chain=lnc, n=B):
                rsqrt(rs[:], first(var, n), LN_EPS, chain, n)
                chain(dve.scalar_tensor_tensor(out=nm[:], in0=first(mean, n), scalar=-1.0, in1=rs[:], op0=ALU.mult, op1=ALU.mult))

            def normalise(dst, b):
                return dve.tensor_scalar(dst, X[:, b, :], rstd[:, bass.ds(b, 1)], nmr[:, bass.ds(b, 1)], ALU.mult, ALU.add)

            for s in at_one["dve"]:
                dve.sem_inc(s, 1)
            dve.wait_ge(x_in, 16)
            with dve.Fori(0, B) as b:
                dve.bn_stats(stats[:, b, :], X[:, b, :]).then_inc(dve_c, 1)
            dve.wait_ge(dve_c, B)
            moments()
            scales()
            dve.wait_ge(small_in, 16 * 13)
            lnc(dve.tensor_scalar(bo_r[:], bo_r[:], 1.0 / H, None, ALU.mult))
            dve.wait_ge(tg_ready, 1)
            lnc(dve.tensor_scalar(tgb[:], bqv_r[:], tg[:, 1:2], None, ALU.mult))
            dve.wait_ge(consts, 1)

            A = Chain(a_chain, 4)

            def norm(g):
                dve.wait_ge(a_sem["t"], g + 1)
                for j in range(GB):
                    ins = normalise(XG[:, j, :], g * GB + j)
                ins.then_inc(a_sem["xn"], 1)

            def queries_keys_values(g):
                dve.wait_ge(a_sem["kv"], g + 2)
                dve.wait_ge(a_sem["s"], g + 1)
                dve.wait_ge(a_sem["v2"], g + 1)
                dve.tensor_scalar(QA[:], PS[:, 1, :], bq_c[:], None, ALU.add)
                mask = hmask[:].unsqueeze(1).broadcast_to([P, GB * L, H])
                for dst, off, bias in ((KA4, 0, bk_c), (VA4, GB * NK, bv_c)):
                    ins = dve.scalar_tensor_tensor(
                        out=dst[:].rearrange("p b (l h) -> p (b l) h", h=H),
                        in0=PS[:, 2, off:off + GB * NK].rearrange("p (a h) -> p a h", h=H),
                        scalar=bias[:], in1=mask, op0=ALU.add, op1=ALU.mult)
                ins.then_inc(a_sem["qkv_sb"], 1)

            def values_out(g):
                dve.wait_ge(a_sem["v2"], g + 2)
                dve.wait_ge(a_sem["y"], g + 1)
                dve.tensor_tensor(V2, PS[:, 3, 0:2 * D].rearrange("p (b d) -> p b d", b=2),
                                  bo_r[:].unsqueeze(1).broadcast_to([P, 2, D]), ALU.add).then_inc(a_sem["v2_sb"], 1)

            def less_row_maximum(g):
                A.begin(g)
                dve.wait_ge(a_sem["s"], g + 2)
                S4 = PS[:, 4, 0:GB * NK]
                A(dve.tensor_reduce(mxA[:], S4.rearrange("p (b l h) -> p b h l", b=GB, h=H), AX.X, ALU.max))
                dve.wait_ge(a_sem["pt"], g + 1)
                dve.tensor_tensor(PA[:], S4.rearrange("p (b l h) -> p b l h", b=GB, h=H),
                                  mxA[:].unsqueeze(2).broadcast_to([P, GB, L, H]), ALU.subtract).then_inc(a_sem["d"], 1)

            def probabilities(g):
                dve.wait_ge(a_sem["e"], g + 2)
                A(dve.tensor_reduce(mxA[:], PA[:].rearrange("p b l h -> p b h l"), AX.X, ALU.add))
                A(dve.reciprocal(mxA[:], mxA[:]))
                dve.tensor_tensor(PA[:], PA[:], mxA[:].unsqueeze(2).broadcast_to([P, GB, L, H]), ALU.mult).then_inc(a_sem["p"], 1)

            def attended(g):
                dve.wait_ge(a_sem["y"], g + 2)
                Xg = X[:, bass.ds(g * GB, GB), :]
                for u in range(2):
                    Xu = Xg.rearrange("p (k u) d -> p k u d", u=2)[:, :, u, :]
                    ins = dve.scalar_tensor_tensor(out=Xu, in0=PS[:, 6 + u, 0:2 * D].rearrange("p (b d) -> p b d", b=2),
                                                   scalar=tg[:, 0:1], in1=Xu, op0=ALU.mult, op1=ALU.add)
                A(ins)
                for j in range(GB):
                    ins = dve.bn_stats(stats[:, g * GB + j, :], X[:, g * GB + j, :])
                ins.then_inc(a_sem["x"], 1)
                A.end()

            norm(0)
            queries_keys_values(0)
            values_out(0)
            with dve.Fori(0, G - 1) as g:
                norm(g + 1)
                less_row_maximum(g)
                probabilities(g)
                queries_keys_values(g + 1)
                attended(g)
                values_out(g + 1)
            less_row_maximum(G - 1)
            probabilities(G - 1)
            attended(G - 1)
            dve.wait_ge(a_sem["x"], G + 1)
            moments()
            scales()
            lnc(dve.tensor_tensor(t_a[:], rstd[:], rstd[:], ALU.mult))
            lnc(dve.tensor_tensor(t_c[:], t_a[:], var[:], ALU.mult))
            rsqrt(r2[:], t_c[:], RMS_EPS)

            PER = 6
            Bc = Chain(b_chain, PER)

            def slot(s, u0):
                def batch(k):
                    return s + k, (u0 + k) % 2

                def ok(k):
                    return not isinstance(s, int) or 0 <= s + k < B

                def rowmax(k, j):
                    b, u = batch(k)
                    dve.wait_ge(b_sem["s"], b * 4 + (j + 1) + 1)
                    dve.tensor_reduce(nmax[:, 4 * j:4 * j + 4], PS[:, j % 2, :].rearrange("p (h t) -> p h t", h=4),
                                      AX.X, ALU.max, negate=True).then_inc(b_sem["max"], 1)

                if ok(1):
                    rowmax(1, 1)
                    rowmax(1, 2)
                    rowmax(1, 3)
                    b, u = batch(1)
                    dve.wait_ge(b_sem["max"], b * 4 + 5)
                    dve.wait_ge(b_sem["q_t"], b + 2)
                    dve.tensor_copy(QS[u][:, :, 48], nmax[:]).then_inc(b_sem["m"], 1)
                    dve.wait_ge(b_sem["m"], b * 2 + 2)
                    dve.tensor_tensor(QS[u][:, :, 49], nmax[:], QS[u][:, :, 48], ALU.subtract).then_inc(b_sem["m"], 1)
                if ok(2):
                    b, u = batch(2)
                    Bc.begin(b)
                    dve.wait_ge(b_sem["h"], b * 2 + 3)
                    q, k = T32[:, 0, :].rearrange("p (h d) -> p h d", h=H), T32[:, 1, :].rearrange("p (h d) -> p h d", h=H)
                    Bc(dve.tensor_tensor(q, q, QS[u][:, :, 0:8], ALU.subtract), 1)
                    Bc(dve.tensor_tensor(k, k, KS[u][:, :, 16:24], ALU.subtract), 1)
                    Bc(dve.tensor_copy(QS[u][:, :, 32:48].rearrange("p h (c d) -> p h c d", c=2),
                                       q.unsqueeze(2).broadcast_to([P, H, 2, DH])), 1)
                    Bc(dve.tensor_copy(KS[u][:].rearrange("p h (c d) -> p h c d", c=2)[:, :, :, 8:16],
                                       k.unsqueeze(2).broadcast_to([P, H, 2, DH])), 1)
                    Bc(dve.memset(QS[u][:, :, 48:50], 0.0), 1)
                    Bc(dve.tensor_tensor(QS[u][:, :, 24:32], q, QS[u][:, :, 32:40], ALU.subtract), 1)
                    dve.tensor_tensor(KS[u][:, :, 0:8], k, KS[u][:, :, 8:16], ALU.subtract).then_inc(b_sem["split"], 1)
                    Bc.end()
                if ok(3):
                    b, u = batch(3)
                    dve.wait_ge(b_sem["qkv"], b + 2)
                    if not (isinstance(b, int) and b == 0):
                        dve.wait_ge(b_sem["split"], b + 1)
                    dve.tensor_scalar(T32[:], PS[:, 4, 0:2 * D].rearrange("p (a d) -> p a d", a=2), r2[:, bass.ds(b, 1)], None,
                                      ALU.mult).then_inc(b_sem["t32"], 1)
                    dve.tensor_scalar(VA[:, b, 0:VW * H].rearrange("p (h d) -> p h d", h=H)[:, :, 0:DH],
                                      PS[:, 4, 2 * D:3 * D].rearrange("p (h d) -> p h d", h=H), r2[:, bass.ds(b, 1)], None,
                                      ALU.mult).then_inc(b_sem["v"], 1)
                if ok(2):
                    b, u = batch(2)
                    dve.wait_ge(b_sem["k_t"], b + 2)
                    src = PS[:, 6, :].bitcast(BF16)
                    dve.tensor_copy(KT[u][0][0:64].rearrange("p c s -> p (c s)"), src[0:64, :])
                    dve.tensor_copy(KT[u][1][64:128].rearrange("p c s -> p (c s)"), src[64:128, :]).then_inc(b_sem["k_sb"], 1)
                if ok(0):
                    b, u = batch(0)
                    O = PS[:, 7, 0:VW * H].rearrange("p (h d) -> p h d", h=H)
                    dve.wait_ge(b_sem["pv"], b * 4 + 5)
                    dve.reciprocal(rden[:], O[:, :, DH]).then_inc(b_sem["norm"], 1)
                    dve.wait_ge(b_sem["norm"], b * 2 + 2)
                    dve.tensor_tensor(CN[:], O[:, :, 0:DH], rden[:].unsqueeze(2).broadcast_to([P, H, DH]),
                                      ALU.mult).then_inc(b_sem["norm"], 1)
                if ok(4):
                    b, u = batch(4)
                    if not (isinstance(b, int) and b < 2):
                        dve.wait_ge(b_sem["t"], b)
                        dve.wait_ge(b_sem["z0"], b)
                    normalise(XNB[u][:], b).then_inc(b_sem["xn"], 1)
                if ok(2):
                    rowmax(2, 0)
                if ok(0):
                    b, u = batch(0)
                    dve.wait_ge(b_sem["wo"], b + 2)
                    dve.wait_ge(b_sem["z0"], b + 2)
                    dve.tensor_tensor(Z[:, b, :], PS[:, 7, 360:488], Z[:, b, :], ALU.add).then_inc(b_sem["z"], 1)
                    dve.wait_ge(b_sem["z"], b + 2)
                    dve.bn_stats(stats[:, b, :], Z[:, b, :]).then_inc(b_sem["zs"], 1)

            for s in range(-4, 0):
                slot(s, s % 2)
            with dve.Fori(0, (B - 4) // 2) as i:
                for u in range(2):
                    slot(i * 2 + u, u)
            for s in range(B - 4, B):
                slot(s, s % 2)
            dve.wait_ge(b_sem["zs"], B + 1)
            moments()
            lnc(dve.tensor_tensor(t_c[:], mean[:], mean[:], ALU.mult))
            lnc(dve.tensor_tensor(t_c[:], t_c[:], var[:], ALU.add))
            rsqrt(r2[:], t_c[:], RMS_EPS)

            def less_maximum(m, C, nb):
                R, E = r_sem[m], (E0, E1)[m]
                EW = E + m
                LGb, LGm, tb = LG[:, 0:nb, 0:EW], LG[:, 0:nb, 0:E], first(t_b, nb)
                wide = tb.unsqueeze(2).broadcast_to([P, nb, E])
                C(dve.tensor_copy(LGb, PS[:, LB[m], 0:nb * EW].rearrange("p (b e) -> p b e", b=nb)))
                C(dve.tensor_reduce(tb, LGm, AX.X, ALU.max))
                if m == 1:
                    C(dve.tensor_scalar(LG[:, 0:nb, E1:E1 + 1], LG[:, 0:nb, E1:E1 + 1], -1.0, None, ALU.mult))
                dve.tensor_tensor(LGm, LGm, wide, ALU.subtract).then_inc(R["e1"], 1)

            def two_largest(m, g, C, nb):
                R, E = r_sem[m], (E0, E1)[m]
                EW = E + m
                LGm, PRm, tb = LG[:, 0:nb, 0:E], PR[:, 0:nb, 0:E], first(t_b, nb)
                wide = tb.unsqueeze(2).broadcast_to([P, nb, E])
                dve.wait_ge(R["e1"], g * 2 + 3)
                C(dve.tensor_reduce(tb, LGm, AX.X, ALU.add))
                C(dve.reciprocal(tb, tb))
                C(dve.tensor_tensor(PRm, LGm, wide, ALU.mult))
                take_wait()
                for b in range(nb):
                    ins = dve.max(top[:, b, :], PR[:, b, 0:E])
                C(ins)
                take_wait()
                for b in range(nb):
                    ins = dve.max_index(topi[:, b, :], top[:, b, :], PR[:, b, 0:E])
                C(ins)
                C(dve.tensor_copy(topf[:, 0:nb, :], topi[:, 0:nb, 0:2]))

            def weights_of_two(m, g, C, nb):
                R, E = r_sem[m], (E0, E1)[m]
                tb = first(t_b, nb)
                w0, w1, p0, p1 = wsel[:, 0:nb, 0], wsel[:, 0:nb, 1], top[:, 0:nb, 0], top[:, 0:nb, 1]
                if m == 0:
                    dve.tensor_tensor(w1, p1, p0, ALU.subtract).then_inc(R["e2"], 1)
                    dve.wait_ge(R["e2"], g * 2 + 3)
                    C(dve.tensor_scalar(tb, w1, 1.0, None, ALU.add))
                    C(dve.reciprocal(w0, tb))
                    C(dve.tensor_tensor(w1, w1, w0, ALU.mult))
                else:
                    C(dve.tensor_tensor(tb, p0, p1, ALU.add))
                    C(dve.reciprocal(tb, tb))
                    C(dve.tensor_tensor(w0, p0, tb, ALU.mult))
                    C(dve.tensor_tensor(w1, p1, tb, ALU.mult))
                dve.wait_ge(consts, 2)
                io = iota_e[:, 0:E].unsqueeze(1).broadcast_to([P, nb, E])
                cm, ct = comb[:, 0:nb, 0:E], combt[:, 0:nb, 0:E]
                C(dve.tensor_tensor(cm, io, topf[:, 0:nb, 0:1].broadcast_to([P, nb, E]), ALU.is_equal))
                C(dve.tensor_tensor(cm, cm, wsel[:, 0:nb, 0:1].broadcast_to([P, nb, E]), ALU.mult))
                C(dve.tensor_tensor(ct, io, topf[:, 0:nb, 1:2].broadcast_to([P, nb, E]), ALU.is_equal))
                C(dve.tensor_tensor(ct, ct, wsel[:, 0:nb, 1:2].broadcast_to([P, nb, E]), ALU.mult))
                C(dve.tensor_tensor(cm, cm, ct, ALU.add))

            def in_pieces(m, g, C, nb):
                R, E = r_sem[m], (E0, E1)[m]
                EW = E + m
                if m == 1:
                    sg = comb[:, 0:nb, E1:E1 + 1]
                    C(dve.tensor_scalar(sg, LG[:, 0:nb, E1:E1 + 1], 1.0, None, ALU.add))
                    C(dve.reciprocal(sg, sg))
                dve.wait_ge(R["ct"], g + 1)
                cf = comb[:, 0:nb, 0:EW]
                for p in range(3):
                    piece = CS[:, 0:nb, p * PIECE:p * PIECE + EW]
                    ins = dve.tensor_copy(piece, cf)
                    if p == 2:
                        ins.then_inc(R["cs"], 1)
                    else:
                        C(ins)
                        C(dve.tensor_tensor(cf, cf, piece, ALU.subtract))
                C.end()

            R = r_sem[0]
            for g in range(G):
                if g >= 2:
                    dve.wait_ge(R["t"], g)
                for j in range(GB):
                    b = g * GB + j
                    ins = dve.tensor_scalar(HG[0][g % 2][:, j, :], Z[:, b, :], r2[:, bass.ds(b, 1)], None, ALU.mult)
                ins.then_inc(R["h"], 1)
            dve.wait_ge(R["lg"], G + 1)
            C0 = Chain(r_chain[0], 20)
            C0.begin(0)
            less_maximum(0, C0, B)
            two_largest(0, 0, C0, B)
            weights_of_two(0, 0, C0, B)
            in_pieces(0, 0, C0, B)

            S = m_sem

            def chunks(m, g, inserts):
                n, per = NCH[m], MOE[m]["per"]
                base = g * n + OFF[m][0]
                start = isinstance(g, int) and m == 0 and g == 0

                def rest(k):
                    dve.wait_ge(S["hi"], base + k + 2)
                    if not (start and k < LAG):
                        dve.wait_ge(S["down"], base + k - (LAG - 1) + 1)
                    t = turn_of(m, g, k)
                    dve.tensor_tensor(HLO[t][:], HH[k % 2][:], HHI[t][:].bitcast(F32), ALU.subtract).then_inc(S["lo"], 1)

                for c in range(n):
                    dve.wait_ge(S["u"], base + c + 2)
                    if c < NSC[m]:
                        dve.wait_ge(S["scaled"], g * NSC[m] + OFF[m][1] + c + 2)
                    else:
                        dve.wait_ge(S["silu"], base + c + 2)
                    if not (start and c < 2):
                        dve.wait_ge(S["lo"], base + c)
                    dve.tensor_tensor(HH[c % 2][:], PS[:, 2 + c % 2, :], SG[c % 2][:], ALU.mult).then_inc(S["hid"], 1)
                    if not (start and c == 0):
                        rest(c - 1)
                    if c == LAG + 1 and not start:
                        residual(m, g)
                    for f in inserts.get(c, ()):
                        f()

            def ffn_input(g):
                Xg = X[:, g * GB:(g + 1) * GB, :]
                dve.scalar_tensor_tensor(out=Xg, in0=Z[:, g * GB:(g + 1) * GB, :], scalar=tg[:, 2:3], in1=Xg,
                                         op0=ALU.mult, op1=ALU.add).then_inc(S["yx"], 1)

            def residual(m, g):
                q = g + m * G
                of_first = m == 0 or (isinstance(g, int) and g == 0)
                dve.wait_ge(S["yn"], q + 1)
                dve.wait_ge(S["yx"], G + 1)
                at = (g - 1) * GB if not (m == 1 and of_first) else (G - 1) * GB
                Xg = X[:, bass.ds(at, GB), :]
                dve.scalar_tensor_tensor(out=Xg, in0=PS[:, 7, :].rearrange("p (b d) -> p b d", b=GB),
                                         scalar=tg[:, 2:3] if of_first else tg[:, 3:4], in1=Xg,
                                         op0=ALU.mult, op1=ALU.add).then_inc(S["x"], 1)
                if of_first:
                    dve.wait_ge(S["x"], q + 1)
                    take_wait()
                    for j in range(GB):
                        ins = dve.bn_stats(gstats[:, j, :], X[:, at + j, :])
                    ins.then_inc(S["st"], 1)

            def turn(t):
                def go():
                    dve.wait_ge(turn_hi, t + 1)
                    c0, c1 = TURNS[t % 3]
                    dve.tensor_tensor(W1L[t // 3][:, c0:c1, :], PS[:, TB[t % 2], 0:(c1 - c0) * P].rearrange("p (c f) -> p c f", f=P),
                                      W1H[t // 3][:, c0:c1, :].bitcast(F32), ALU.subtract).then_inc(turn_lo, 1)
                return go

            CC = Chain(c_chain, 3)
            G_LN = Chain(m_ln, 18)
            CR = Chain(r_chain[1], 24)

            def matching(g):
                def norm_group(dst, k, signal):
                    for j in range(GB):
                        ins = dve.tensor_scalar(dst[:, j, :], X[:, g * GB + j, :], grstd[:, k + j:k + j + 1], gnmr[:, k + j:k + j + 1],
                                                ALU.mult, ALU.add)
                    ins.then_inc(signal, 1)

                def norm_a(i=g):
                    dve.wait_ge(S["st"], 1 + (min(i + 1, G) if isinstance(i, int) else i + 1))
                    dve.wait_ge(c_sem["x"], i + 1)
                    G_LN.begin(i)
                    moments(gstats, G_LN, 2 * GB)

                def norm_b():
                    scales(grstd, gnmr, G_LN, 2 * GB)
                    G_LN.end()

                def xn():
                    dve.wait_ge(c_sem["hc"], g + 1)
                    norm_group(XG, 0, c_sem["xn"])

                def e3():
                    dve.wait_ge(c_sem["xt"], g + 2)
                    dve.wait_ge(c_sem["s"], g + 1)
                    dve.wait_ge(c_sem["o"], g + 1)
                    dve.tensor_scalar(E3T[:], XGT[:], w3s[:], w2s[:], ALU.mult, ALU.add).then_inc(c_sem["e3"], 1)

                def mx():
                    CC.begin(g)
                    dve.wait_ge(c_sem["s"], g + 2)
                    CC(dve.tensor_reduce(nmx[:], PS[:, 7, 0:GB * TC].rearrange("p (b t) -> p b t", b=GB), AX.X, ALU.max,
                                         negate=True))
                    dve.scalar_tensor_tensor(out=bt[:], in0=PS[:, 7, GB * TC:GB * TC + GB], scalar=bsim_c[:], in1=nmx[:],
                                             op0=ALU.add, op1=ALU.subtract).then_inc(c_sem["mx"], 1)

                def bmax():
                    dve.wait_ge(c_sem["bt"], g * 2 + 2)
                    dve.tensor_reduce(bm[:], PS[0:GB, 5, 0:P], AX.X, ALU.max, negate=True).then_inc(c_sem["bt"], 1)

                def soft():
                    dve.wait_ge(c_sem["exp"], g * GB + GB + 1)
                    CC(dve.reciprocal(rca[:], suma[:]))
                    dve.tensor_tensor(AM, AM, rca[:].unsqueeze(2).broadcast_to([P, GB, TC]), ALU.mult).then_inc(c_sem["a"], 1)
                    dve.wait_ge(c_sem["bexp"], g + 2)
                    CC(dve.reciprocal(bs[:, 1:2], bs[:, 0:1]))
                    dve.tensor_scalar(BB[0:GB, :], BB[0:GB, :], bs[:, 1:2], None, ALU.mult).then_inc(c_sem["bb"], 1)
                    CC.end()

                def bcol():
                    dve.wait_ge(c_sem["bbt"], g + 2)
                    dve.tensor_copy(BCOL[:], PS[:, 5, P:P + GB]).then_inc(c_sem["bc"], 1)

                def product():
                    dve.wait_ge(c_sem["hq_sb"], g + 2)
                    dve.tensor_tensor(XH[:], PS[:, 7, :], XGT[:], ALU.mult).then_inc(c_sem["xh"], 1)

                def weights():
                    dve.wait_ge(c_sem["hc"], g + 2)
                    dve.tensor_copy(HC[:], PS[:, 5, 2 * P:2 * P + GB]).then_inc(c_sem["hcr"], 1)
                    dve.wait_ge(c_sem["hcr"], g + 2)
                    for j in range(GB):
                        ins = dve.scalar_tensor_tensor(out=WB[:, j, :], in0=wqv[:, 3, :], scalar=HC[:, j:j + 1], in1=wqv[:, 0, :],
                                                       op0=ALU.mult, op1=ALU.add)
                    ins.then_inc(c_sem["wb"], 1)

                def update():
                    dve.wait_ge(c_sem["o"], g + 2)
                    dve.wait_ge(c_sem["xb"], g * 2 + 3)
                    Xg = X[:, bass.ds(g * GB, GB), :]
                    dve.scalar_tensor_tensor(out=Xg, in0=PS[:, 5, :].rearrange("p (b d) -> p b d", b=GB), scalar=tg[:, 1:2],
                                             in1=Xg, op0=ALU.mult, op1=ALU.add).then_inc(c_sem["xu"], 1)
                    dve.wait_ge(c_sem["xu"], g + 2)
                    take_wait()
                    for j in range(GB):
                        ins = dve.bn_stats(gstats[:, GB + j, :], X[:, g * GB + j, :])
                    ins.then_inc(c_sem["x"], 1)

                def hn():
                    norm_group(HG1, GB, r_sem[1]["h"])

                def route_a():
                    dve.wait_ge(r_sem[1]["lg"], g + 2)
                    CR.begin(g)
                    less_maximum(1, CR, GB)

                steps = [(5, norm_a), (6, norm_b), (7, xn), (9, e3), (11, mx), (12, bmax), (14, soft), (16, bcol), (18, product),
                         (18, weights), (20, update)]
                if is_last(g):
                    steps += [(21, lambda: norm_a(G)), (21, norm_b)]
                r = (22, 24, 25, 25, 26) if is_last(g) else (25, 28, 32, 33, 34)
                steps += [(r[0], hn), (r[1], route_a), (r[2], lambda: two_largest(1, g, CR, GB)),
                          (r[3], lambda: weights_of_two(1, g, CR, GB)), (r[4], lambda: in_pieces(1, g, CR, GB))]
                return by_chunk(*steps)

            dve.memset(gstats[:], 0.0)
            mixtures(dve, chunks, by_chunk(*((c, turn(t)) for t, c in enumerate(TURN_AT[:9])),
                                           *((8 + g, lambda g=g: ffn_input(g)) for g in range(G))), matching)
            every = G * NCH[1] + OFF[1][0]
            dve.wait_ge(S["hi"], every + 1)
            dve.wait_ge(S["down"], every - LAG + 1)
            t = (every - 1) % LAG
            dve.tensor_tensor(HLO[t][:], HH[1][:], HHI[t][:].bitcast(F32), ALU.subtract).then_inc(S["lo"], 1)
            residual(1, G)

        @block.tensor
        def _(pe):
            for s in at_one["pe"]:
                pe.sem_inc(s, 1)
            pe.wait_ge(consts, 1)
            pe.wait_ge(wa_in, 16 * 4)
            for i in range(4):
                ins = pe.transpose(PS[:, 0, i * D:(i + 1) * D], w_nat[:, i, :], identf[:])
            ins.then_inc(pre_ps, 1)
            pe.wait_ge(ctx_in, 16)
            for k in range(4):
                for j in range(4):
                    ins = pe.transpose(PS[:, 1 + k, j * TC:(j + 1) * TC], ctx_nat[:, 4 * k + j, :], identf[0:TC, 0:TC])
                ins.then_inc(pre_ps, 1)
            pe.wait_ge(pre_sb, 5)

            def turn_and_project(g):
                pe.wait_ge(a_sem["xn"], g + 2)
                pe.wait_ge(a_sem["xt"], g + 1)
                for j in range(GB):
                    ins = pe.transpose(PS[:, 0, j * P:(j + 1) * P], XG[:, j, :], identf[:])
                ins.then_inc(a_sem["t"], 1)
                pe.wait_ge(a_sem["xt"], g + 2)
                pe.wait_ge(a_sem["qkv_sb"], g + 1)
                pe.matmul(PS[:, 1, :], w_t[:, 0, :], XGT[:], start=True, stop=True)
                keys = ctx_t[:, bass.ds(g * GB, GB), 0:NK]
                pe.matmul(PS[:, 2, 0:GB * NK], w_t[:, 1, :], keys, start=True, stop=True)
                pe.matmul(PS[:, 2, GB * NK:2 * GB * NK], w_t[:, 2, :], keys, start=True, stop=True).then_inc(a_sem["kv"], 1)

            def project_values(g):
                pe.wait_ge(a_sem["qkv_sb"], g + 2)
                pe.wait_ge(a_sem["v2_sb"], g + 1)
                for j in range(2):
                    ins = pe.matmul(PS[:, 3, j * D:(j + 1) * D], VA4[:, 2 * j:2 * j + 2, :].rearrange("p b k -> p (b k)"), w_t[:, 3, :],
                                    start=True, stop=True)
                ins.then_inc(a_sem["v2"], 1)

            def strided_scores(g):
                pe.wait_ge(a_sem["qkv_sb"], g + 2)
                pe.wait_ge(a_sem["d"], g + 1)
                for j in range(GB):
                    ins = pe.matmul(PS[:, 4, j * NK:(j + 1) * NK], QA[:, j * P:(j + 1) * P], KA4[:, j, :], start=True, stop=True)
                ins.then_inc(a_sem["s"], 1)

            def turn_probabilities(g):
                pe.wait_ge(a_sem["p"], g + 2)
                pe.wait_ge(a_sem["pt_sb"], g + 1)
                for j in range(2):
                    ins = pe.transpose(PS[:, 5, j * P:(j + 1) * P], PA[:, 2 * j:2 * j + 2, :, :].rearrange("p b l h -> p (b l h)"),
                                       identf[:])
                ins.then_inc(a_sem["pt"], 1)

            def attend(g):
                pe.wait_ge(a_sem["pt_sb"], g + 2)
                pe.wait_ge(a_sem["v2_sb"], g + 2)
                pe.wait_ge(a_sem["x"], g + 1)
                for j in range(GB):
                    k, r = j // 2, slice(NK * (j % 2), NK * (j % 2 + 1))
                    ins = pe.matmul(PS[:, 6 + j % 2, k * D:(k + 1) * D], PAT[r, k * P:(k + 1) * P], V2[r, k, :], start=True, stop=True)
                ins.then_inc(a_sem["y"], 1)

            turn_and_project(0)
            project_values(0)
            with pe.Fori(0, G - 1) as g:
                strided_scores(g)
                turn_and_project(g + 1)
                turn_probabilities(g)
                attend(g)
                project_values(g + 1)
            strided_scores(G - 1)
            turn_probabilities(G - 1)
            attend(G - 1)

            pe.wait_ge(a_sem["x"], G + 1)
            pe.wait_ge(wb_in, 16 * 4)

            def slot(s, u0):
                def batch(k):
                    return s + k, (u0 + k) % 2

                def ok(k):
                    return not isinstance(s, int) or 0 <= s + k < B

                def scores(k, j):
                    b, u = batch(k)
                    if j == 0:
                        pe.wait_ge(b_sem["k_sb"], b + 2)
                        pe.wait_ge(b_sem["q_sb"], b + 2)
                    if not (isinstance(b, int) and 4 * b + j < 2):
                        pe.wait_ge(b_sem["max"], b * 4 + (j - 1) + 1)
                    for h in range(4 * j, 4 * j + 4):
                        ins = pe.matmul(PS[:, j % 2, (h % 4) * P:(h % 4 + 1) * P], QT[:, h // 2, :], KT[u][h % 2][:, h // 2, :],
                                        start=True, stop=True)
                    ins.then_inc(b_sem["s"], 1)

                def scores_t(k, j):
                    b, u = batch(k)
                    if j == 0:
                        pe.wait_ge(b_sem["qm_sb"], b + 2)
                    if not (isinstance(b, int) and 4 * b + j < 2):
                        pe.wait_ge(b_sem["exp"], b * 4 + (j - 1) + 1)
                    for h in range(4 * j, 4 * j + 4):
                        ins = pe.matmul(PS[:, 2 + j % 2, (h % 4) * P:(h % 4 + 1) * P], KT[u][h % 2][:, h // 2, :], QM[u][:, h // 2, :],
                                        start=True, stop=True)
                    ins.then_inc(b_sem["st"], 1)

                def values(j):
                    b, u = batch(0)
                    pe.wait_ge(b_sem["exp"], b * 4 + (j + 1) + 1)
                    if j == 0 and not (isinstance(b, int) and b == 0):
                        pe.wait_ge(b_sem["z"], b + 1)
                    for h in range(4 * j, 4 * j + 4):
                        ins = pe.matmul(PS[:, 7, VW * h:VW * h + PV_N], EX[j % 2][:, (h % 4) * P:(h % 4 + 1) * P],
                                        VA[:, b, VW * h:VW * h + PV_N], start=True, stop=True)
                    ins.then_inc(b_sem["pv"], 1)

                def turn(source, bank, signal):
                    for c in range(H // 2):
                        ins = pe.transpose(PS[:, bank, :].bitcast(BF16)[:, c * P:(c + 1) * P],
                                           source[:, 2 * c:2 * c + 2, :].rearrange("p h d -> p (h d)"), identb[:])
                    ins.then_inc(signal, 1)

                if ok(1):
                    scores(1, 2)
                if ok(0):
                    scores_t(0, 1)
                    values(0)
                if ok(3):
                    b, u = batch(3)
                    pe.wait_ge(b_sem["xn"], b + 2)
                    if not (isinstance(b, int) and b == 0):
                        pe.wait_ge(b_sem["xt"], b + 1)
                        pe.wait_ge(b_sem["v"], b + 1)
                    pe.transpose(PS[:, 4, 3 * D:4 * D], XNB[u][:], identf[:]).then_inc(b_sem["t"], 1)
                if ok(1):
                    scores(1, 3)
                if ok(0):
                    scores_t(0, 2)
                    values(1)
                if ok(3):
                    b, u = batch(3)
                    pe.wait_ge(b_sem["xt"], b + 2)
                    pe.matmul(PS[:, 4, 0:3 * D], XNT[u][:], wqkv[:], start=True, stop=True).then_inc(b_sem["qkv"], 1)
                if ok(0):
                    scores_t(0, 3)
                if ok(1):
                    b, u = batch(1)
                    pe.wait_ge(b_sem["m"], b * 2 + 3)
                    pe.wait_ge(b_sem["q_sb"], b + 2)
                    turn(QS[u], 5, b_sem["qm_t"])
                if ok(0):
                    values(2)
                if ok(2):
                    b, u = batch(2)
                    pe.wait_ge(b_sem["split"], b + 2)
                    if not (isinstance(b, int) and b == 0):
                        pe.wait_ge(b_sem["k_sb"], b + 1)
                    turn(KS[u], 6, b_sem["k_t"])
                    if not (isinstance(b, int) and b == 0):
                        pe.wait_ge(b_sem["qm_sb"], b + 1)
                    turn(QS[u], 5, b_sem["q_t"])
                if ok(0):
                    values(3)
                if ok(2):
                    scores(2, 0)
                    scores(2, 1)
                if ok(0):
                    b, u = batch(0)
                    pe.wait_ge(b_sem["norm"], b * 2 + 3)
                    pe.transpose(PS[:, 7, 232:360], CN[:].rearrange("p h d -> p (h d)"), identf[:]).then_inc(b_sem["ct"], 1)
                if ok(1):
                    scores_t(1, 0)
                if ok(0):
                    b, u = batch(0)
                    pe.wait_ge(b_sem["ct_sb"], b + 2)
                    pe.matmul(PS[:, 7, 360:488], CT[:], wo[:], start=True, stop=True).then_inc(b_sem["wo"], 1)

            for s in range(-4, 0):
                slot(s, s % 2)
            with pe.Fori(0, (B - 4) // 2) as i:
                for u in range(2):
                    slot(i * 2 + u, u)
            for s in range(B - 4, B):
                slot(s, s % 2)

            def logits(m, g, at):
                R, EW, w = r_sem[m], (E0, E1 + 1)[m], (wr0, wr1)[m]
                pe.wait_ge(R["ht"], g * 2 + 3)
                for j in range(GB):
                    ins = pe.matmul(PS[:, LB[m], bass.ds((at + j) * EW, EW)], HT[m][side(m, g)][:, j * P:(j + 1) * P], w[:], start=True, stop=True)
                ins.then_inc(R["lg"], 1)

            def turn_tokens(m, g):
                R = r_sem[m]
                pe.wait_ge(R["h"], g + 2)
                if m == 1:
                    pe.wait_ge(R["ht"], g * 2 + 1)
                elif g >= 2:
                    pe.wait_ge(R["ht"], (g - 1) * 2 + 1)
                for j in range(GB):
                    ins = pe.transpose(PS[:, RB[m][side(m, g)], j * P:(j + 1) * P], HG[m][side(m, g)][:, j, :], identf[:])
                ins.then_inc(R["t"], 1)

            pe.wait_ge(b_sem["z"], B + 1)
            pe.wait_ge(wr_in, 16 * 3)
            turn_tokens(0, 0)
            for g in range(G):
                if g + 1 < G:
                    turn_tokens(0, g + 1)
                logits(0, g, g * GB)
            pe.wait_ge(r_sem[0]["cs"], 2)
            for b in range(B):
                ins = pe.transpose(PS[:, 2 + b // 8, :].bitcast(BF16)[:, (b % 8) * P:(b % 8 + 1) * P], CS[:, b, :], identb[:])
                if b % 8 == 7:
                    ins.then_inc(r_sem[0]["ct"], 1)
            pe.wait_ge(r_sem[0]["ct_sb"], 3)
            pe.wait_ge(r_sem[0]["low"], G + 1)
            pe.wait_ge(halved, 3)

            S = m_sem

            def split_product(bank, high, low, x_high, x_low, start=True, stop=True):
                pe.matmul(PS[:, bank, :], high, x_high, start=start, stop=False)
                pe.matmul(PS[:, bank, :], high, x_low, start=False, stop=False)
                return pe.matmul(PS[:, bank, :], low, x_high, start=False, stop=stop)

            def down(m, g, base, k, q):
                pe.wait_ge(S["lo"], base + k + 2)
                if k == 0:
                    pe.wait_ge(S["yt"], q + 1)
                t = turn_of(m, g, k)
                split_product(6, WH[m][2][:, k, :], WL[m][2][:, k, :], HHI[t][:], HLO[t][:],
                              start=(k == 0), stop=(k == NCH[m] - 1)).then_inc(S["down"], 1)

            def turn_out(q):
                pe.wait_ge(S["yt"], q + 1)
                pe.wait_ge(S["x"], q)
                if not isinstance(q, int):
                    pe.wait_ge(c_sem["xh"], q)
                elif q > 1:
                    pe.wait_ge(c_sem["xh"], {4: 3, 5: 3}.get(q, G) + 1)
                if isinstance(q, int) and q == 5:
                    pe.wait_ge(c_sem["exp"], G * GB + 1)
                for j in range(GB):
                    ins = pe.transpose(PS[:, 7, j * P:(j + 1) * P], YT[:, j * P:(j + 1) * P], identf[:])
                ins.then_inc(S["yn"], 1)

            def chunks(m, g, inserts):
                n, per = NCH[m], MOE[m]["per"]
                base = g * n + OFF[m][0]
                start = isinstance(g, int) and m == 0 and g == 0
                q = g + m * G
                xh, xl = H2H[:, bass.ds(g * GT, GT)], H2L[:, bass.ds(g * GT, GT)]
                before = 0 if m == 1 and isinstance(g, int) and g == 0 else m
                if m == 1:
                    pe.wait_ge(r_sem[1]["low"], g + 2)
                    pe.wait_ge(r_sem[1]["ct_sb"], g + 2)
                for c in range(n):
                    if first_of_expert(m, c):
                        e = c // per
                        pe.wait_ge(S["bc_sb"], g * NBC[m] + OFF[m][2] + e + 1)
                        pe.matmul(PS[:, 4, :], SEL[m][:, e, :], CWT[:, bass.ds(g * GT, GT)], start=True, stop=True).then_inc(S["bc"], 1)
                    if not (start and c < 2):
                        pe.wait_ge(S["silu"], base + c)
                    split_product(c % 2, WH[m][0][:, c, :], WL[m][0][:, c, :], xh, xl).then_inc(S["g"], 1)
                    if not (start and c < 2):
                        pe.wait_ge(S["hid"], base + c)
                    split_product(2 + c % 2, WH[m][1][:, c, :], WL[m][1][:, c, :], xh, xl).then_inc(S["u"], 1)
                    if c >= LAG:
                        down(m, g, base, c - LAG, q)
                    elif not start:
                        down(before, g - 1, base - NCH[before], NCH[before] + c - LAG, q)
                    if c == LAG + 1 and not start:
                        turn_out(q)
                    for f in inserts.get(c, ()):
                        f()

            def turn(t):
                def go():
                    bank = TB[t % 2]
                    if t == 9:
                        pe.wait_ge(turn_lo, 8)
                        pe.transpose(PS[:, bank, 0:E1 + 1], wr1_nat[:], identf[0:E1 + 1, 0:E1 + 1]).then_inc(turn_ps, 1)
                        pe.wait_ge(turn_lo, 9)
                        pe.wait_ge(turn_hi, 10)
                        return
                    if t % 3 == 0:
                        pe.wait_ge(raw_in[3 + t // 3], 32)
                    if t >= 2:
                        pe.wait_ge(turn_lo, t - 1)
                    c0, c1 = TURNS[t % 3]
                    for c in range(c0, c1):
                        ins = pe.transpose(PS[:, bank, (c - c0) * P:(c - c0 + 1) * P], raw[(t // 3 + 1) % 2][:, c, :], identf[:])
                    ins.then_inc(turn_ps, 1)
                return go

            def matching(g):
                def t():
                    pe.wait_ge(c_sem["xn"], g + 2)
                    for j in range(GB):
                        ins = pe.transpose(PS[:, 7, j * P:(j + 1) * P], XG[:, j, :], identf[:])
                    ins.then_inc(c_sem["t"], 1)

                def sims():
                    pe.wait_ge(c_sem["e3"], g + 2)
                    pe.wait_ge(c_sem["xt"], g + 2)
                    for j in range(GB):
                        pe.matmul(PS[:, 7, j * TC:(j + 1) * TC], E3T[:, j * P:(j + 1) * P], ctx_t[:, g * GB + j, :], start=True, stop=True)
                        ins = pe.matmul(PS[:, 7, GB * TC + j:GB * TC + j + 1], XGT[:, j * P:(j + 1) * P], w1_c[:], start=True, stop=True)
                    ins.then_inc(c_sem["s"], 1)

                def bts():
                    pe.wait_ge(c_sem["mx"], g + 2)
                    pe.transpose(PS[0:GB, 5, 0:P], bt[:], identf[:]).then_inc(c_sem["bt"], 1)

                def ats():
                    pe.wait_ge(c_sem["a"], g + 2)
                    if is_last(g):
                        pe.wait_ge(S["x"], G + 2)
                    for j in range(GB):
                        ins = pe.transpose(PS[0:TC, 7, j * P:(j + 1) * P], AM[:, j, :], identf[:])
                    ins.then_inc(c_sem["at"], 1)

                def bbts():
                    pe.wait_ge(c_sem["bb"], g + 2)
                    pe.transpose(PS[:, 5, P:2 * P], BB[:], identf[:]).then_inc(c_sem["bbt"], 1)

                def hqs():
                    pe.wait_ge(c_sem["at_sb"], g + 2)
                    pe.wait_ge(c_sem["cg"], g * 2 + 3)
                    for j in range(GB):
                        ins = pe.matmul(PS[:, 7, j * P:(j + 1) * P], CG[:, j, :], AMT[:, j * P:(j + 1) * P], start=True, stop=True)
                    ins.then_inc(c_sem["hq"], 1)

                def hcs():
                    pe.wait_ge(c_sem["bc"], g + 2)
                    pe.wait_ge(r_sem[1]["ct_sb"], g + 1)
                    for j in range(GB):
                        ins = pe.matmul(PS[:, 5, 2 * P + j:2 * P + j + 1], XG[:, j, :], BCOL[:, j:j + 1], start=True, stop=True)
                    ins.then_inc(c_sem["hc"], 1)

                def outs():
                    pe.wait_ge(c_sem["xh"], g + 2)
                    pe.wait_ge(c_sem["wb"], g + 2)
                    for j in range(GB):
                        o = PS[:, 5, j * D:(j + 1) * D]
                        pe.matmul(o, XGT[:, j * P:(j + 1) * P], WB[:, j, :], start=True, stop=False)
                        pe.matmul(o, HQ[:, j * P:(j + 1) * P], wqv[:, 1, :], start=False, stop=False)
                        ins = pe.matmul(o, XH[:, j * P:(j + 1) * P], wqv[:, 2, :], start=False, stop=True)
                    ins.then_inc(c_sem["o"], 1)

                def ct():
                    pe.wait_ge(r_sem[1]["cs"], g + 2)
                    if not is_last(g):
                        pe.wait_ge(c_sem["bc"], g + 3)
                    for j in range(GB):
                        ins = pe.transpose(PS[:, 5, :].bitcast(BF16)[:, j * P:(j + 1) * P], CS[:, j, :], identb[:])
                    ins.then_inc(r_sem[1]["ct"], 1)

                r = (23, 24, 28) if is_last(g) else (27, 28, 35)
                return by_chunk((9, t), (11, sims), (12, bts), (16, ats), (16, bbts), (17, hqs), (18, hcs), (20, outs),
                                (r[0], lambda: turn_tokens(1, g)), (r[1], lambda: logits(1, g, 0)), (r[2], ct))

            pe.wait_ge(wqv_in, 16)
            mixtures(pe, chunks, by_chunk(*((c, turn(t)) for t, c in enumerate(TURN_AT))), matching)
            last_base = (G - 1) * NCH[1] + OFF[1][0]
            for k in range(NCH[1] - LAG, NCH[1]):
                down(1, G - 1, last_base, k, 2 * G - 1)
            turn_out(2 * G)


_INS = ['x', 'ctx_1024', 'g_xattn', 'g_ffn', 'L0_xattn_Wq', 'L0_xattn_bq', 'L0_xattn_Wk', 'L0_xattn_bk', 'L0_xattn_Wv',
        'L0_xattn_bv', 'L0_xattn_Wo', 'L0_xattn_bo', 'L0_ffn_norm1_w', 'L0_ffn_norm2_w', 'L0_ffn_wq', 'L0_ffn_wk',
        'L0_ffn_wv', 'L0_ffn_wo', 'L0_ffn_router_w', 'L0_ffn_sh_gate', 'L0_ffn_sh_up', 'L0_ffn_sh_down', 'L0_ffn_e_gate',
        'L0_ffn_e_up', 'L0_ffn_e_down', 'L1_xattn_w_sim', 'L1_xattn_b_sim', 'L1_xattn_W_qv', 'L1_xattn_b_qv', 'L1_ffn_Wg',
        'L1_ffn_We_gate', 'L1_ffn_We_up', 'L1_ffn_We_down', 'L1_ffn_Ws_gate', 'L1_ffn_Ws_up', 'L1_ffn_Ws_down', 'L1_ffn_Wsg']


def kernel(**inputs):
    import numpy as _np
    import concourse.bacc as _bacc
    from concourse import mybir as _mybir
    from concourse.bass_utils import run_bass_kernel_spmd as _run

    nc = _bacc.Bacc("TRN2", target_bir_lowering=False, num_devices=1)
    arrays, args = {}, {}
    for name in _INS:
        v = _np.ascontiguousarray(inputs[name])
        arrays[f"in_{name}_dram"] = v
        args[name] = nc.dram_tensor(f"in_{name}_dram", v.shape, _mybir.dt.from_np(v.dtype), kind="ExternalInput").ap()
    out = nc.dram_tensor("out_0_dram", (B, P, D), _mybir.dt.float32, kind="ExternalOutput").ap()
    build(nc, args, out)
    r = _run(nc, [arrays], core_ids=[0])
    return r.results[0]["out_0_dram"]
```
